# Optimizing a Trainium2 kernel written in Bass

```python
import numpy as np
import jax
import jax.numpy as jnp

def _softmax(x, axis=-1):
    return jax.nn.softmax(x, axis=axis)

def _gelu(x):
    return jax.nn.gelu(x, approximate=True)

def _silu(x):
    return jax.nn.silu(x)

def _sigmoid(x):
    return jax.nn.sigmoid(x)

def _layernorm(x, axis=-1, eps=1e-05):
    m = jnp.mean(x, axis=axis, keepdims=True)
    v = jnp.var(x, axis=axis, keepdims=True)
    return (x - m) / jnp.sqrt(v + eps)

def _scatter_add(tgt, idx, src, axis=0):
    return tgt.at[idx].add(src)

def _segment_sum(src, seg, n):
    return jax.ops.segment_sum(src, seg, n)
kernel_name = 'mk_flamingo_gated_d2_seqx_r8_573f72'

def setup_inputs(seed: int=0):
    np.random.seed(seed)
    _w = jnp.asarray

    def _rec_inputs():
        import jax
        import jax.numpy as jnp
        _rk = jax.random.key(seed)
        x = 7.22e-05 + 1 * jax.random.normal(jax.random.fold_in(_rk, 1), (8, 128, 512), jnp.float32)
        _lenS = 128 - jax.random.randint(jax.random.fold_in(_rk, 7), (8,), 0, max(1, 128 // 4) + 1, jnp.int32)
        _lenS2 = 128 - jax.random.randint(jax.random.fold_in(_rk, 8), (8,), 0, max(1, 128 // 4) + 1, jnp.int32)
        _ctx_4096P = jax.random.normal(jax.random.fold_in(_rk, 11), (8, 16, 512), jnp.float32)
        _ctx_4096c = jax.random.dirichlet(jax.random.fold_in(_rk, 511), 0.3 * jnp.ones((16,), jnp.float32), (8, 128))
        _ctx_4096t = jnp.einsum('bsk,bkd->bsd', _ctx_4096c, _ctx_4096P)
        _ctx_4096t = _ctx_4096t * jax.lax.rsqrt(jnp.mean(jnp.square(_ctx_4096t)) + 1e-12) * 0.953939
        ctx_4096 = 4.13588e-05 + 0.999923 * (_ctx_4096t + 0.3 * jax.random.normal(jax.random.fold_in(_rk, 611), (8, 128, 512), jnp.float32))
        _validS = jnp.arange(128)[None, :] < _lenS[:, None]
        _validS2 = jnp.arange(128)[None, :] < _lenS2[:, None]
        _causal = jnp.tril(jnp.ones((128, 128), dtype=bool))
        mask_BxSxS2_bk0 = jnp.logical_not(jnp.broadcast_to(_validS2[:, None, :], (8, 128, 128)))
        _g = jax.random.normal(jax.random.fold_in(_rk, 9001), (2, 2), jnp.float32)
        _g = jnp.sign(_g) * jnp.maximum(jnp.abs(_g), 1.0) + (_g == 0) * 1.0
        g_xattn = _g[0]
        g_ffn = _g[1]
        return (x, ctx_4096, mask_BxSxS2_bk0, g_xattn, g_ffn)
    x, ctx_4096, mask_BxSxS2_bk0, g_xattn, g_ffn = _rec_inputs()

    def _L0_xattn_setup():
        import jax, jax.numpy as jnp
        import numpy as np
        B, LQ, LK, D, H, DH = (2, 128, 128, 512, 32, 128)
        EPS = 1e-05

        def _rmsnorm(x, weight):
            var = jnp.mean(jnp.square(x), axis=-1, keepdims=True)
            return x * jax.lax.rsqrt(var + EPS) * weight
        key = jax.random.key(seed)
        ks = jax.random.split(key, 8)
        scale = 0.02
        return {'hidden_states': jax.random.normal(ks[0], (B, LQ, D), jnp.float32), 'key_value_states': jax.random.normal(ks[1], (B, LK, D), jnp.float32), 'attention_mask': jax.random.randint(ks[2], (B, LQ, LK), 0, 2) > 0, 'position_bias': jax.random.normal(ks[3], (H, LQ, LK), jnp.float32), 'ln_weight': jnp.ones((D,), jnp.float32), 'w_q': jax.random.normal(ks[4], (H * DH, D), jnp.float32) * scale, 'w_k': jax.random.normal(ks[5], (H * DH, D), jnp.float32) * scale, 'w_v': jax.random.normal(ks[6], (H * DH, D), jnp.float32) * scale, 'w_out': jax.random.normal(ks[7], (D, H * DH), jnp.float32) * scale}
    _L0_xattn_all = _L0_xattn_setup()
    _L0_xattn_in = {k: v for k, v in _L0_xattn_all.items() if k in ('position_bias', 'ln_weight', 'w_q', 'w_k', 'w_v', 'w_out')}
    del _L0_xattn_all

    def _L0_ffn_setup():
        import jax, jax.numpy as jnp
        import numpy as np
        IN_FEATURES = 512
        OUT_FEATURES = 512
        WBITS = 4
        GROUPSIZE = 128
        PACK_FACTOR = 32 // WBITS
        MASK = (1 << WBITS) - 1

        def _unpack4(packed, axis_len):
            shifts = jnp.arange(PACK_FACTOR, dtype=jnp.int32) * WBITS
            nib = packed[..., :, None] >> shifts & MASK
            return nib.reshape(*packed.shape[:-1], axis_len)
        key = jax.random.key(seed)
        k1, k2, k3, k4, k5 = jax.random.split(key, 5)
        x = jax.random.normal(k1, (4, 256, IN_FEATURES), dtype=jnp.float32)
        qweight = jax.random.randint(k2, (IN_FEATURES * WBITS // 32, OUT_FEATURES), jnp.iinfo(jnp.int32).min, jnp.iinfo(jnp.int32).max, dtype=jnp.int32)
        num_groups = IN_FEATURES // GROUPSIZE
        qzeros = jax.random.randint(k3, (num_groups, OUT_FEATURES * WBITS // 32), jnp.iinfo(jnp.int32).min, jnp.iinfo(jnp.int32).max, dtype=jnp.int32)
        scales = jax.random.uniform(k4, (num_groups, OUT_FEATURES), dtype=jnp.float32, minval=0.001, maxval=0.02)
        bias = jax.random.normal(k5, (OUT_FEATURES,), dtype=jnp.float32)
        return {'x': x, 'qweight': qweight, 'qzeros': qzeros, 'scales': scales, 'bias': bias}
    _L0_ffn_all = _L0_ffn_setup()
    _L0_ffn_in = {k: v for k, v in _L0_ffn_all.items() if k in ('qweight', 'qzeros', 'scales', 'bias')}
    del _L0_ffn_all

    def _L1_xattn_setup():
        import jax, jax.numpy as jnp
        import numpy as np
        EPS = 1e-06

        def rmsnorm(x, w):
            xf = x.astype(jnp.float32)
            var = jnp.mean(xf * xf, axis=-1, keepdims=True)
            return (xf * jax.lax.rsqrt(var + EPS)).astype(x.dtype) * w
        key = jax.random.key(seed)
        ks = jax.random.split(key, 6)
        B, T, S, Dt, Df = (4, 128, 72, 512, 512)
        text = jax.random.normal(ks[0], (B, T, Dt), dtype=jnp.float32)
        features = jax.random.normal(ks[1], (B, S, Df), dtype=jnp.float32)
        lim_q = float(np.sqrt(6.0 / (Dt + Df)))
        lim_k = float(np.sqrt(6.0 / (Df + Df)))
        Wq_w = jax.random.uniform(ks[2], (Df, Dt), minval=-lim_q, maxval=lim_q, dtype=jnp.float32)
        Wk_w = jax.random.uniform(ks[3], (Df, Df), minval=-lim_k, maxval=lim_k, dtype=jnp.float32)
        bq = 1.0 / np.sqrt(Dt)
        bk = 1.0 / np.sqrt(Df)
        Wq_b = jax.random.uniform(ks[4], (Df,), minval=-bq, maxval=bq, dtype=jnp.float32)
        Wk_b = jax.random.uniform(ks[5], (Df,), minval=-bk, maxval=bk, dtype=jnp.float32)
        fn_w = jnp.ones((Df,), dtype=jnp.float32)
        qn_w = jnp.ones((Df,), dtype=jnp.float32)
        kn_w = jnp.ones((Df,), dtype=jnp.float32)
        return {'text': text, 'features': features, 'Wq_w': Wq_w, 'Wq_b': Wq_b, 'Wk_w': Wk_w, 'Wk_b': Wk_b, 'fn_w': fn_w, 'qn_w': qn_w, 'kn_w': kn_w}
    _L1_xattn_all = _L1_xattn_setup()
    _L1_xattn_in = {k: v for k, v in _L1_xattn_all.items() if k in ('Wq_w', 'Wq_b', 'Wk_w', 'Wk_b', 'fn_w', 'qn_w', 'kn_w')}
    del _L1_xattn_all

    def _L1_ffn_setup():
        import jax, jax.numpy as jnp
        import numpy as np
        SCALING = 32.0 / 16.0
        key = jax.random.key(seed)
        ks = jax.random.split(key, 7)
        B, T, D, O, R, E = (4, 256, 512, 512, 16, 8)
        x = jax.random.normal(ks[0], (B, T, D), dtype=jnp.float32)
        base_W = jax.random.normal(ks[1], (O, D), dtype=jnp.float32) * D ** (-0.5)
        base_b = jax.random.normal(ks[2], (O,), dtype=jnp.float32) * 0.01
        router_W = jax.random.normal(ks[3], (2 * E - 1, D), dtype=jnp.float32) * D ** (-0.5)
        router_b = jax.random.normal(ks[4], (2 * E - 1,), dtype=jnp.float32) * 0.01
        A = jax.random.normal(ks[5], (E, R, D), dtype=jnp.float32) * D ** (-0.5)
        Bm = jax.random.normal(ks[6], (E, O, R), dtype=jnp.float32) * R ** (-0.5)
        assigned_idx = 0
        others = [i for i in range(E) if i != assigned_idx]
        expert_map = jnp.array([assigned_idx] * E + others, dtype=jnp.int32)
        return {'x': x, 'base_W': base_W, 'base_b': base_b, 'router_W': router_W, 'router_b': router_b, 'A': A, 'B': Bm, 'expert_map': expert_map}
    _L1_ffn_all = _L1_ffn_setup()
    _L1_ffn_in = {k: v for k, v in _L1_ffn_all.items() if k in ('base_W', 'base_b', 'router_W', 'router_b', 'A', 'B', 'expert_map')}
    del _L1_ffn_all
    return {'x': x, 'ctx_4096': ctx_4096, 'mask_BxSxS2_bk0': mask_BxSxS2_bk0, 'g_xattn': g_xattn, 'g_ffn': g_ffn, 'L0_xattn_position_bias': _L0_xattn_in['position_bias'], 'L0_xattn_ln_weight': _L0_xattn_in['ln_weight'], 'L0_xattn_w_q': _L0_xattn_in['w_q'], 'L0_xattn_w_k': _L0_xattn_in['w_k'], 'L0_xattn_w_v': _L0_xattn_in['w_v'], 'L0_xattn_w_out': _L0_xattn_in['w_out'], 'L0_ffn_qweight': _L0_ffn_in['qweight'], 'L0_ffn_qzeros': _L0_ffn_in['qzeros'], 'L0_ffn_scales': _L0_ffn_in['scales'], 'L0_ffn_bias': _L0_ffn_in['bias'], 'L1_xattn_Wq_w': _L1_xattn_in['Wq_w'], 'L1_xattn_Wq_b': _L1_xattn_in['Wq_b'], 'L1_xattn_Wk_w': _L1_xattn_in['Wk_w'], 'L1_xattn_Wk_b': _L1_xattn_in['Wk_b'], 'L1_xattn_fn_w': _L1_xattn_in['fn_w'], 'L1_xattn_qn_w': _L1_xattn_in['qn_w'], 'L1_xattn_kn_w': _L1_xattn_in['kn_w'], 'L1_ffn_base_W': _L1_ffn_in['base_W'], 'L1_ffn_base_b': _L1_ffn_in['base_b'], 'L1_ffn_router_W': _L1_ffn_in['router_W'], 'L1_ffn_router_b': _L1_ffn_in['router_b'], 'L1_ffn_A': _L1_ffn_in['A'], 'L1_ffn_B': _L1_ffn_in['B'], 'L1_ffn_expert_map': _L1_ffn_in['expert_map']}

def reference(x, ctx_4096, mask_BxSxS2_bk0, g_xattn, g_ffn, L0_xattn_position_bias, L0_xattn_ln_weight, L0_xattn_w_q, L0_xattn_w_k, L0_xattn_w_v, L0_xattn_w_out, L0_ffn_qweight, L0_ffn_qzeros, L0_ffn_scales, L0_ffn_bias, L1_xattn_Wq_w, L1_xattn_Wq_b, L1_xattn_Wk_w, L1_xattn_Wk_b, L1_xattn_fn_w, L1_xattn_qn_w, L1_xattn_kn_w, L1_ffn_base_W, L1_ffn_base_b, L1_ffn_router_W, L1_ffn_router_b, L1_ffn_A, L1_ffn_B, L1_ffn_expert_map):
    import jax
    import jax.numpy as jnp

    def _L0_xattn_ref(hidden_states, key_value_states, attention_mask, position_bias, ln_weight, w_q, w_k, w_v, w_out):
        import jax, jax.numpy as jnp
        import numpy as np
        B, LQ, LK, D, H, DH = (2, 128, 128, 512, 32, 128)
        EPS = 1e-05

        def _rmsnorm(x, weight):
            var = jnp.mean(jnp.square(x), axis=-1, keepdims=True)
            return x * jax.lax.rsqrt(var + EPS) * weight
        x = _rmsnorm(hidden_states, ln_weight)
        b, lq, _ = x.shape
        lk = key_value_states.shape[1]
        h_q = (x @ w_q.T).reshape(b, lq, H, DH)
        h_k = (key_value_states @ w_k.T).reshape(b, lk, H, DH)
        h_v = (key_value_states @ w_v.T).reshape(b, lk, H, DH)
        score = jnp.einsum('bqhd,bkhd->bhqk', h_q, h_k)
        score = score + position_bias[None]
        m = attention_mask[:, None]
        score = jnp.where(m, score, -jnp.inf)
        score = jax.nn.softmax(score, axis=-1)
        score = jnp.where(m, score, 0.0)
        attn = jnp.einsum('bhqk,bkhd->bqhd', score, h_v).reshape(b, lq, H * DH)
        out = attn @ w_out.T
        return hidden_states + out

    def _L0_ffn_ref(x, qweight, qzeros, scales, bias):
        import jax, jax.numpy as jnp
        import numpy as np
        IN_FEATURES = 512
        OUT_FEATURES = 512
        WBITS = 4
        GROUPSIZE = 128
        PACK_FACTOR = 32 // WBITS
        MASK = (1 << WBITS) - 1

        def _unpack4(packed, axis_len):
            shifts = jnp.arange(PACK_FACTOR, dtype=jnp.int32) * WBITS
            nib = packed[..., :, None] >> shifts & MASK
            return nib.reshape(*packed.shape[:-1], axis_len)
        shifts = jnp.arange(PACK_FACTOR, dtype=jnp.int32) * WBITS
        wq = qweight[:, None, :] >> shifts[None, :, None] & MASK
        wq = wq.reshape(IN_FEATURES, OUT_FEATURES)
        zq = _unpack4(qzeros, OUT_FEATURES) + 1
        g_idx = jnp.arange(IN_FEATURES, dtype=jnp.int32) // GROUPSIZE
        W = scales[g_idx] * (wq - zq[g_idx]).astype(scales.dtype)
        return jnp.einsum('bsi,io->bso', x, W) + bias

    def _L1_xattn_ref(text, features, Wq_w, Wq_b, Wk_w, Wk_b, fn_w, qn_w, kn_w):
        import jax, jax.numpy as jnp
        import numpy as np
        EPS = 1e-06

        def rmsnorm(x, w):
            xf = x.astype(jnp.float32)
            var = jnp.mean(xf * xf, axis=-1, keepdims=True)
            return (xf * jax.lax.rsqrt(var + EPS)).astype(x.dtype) * w
        features_n = rmsnorm(features, fn_w)
        Q = jnp.einsum('btd,fd->btf', text, Wq_w) + Wq_b
        K = jnp.einsum('bsd,fd->bsf', features_n, Wk_w) + Wk_b
        Q = rmsnorm(Q, qn_w)
        K = rmsnorm(K, kn_w)
        scale = 1.0 / jnp.sqrt(jnp.asarray(K.shape[-1], dtype=Q.dtype))
        scores = jnp.einsum('btf,bsf->bts', Q, K) * scale
        attn = jax.nn.softmax(scores, axis=-1)
        attended = jnp.einsum('bts,bsf->btf', attn, features_n)
        return attended

    def _L1_ffn_ref(x, base_W, base_b, router_W, router_b, A, B, expert_map):
        import jax, jax.numpy as jnp
        import numpy as np
        SCALING = 32.0 / 16.0
        E = A.shape[0]
        base_out = jnp.einsum('btd,od->bto', x, base_W) + base_b
        logits = jnp.einsum('btd,nd->btn', x, router_W) + router_b
        probs = jax.nn.softmax(logits, axis=-1)
        topk_p, topk_i = jax.lax.top_k(probs, E)
        mapped = expert_map[topk_i]
        onehot = (mapped[..., None] == jnp.arange(E)).astype(x.dtype)
        w = jnp.einsum('btk,btke->bte', topk_p, onehot)
        h = jnp.einsum('btd,erd->bter', x, A)
        lora = jnp.einsum('bter,eor->bto', h * w[..., None], B) * SCALING
        return base_out + lora
    x = x + jnp.tanh(g_xattn[0]) * _L0_xattn_ref(_layernorm(x, axis=-1), ctx_4096, mask_BxSxS2_bk0, L0_xattn_position_bias, L0_xattn_ln_weight, L0_xattn_w_q, L0_xattn_w_k, L0_xattn_w_v, L0_xattn_w_out)
    x = x + jnp.tanh(g_ffn[0]) * _L0_ffn_ref(_layernorm(x, axis=-1), L0_ffn_qweight, L0_ffn_qzeros, L0_ffn_scales, L0_ffn_bias)
    x = x + jnp.tanh(g_xattn[1]) * _L1_xattn_ref(_layernorm(x, axis=-1), ctx_4096, L1_xattn_Wq_w, L1_xattn_Wq_b, L1_xattn_Wk_w, L1_xattn_Wk_b, L1_xattn_fn_w, L1_xattn_qn_w, L1_xattn_kn_w)
    x = x + jnp.tanh(g_ffn[1]) * _L1_ffn_ref(_layernorm(x, axis=-1), L1_ffn_base_W, L1_ffn_base_b, L1_ffn_router_W, L1_ffn_router_b, L1_ffn_A, L1_ffn_B, L1_ffn_expert_map)
    return x

_drawn_inputs = setup_inputs


def setup_inputs(seed=0):
    import zlib

    import numpy as np

    out = dict(_drawn_inputs(seed))
    spreads = {'g_ffn': (-1.0, 0.2),
     'L0_xattn_ln_weight': (1.0, 0.55),
     'L1_xattn_fn_w': (1.0, 0.2),
     'L1_xattn_qn_w': (1.0, 0.6),
     'L1_xattn_kn_w': (1.0, 0.6)}
    factors = {'L1_xattn_Wq_b': 8.0, 'L1_xattn_Wk_b': 8.0, 'L1_ffn_base_b': 8.0, 'L1_ffn_router_b': 8.0}
    for name, (base, spread) in spreads.items():
        noise = np.random.default_rng([zlib.crc32(name.encode()), seed]).standard_normal(out[name].shape)
        drawn = base * np.exp(spread * noise) if base else spread * noise
        out[name] = jnp.asarray(drawn.astype(out[name].dtype))
    for name, factor in factors.items():
        out[name] = (out[name] * factor).astype(out[name].dtype)
    return out
```

```python
from contextlib import ExitStack

import concourse.bass as bass
from concourse import mybir
import numpy as np

P = 128
B = 8
D = 512
KC = D // P
TOK = B * P
HEADS = 32
GH = 4
GROUPS = HEADS // GH
NEXP = 8
RANK = 16
ER = NEXP * RANK
ROUT = 2 * NEXP - 1
RAW = 256
LORA_SCALE = 2.0
EPS_LN = 1e-5
EPS_RMS0 = 1e-5
EPS_RMS1 = 1e-6
MASKED = -1e30

CHUNKS = ["q0", "k0", "v0", "v1", "v2", "v3", "q1", "k1", "o0", "o1", "o2", "o3", "q2", "k2", "q3", "k3"]
NCH = len(CHUNKS)
SLOTS = 8
UNITS = (["q0a", "q0b", "k0a", "k0b"] + [f"v{b}" for b in range(B)]
         + [f"{t}{h}{s}" for h in range(1, GH) for t in "qk" for s in "ab"]
         + [f"o{b}" for b in range(B)] + [f"p{b}" for b in range(B)])
NUNIT = len(UNITS)
RING = 4
ACT_UNITS = [u for u in UNITS if u[0] in "qkv"]
DVE_UNITS = [u for u in UNITS if u[0] in "op"]
PASSES = ((0, 0), (0, 1), (1, 0))


def build(nc, a, out):
    fp32, fp32r, i32, u8 = mybir.dt.float32, mybir.dt.float32r, mybir.dt.int32, mybir.dt.uint8
    ALU, ACT, AX = mybir.AluOpType, mybir.ActivationFunctionType, mybir.AxisListType.X

    cursor = [-(-nc.sbuf_base // 64) * 64]

    def place(name, shape, dt):
        size = int(np.prod(shape[1:])) * (1 if dt == u8 else 4)
        t = nc.alloc_sbuf_tensor_at(name, shape, dt, offset=cursor[0])
        cursor[0] += -(-size // 64) * 64
        assert cursor[0] <= nc.sbuf_usable_end, (name, cursor[0])
        return t

    acc = place("acc", [P, B, D], fp32)
    stage = place("stage", [P, SLOTS, D], fp32)
    ident = place("ident", [P, P], fp32)
    gates = place("gates", [P, 4], fp32)
    tg = place("tg", [P, 4], fp32)
    cols = place("cols", [P, 3, KC], fp32)
    mhalf = place("mhalf", [P, B], fp32)
    small0 = cursor[0]

    xt = place("xt", [P, 2, KC, TOK], fp32r)
    ct = place("ct", [P, 2, KC, TOK], fp32r)
    after_xc = cursor[0]
    wq = place("wq", [P, 2, KC, P], fp32r)
    wk = place("wk", [P, 2, KC, P], fp32r)
    wvo = place("wvo", [P, 2, KC, D], fp32r)
    bias = place("bias", [P, GH, P], fp32)
    maskneg = place("maskneg", [P, B, P], fp32)
    bm = place("bm", [P, 2, B, P], fp32)
    qt = place("qt", [P, TOK], fp32)
    kt = place("kt", [P, TOK], fp32)
    vals = place("vals", [P, B, D], fp32)
    prob = place("prob", [P, B, P], fp32)
    pt = place("pt", [P, B, P], fp32)
    ao_at = cursor[0]
    ao = place("ao", [P, GH, 2, TOK], fp32r)
    anykey = place("anykey", [P, B], fp32)
    nmax = place("nmax", [P, B], fp32)
    esum = place("esum", [P, B], fp32)
    rinv = place("rinv", [P, B], fp32)
    stats = place("stats", [P, B, 6], fp32)
    mv = place("mv", [P, B, 2], fp32)
    vsum = place("vsum", [P, B], fp32)
    rstd = place("rstd", [P, B], fp32)
    ssq = place("ssq", [P, B], fp32)
    msq = place("msq", [P, B], fp32)
    rrms = place("rrms", [P, B], fp32)
    xraw = vals
    cursor[0] = ao_at
    craw = place("craw", [P, B, D], fp32)
    masku = place("masku", [P, B, P], u8)
    maskf = prob

    cursor[0] = small0
    NW = 4
    wt = [place(f"wt{n}", [P, 2, KC, D], fp32r) for n in range(NW)]
    assert cursor[0] <= after_xc
    W_KEY, W_FFN, W_QRY, W_BASE = range(NW)
    cursor[0] = after_xc
    wra = place("wra", [P, 2, KC, RAW], fp32r)
    wbm = place("wbm", [P, D], fp32)
    rows = place("rows", [P, 5, D], fp32)
    R_FFN, R_FN, R_BQ, R_BK, R_BASE = range(5)
    rb = place("rb", [P, ROUT], fp32)
    emap_i = place("emap_i", [P, ROUT], i32)
    emap = place("emap", [P, ROUT], fp32)
    consts = place("consts", [P, ROUT * ROUT + NEXP], fp32)
    onehot = place("onehot", [P, NEXP, ROUT], fp32)
    zq = place("zq", [P, D // 8], i32)
    U = 4
    tmpk_at = cursor[0]
    tmpk = place("tmpk", [P, U, D], fp32)
    after_tmpk, cursor[0] = cursor[0], tmpk_at
    qw = place("qw", [P, D], i32)
    zint = place("zint", [P, D], i32)
    wint = place("wint", [P, D], i32)
    scl = place("scl", [P, D], fp32)
    assert cursor[0] == after_tmpk
    xs = place("xs", [P, U, D], fp32)
    cs = place("cs", [P, U, D], fp32)
    tmp = place("tmp", [P, U, D], fp32)
    tt = place("tt", [P, U, 2, KC, P], fp32r)
    qt1 = place("qt1", [P, U, KC, P], fp32)
    kt1 = place("kt1", [P, U, KC, P], fp32)
    pr1 = place("pr1", [P, U, P], fp32)
    pt1 = place("pt1", [P, U, P], fp32)
    st1 = place("st1", [P, U, 6], fp32)
    mv1 = place("mv1", [P, U, 2], fp32)
    sc1 = place("sc1", [P, U, 12], fp32)
    S_VE, S_RS, S_SS, S_MS, S_RR, S_NM, S_ES, S_RI, K_SS, K_MS, K_RR = range(11)
    rt = place("rt", [P, U, 4, 16], fp32)
    cmp = place("cmp", [P, U, 2, ROUT, ROUT], fp32)
    wexp = place("wexp", [P, U, NEXP, ROUT], fp32)
    wsum = place("wsum", [P, U, NEXP], fp32)

    ctx = ExitStack()
    with ctx:
        bank = [ctx.enter_context(nc.psum_tensor(f"bank{i}", [P, D], fp32)) for i in range(8)]

        def sem(name):
            return ctx.enter_context(nc.semaphore(name))

        s_const = sem("const_in")
        s_cin = [sem(f"ctx_in{q}") for q in range(2)]
        s_xin = sem("x_in")
        s_min = sem("mask_in")
        s_bias = sem("bias_in")
        s_stage = [sem(f"stage_in{i}") for i in range(SLOTS // 2)]
        s_d = sem("dve_prep")
        s_a = sem("act_prep")
        s_g = sem("pool_prep")
        s_cT = sem("ctx_transposed")
        s_xT = sem("x_transposed")
        s_chi = sem("ctx_hi")
        s_clo = sem("ctx_lo")
        s_xhi = sem("x_hi")
        s_xlo = sem("x_lo")
        s_mneg = sem("maskneg_done")
        s_whi = sem("weights_hi")
        s_wlo = sem("weights_lo")
        s_bm = sem("biasmask_done")
        s_unit = sem("unit_done")
        s_aev = sem("act_emptied")
        s_dev = sem("dve_emptied")
        s_s = sem("scores_done")
        s_sadd = sem("scores_read")
        s_smax = sem("scores_max")
        s_nmax = sem("negmax_done")
        s_exp = sem("exp_done")
        s_rinv = sem("rinv_steps")
        s_p = sem("probs_scaled")
        s_pt = sem("pt_done")
        s_pte = sem("pt_emptied")
        s_pv = sem("pv_done")
        s_aohi = sem("ao_hi")
        s_aolo = sem("ao_lo")
        s_out = sem("stored")

        ahead = SLOTS // 2
        npairs = GROUPS * NCH // 2
        ix = {c: i for i, c in enumerate(CHUNKS)}
        un = {u: i for i, u in enumerate(UNITS)}
        ax = {u: i for i, u in enumerate(ACT_UNITS)}
        dx = {u: i for i, u in enumerate(DVE_UNITS)}
        half = lambda s: slice(s * 512, s * 512 + 512)

        with nc.Block() as block:

            @block.sync
            def _(sp):
                sp.dma_start(ident[:, :], a["ident"]).then_inc(s_const, 16)
                sp.dma_start(gates[:, :], a["gates"].partition_broadcast(P)).then_inc(s_const, 16)
                sp.dma_start(cols[:, :, :], a["cols"]).then_inc(s_const, 16)
                for q in range(2):
                    sp.dma_start(craw[:, 4 * q:4 * q + 4, :], a["ctx"][:, 4 * q:4 * q + 4, :]).then_inc(s_cin[q], 16)
                sp.dma_start(masku[:, :, :], a["mask"]).then_inc(s_min, 16)

                def load(pair, slot):
                    sp.dma_start(stage[:, 2 * slot:2 * slot + 2, :], a["w0"][pair, :, :, :]).then_inc(s_stage[slot], 16)

                for j in range(ahead):
                    load(j, j)
                sp.dma_start(bias[:, :, :], a["bias"][0, :, :, :]).then_inc(s_bias, 16)
                with sp.Fori(0, GROUPS - 1) as g:
                    for j in range(NCH // 2):
                        sp.wait_ge(s_wlo, g * NCH + 2 * j + 2)
                        load(g * (NCH // 2) + (j + ahead), j % ahead)
                    sp.wait_ge(s_bm, g * GH + GH)
                    sp.dma_start(bias[:, :, :], a["bias"][g + 1, :, :, :]).then_inc(s_bias, 16)
                for j in range(NCH // 2 - ahead):
                    sp.wait_ge(s_wlo, (GROUPS - 1) * NCH + 2 * j + 2)
                    load((GROUPS - 1) * (NCH // 2) + j + ahead, j % ahead)

            @block.gpsimd
            def _(pool):
                pool.memset(mhalf[:, :], -0.5).then_inc(s_g, 1)
                pool.wait_ge(s_g, 1)
                pool.wait_ge(s_d, 2 * B + 1)
                pool.tensor_tensor(rstd[:, :], vsum[:, :], mhalf[:, :], ALU.pow).then_inc(s_g, 1)
                pool.wait_ge(s_d, 3 * B + 2)
                pool.tensor_tensor(rrms[:, :], msq[:, :], mhalf[:, :], ALU.pow).then_inc(s_g, 1)

                def w_lo(g, c):
                    i = ix[c]
                    kind, h = c[0], int(c[1])
                    src = stage[:, i % SLOTS, :]
                    if kind in "qk":
                        w = wq if kind == "q" else wk
                        hi, lo = (w[:, s, :, :].rearrange("p c d -> p (c d)") for s in (0, 1))
                    else:
                        hi, lo = wvo[:, 0, h, :], wvo[:, 1, h, :]
                    pool.wait_ge(s_whi, g * NCH + i + 1)
                    pool.tensor_tensor(lo, src, hi.bitcast(fp32), ALU.subtract).then_inc(s_wlo, 1)

                def biasmask(g, h):
                    if h == 0:
                        pool.wait_ge(s_bias, g * 16 + 16)
                    pool.wait_ge(s_sadd, g * 2 * GH + 2 * h + 1)
                    pool.tensor_tensor(bm[:, h % 2, :, :], maskneg[:, :, :],
                                       bias[:, h:h + 1, :].to_broadcast([P, B, P]), ALU.add).then_inc(s_bm, 1)

                pool.wait_ge(s_mneg, 1)
                with pool.Fori(0, GROUPS) as g:
                    w_lo(g, "q0")
                    w_lo(g, "k0")
                    biasmask(g, 0)
                    for c in ("v0", "v1", "v2", "v3"):
                        w_lo(g, c)
                    biasmask(g, 1)
                    for c in ("q1", "k1", "o0", "o1", "o2", "o3", "q2", "k2"):
                        w_lo(g, c)
                    biasmask(g, 2)
                    w_lo(g, "q3")
                    w_lo(g, "k3")
                    biasmask(g, 3)

            @block.scalar
            def _(act):
                act.dma_start(xraw[:, 0:4, :], a["x"][:, 0:4, :]).then_inc(s_xin, 16)
                act.dma_start(xraw[:, 4:8, :], a["x"][:, 4:8, :]).then_inc(s_xin, 16)
                act.wait_ge(s_const, 48)
                act.activation(tg[:, :], gates[:, :], ACT.Tanh).then_inc(s_a, 1)
                for b in range(B):
                    act.wait_ge(s_cT, b + 1)
                    act.activation(ct[:, 0, :, b * P:(b + 1) * P], bank[b][:, :].rearrange("p (c t) -> p c t", c=KC),
                                   ACT.Copy).then_inc(s_chi, 1)
                act.wait_ge(s_clo, B)
                for b in range(B):
                    act.wait_ge(s_d, 2 * B + 2 + b)
                    act.activation(craw[:, b, :], acc[:, b, :], ACT.Square, accum_out=ssq[:, b:b + 1]).then_inc(s_a, 1)
                act.wait_ge(s_g, 3)
                for b in range(B):
                    act.activation(xraw[:, b, :], acc[:, b, :], ACT.Copy, scale=rrms[:, b:b + 1]).then_inc(s_a, 1)
                for b in range(B):
                    act.wait_ge(s_xT, b + 1)
                    for c in range(KC):
                        act.activation(xt[:, 0, c, b * P:(b + 1) * P], bank[b][:, c * P:(c + 1) * P],
                                       ACT.Copy, scale=cols[:, 0, c:c + 1]).then_inc(s_xhi, 1)

                def w_hi(g, c):
                    i = ix[c]
                    kind, h = c[0], int(c[1])
                    act.wait_ge(s_stage[i // 2 % ahead], g * 32 + 16 * (i // 2 // ahead) + 16)
                    if kind in "qk":
                        last = un[f"{kind}{h - 1}b"] + NUNIT if h else un[f"{kind}{GH - 1}b"]
                        hi = (wq if kind == "q" else wk)[:, 0, :, :].rearrange("p c d -> p (c d)")
                    else:
                        last = un[f"v{B - 1}"] + NUNIT if kind == "o" else un[f"p{B - 1}"]
                        hi = wvo[:, 0, h, :]
                    act.wait_ge(s_unit, g * NUNIT + last + 1)
                    act.activation(hi, stage[:, i % SLOTS, :], ACT.Copy).then_inc(s_whi, 1)

                def empty(g, u):
                    i = un[u]
                    act.wait_ge(s_unit, g * NUNIT + NUNIT + i + 1)
                    if u[0] == "v":
                        dst = vals[:, int(u[1]), :]
                    else:
                        dst = (qt if u[0] == "q" else kt)[:, half("ab".index(u[2]))]
                    act.activation(dst, bank[i % RING][:, :], ACT.Copy).then_inc(s_aev, 1)

                def exps(g, h):
                    for s in range(2):
                        act.wait_ge(s_nmax, g * 2 * GH + 2 * h + s + 1)
                        for b in range(4 * s, 4 * s + 4):
                            act.activation(prob[:, b, :], prob[:, b, :], ACT.Exp, bias=nmax[:, b:b + 1],
                                           accum_out=esum[:, b:b + 1]).then_inc(s_exp, 1)

                def ao_hi(g, h):
                    for s in range(2):
                        act.wait_ge(s_pv, g * 2 * GH + 2 * h + s + 1)
                        act.activation(ao[:, h, 0, half(s)], bank[6 + s][:, :], ACT.Copy).then_inc(s_aohi, 1)

                with act.Fori(0, GROUPS) as g:
                    w_hi(g, "q0")
                    w_hi(g, "k0")
                    for u, c in (("q0a", "v0"), ("q0b", "v1"), ("k0a", "v2"), ("k0b", "v3")):
                        empty(g, u)
                        w_hi(g, c)
                    exps(g, 0)
                    for b in range(4):
                        empty(g, f"v{b}")
                    w_hi(g, "q1")
                    w_hi(g, "k1")
                    for b in range(4, B):
                        empty(g, f"v{b}")
                    ao_hi(g, 0)
                    for j in range(GH):
                        w_hi(g, f"o{j}")
                    for h in (1, 2, 3):
                        empty(g, f"q{h}a")
                        empty(g, f"q{h}b")
                        if h < 3:
                            w_hi(g, f"q{h + 1}")
                        empty(g, f"k{h}a")
                        empty(g, f"k{h}b")
                        if h < 3:
                            w_hi(g, f"k{h + 1}")
                        if h >= 2:
                            ao_hi(g, h - 1)
                        exps(g, h)
                    ao_hi(g, 3)

            @block.vector
            def _(dve):
                dve.wait_ge(s_xin, 32)
                for b in range(B):
                    dve.bn_stats(stats[:, b, :], xraw[:, b, :]).then_inc(s_d, 1)
                for b in range(B):
                    dve.wait_ge(s_d, b + 1)
                    dve.bn_aggr(mv[:, b, :], stats[:, b, :]).then_inc(s_d, 1)
                dve.wait_ge(s_d, 2 * B)
                dve.tensor_scalar(vsum[:, :], mv[:, :, 1], EPS_LN, None, ALU.add).then_inc(s_d, 1)
                for b in range(B):
                    dve.wait_ge(s_chi, b + 1)
                    dve.tensor_tensor(ct[:, 1, :, b * P:(b + 1) * P], bank[b][:, :].rearrange("p (c t) -> p c t", c=KC),
                                      ct[:, 0, :, b * P:(b + 1) * P].bitcast(fp32), ALU.subtract).then_inc(s_clo, 1)
                dve.wait_ge(s_g, 2)
                for b in range(B):
                    dve.tensor_scalar(acc[:, b, :], xraw[:, b, :], mv[:, b, 0:1], rstd[:, b:b + 1],
                                      ALU.subtract, ALU.mult).then_inc(s_d, 1)
                dve.wait_ge(s_a, 1 + B)
                dve.tensor_scalar(msq[:, :], ssq[:, :], 1.0 / D, EPS_RMS0, ALU.mult, ALU.add).then_inc(s_d, 1)
                dve.wait_ge(s_min, 16)
                dve.tensor_copy(maskf[:, :, :], masku[:, :, :]).then_inc(s_d, 1)
                dve.wait_ge(s_d, 3 * B + 3)
                dve.tensor_reduce(anykey[:, :], maskf[:, :, :], AX, ALU.max).then_inc(s_d, 1)
                dve.tensor_scalar(maskneg[:, :, :], maskf[:, :, :], 1.0, -MASKED, ALU.subtract, ALU.mult).then_inc(s_mneg, 1)
                for b in range(B):
                    dve.wait_ge(s_xhi, b * KC + KC)
                    for c in range(KC):
                        dve.scalar_tensor_tensor(out=xt[:, 1, c, b * P:(b + 1) * P], in0=bank[b][:, c * P:(c + 1) * P],
                                                 scalar=cols[:, 0, c:c + 1],
                                                 in1=xt[:, 0, c, b * P:(b + 1) * P].bitcast(fp32),
                                                 op0=ALU.mult, op1=ALU.subtract).then_inc(s_xlo, 1)
                dve.wait_ge(s_d, 3 * B + 4)
                dve.sem_inc(s_dev, len(DVE_UNITS))
                dve.sem_inc(s_sadd, 2)
                dve.sem_inc(s_aolo, 2)

                def softmax_in(g, h):
                    n = g * 2 * GH + 2 * h
                    dve.wait_ge(s_bm, g * GH + h + 1)
                    for s in range(2):
                        bs = slice(4 * s, 4 * s + 4)
                        dve.wait_ge(s_s, n + s + 1)
                        dve.tensor_tensor(prob[:, bs, :], bank[4 + s][:, :].rearrange("p (b k) -> p b k", b=4),
                                          bm[:, h % 2, bs, :], ALU.add).then_inc(s_sadd, 1)
                        dve.wait_ge(s_sadd, n + s + 3)
                        dve.tensor_reduce(rinv[:, bs], prob[:, bs, :], AX, ALU.max).then_inc(s_smax, 1)
                        dve.wait_ge(s_smax, n + s + 1)
                        dve.tensor_scalar(nmax[:, bs], rinv[:, bs], -1.0, None, ALU.mult).then_inc(s_nmax, 1)

                def softmax_out(g, h, s):
                    n = g * 2 * GH + 2 * h + s
                    bs = slice(4 * s, 4 * s + 4)
                    dve.wait_ge(s_exp, g * B * GH + h * B + 4 * s + 4)
                    dve.reciprocal(rinv[:, bs], esum[:, bs]).then_inc(s_rinv, 1)
                    dve.wait_ge(s_rinv, 2 * n + 1)
                    dve.tensor_tensor(rinv[:, bs], rinv[:, bs], anykey[:, bs], ALU.mult).then_inc(s_rinv, 1)
                    dve.wait_ge(s_rinv, 2 * n + 2)
                    dve.tensor_tensor(prob[:, bs, :], prob[:, bs, :],
                                      rinv[:, bs].unsqueeze(2).to_broadcast([P, 4, P]), ALU.mult).then_inc(s_p, 1)

                def pt_out(g, h):
                    for s in range(2):
                        dve.wait_ge(s_pt, g * 2 * GH + 2 * h + s + 1)
                        dve.tensor_copy(pt[:, 4 * s:4 * s + 4, :],
                                        bank[6 + s][:, :].rearrange("p (b k) -> p b k", b=4)).then_inc(s_pte, 1)

                def ao_lo(g, h):
                    for s in range(2):
                        dve.wait_ge(s_aohi, g * 2 * GH + 2 * h + s + 1)
                        dve.tensor_tensor(ao[:, h, 1, half(s)], bank[6 + s][:, :], ao[:, h, 0, half(s)].bitcast(fp32),
                                          ALU.subtract).then_inc(s_aolo, 1)

                def add_out(g, u):
                    i, b = un[u], int(u[1])
                    dve.wait_ge(s_unit, g * NUNIT + NUNIT + i + 1)
                    dve.wait_ge(s_dev, g * len(DVE_UNITS) + len(DVE_UNITS) + dx[u] - 7)
                    dve.tensor_tensor(acc[:, b, :], acc[:, b, :], bank[i % RING][:, :], ALU.add).then_inc(s_dev, 1)

                with dve.Fori(0, GROUPS) as g:
                    for h in range(GH):
                        softmax_in(g, h)
                        if h == 3:
                            add_out(g, "o0")
                            add_out(g, "o1")
                        softmax_out(g, h, 0)
                        if h == 3:
                            add_out(g, "o2")
                        softmax_out(g, h, 1)
                        if h == 3:
                            add_out(g, "o3")
                        pt_out(g, h)
                        if h == 3:
                            add_out(g, "o4")
                            add_out(g, "o5")
                        ao_lo(g, h)
                    add_out(g, "o6")
                    add_out(g, "o7")
                    for b in range(B):
                        add_out(g, f"p{b}")

            @block.tensor
            def _(pe):
                pe.wait_ge(s_const, 48)
                for b in range(B):
                    pe.wait_ge(s_cin[b // 4], 16)
                    for c in range(KC):
                        mm = pe.transpose(bank[b][:, c * P:(c + 1) * P], craw[:, b, c * P:(c + 1) * P], ident[:, :])
                    mm.then_inc(s_cT, 1)
                for b in range(B):
                    pe.wait_ge(s_clo, b + 1)
                    pe.wait_ge(s_a, 2 + B + b)
                    for c in range(KC):
                        mm = pe.transpose(bank[b][:, c * P:(c + 1) * P], xraw[:, b, c * P:(c + 1) * P], ident[:, :])
                    mm.then_inc(s_xT, 1)
                pe.wait_ge(s_xlo, B * KC)
                pe.sem_inc(s_unit, NUNIT)

                def bank_free(g, u):
                    i = un[u]
                    before = UNITS[i - RING]
                    if before in dx:
                        n = dx[before] + 1 + (len(DVE_UNITS) if i >= RING else 0)
                        pe.wait_ge(s_dev, g * len(DVE_UNITS) + n)
                    else:
                        pe.wait_ge(s_aev, g * len(ACT_UNITS) + ax[before] + 1)

                def weights(g, c):
                    pe.wait_ge(s_wlo, g * NCH + ix[c] + 1)

                def proj(g, kind, h, s):
                    u = f"{kind}{h}{'ab'[s]}"
                    w, t = (wq, xt) if kind == "q" else (wk, ct)
                    if s == 0:
                        weights(g, f"{kind}{h}")
                    bank_free(g, u)
                    for c in range(KC):
                        for i, j in PASSES:
                            mm = pe.matmul(bank[un[u] % RING][:, :], w[:, i, c, :], t[:, j, c, half(s)],
                                           start=(c == 0 and i + j == 0), stop=(c == KC - 1 and i == 1))
                    mm.then_inc(s_unit, 1)

                def value(g, b):
                    u = f"v{b}"
                    if b == 0:
                        weights(g, "v3")
                    bank_free(g, u)
                    for c in range(KC):
                        for i, j in PASSES:
                            mm = pe.matmul(bank[un[u] % RING][:, :], ct[:, i, c, b * P:(b + 1) * P], wvo[:, j, c, :],
                                           start=(c == 0 and i + j == 0), stop=(c == KC - 1 and i == 1))
                    mm.then_inc(s_unit, 1)

                def scores(g, h):
                    pe.wait_ge(s_aev, g * len(ACT_UNITS) + ax[f"k{h}b"] + 1)
                    for s in range(2):
                        pe.wait_ge(s_sadd, g * 2 * GH + 2 * h + s + 1)
                        for b in range(4 * s, 4 * s + 4):
                            mm = pe.matmul(bank[4 + s][:, (b - 4 * s) * P:(b - 4 * s + 1) * P],
                                           qt[:, b * P:(b + 1) * P], kt[:, b * P:(b + 1) * P], start=True, stop=True)
                        mm.then_inc(s_s, 1)

                def transposes(g, h):
                    n = g * 2 * GH + 2 * h
                    for s in range(2):
                        pe.wait_ge(s_p, n + s + 1)
                        pe.wait_ge(s_aolo, n + s + 1)
                        for b in range(4 * s, 4 * s + 4):
                            mm = pe.transpose(bank[6 + s][:, (b - 4 * s) * P:(b - 4 * s + 1) * P], prob[:, b, :], ident[:, :])
                        mm.then_inc(s_pt, 1)

                def attend(g, h):
                    if h == 0:
                        pe.wait_ge(s_aev, g * len(ACT_UNITS) + ax[f"v{B - 1}"] + 1)
                    for s in range(2):
                        pe.wait_ge(s_pte, g * 2 * GH + 2 * h + s + 1)
                        for b in range(4 * s, 4 * s + 4):
                            mm = pe.matmul(bank[6 + s][:, (b - 4 * s) * P:(b - 4 * s + 1) * P],
                                           vals[:, b, h * P:(h + 1) * P], pt[:, b, :], start=True, stop=True)
                        mm.then_inc(s_pv, 1)

                def project(g, u, heads):
                    b = int(u[1])
                    if u == "o0":
                        weights(g, "o3")
                    pe.wait_ge(s_aolo, g * 2 * GH + 2 * max(heads) + b // 4 + 3)
                    bank_free(g, u)
                    for h in heads:
                        for i, j in PASSES:
                            mm = pe.matmul(bank[un[u] % RING][:, :], ao[:, h, i, b * P:(b + 1) * P], wvo[:, j, h, :],
                                           start=(h == heads[0] and i + j == 0), stop=(h == heads[-1] and i == 1))
                    mm.then_inc(s_unit, 1)

                with pe.Fori(0, GROUPS) as g:
                    for kind in "qk":
                        for s in range(2):
                            proj(g, kind, 0, s)
                    scores(g, 0)
                    for b in range(4):
                        value(g, b)
                    transposes(g, 0)
                    for b in range(4, B):
                        value(g, b)
                    attend(g, 0)
                    for h in range(1, GH):
                        proj(g, "q", h, 0)
                        proj(g, "q", h, 1)
                        proj(g, "k", h, 0)
                        if h > 1:
                            transposes(g, h - 1)
                        proj(g, "k", h, 1)
                        if h > 1:
                            attend(g, h - 1)
                        scores(g, h)
                    for b in range(4):
                        project(g, f"o{b}", [0, 1, 2])
                    transposes(g, 3)
                    for b in (4, 5):
                        project(g, f"o{b}", [0, 1, 2])
                    attend(g, 3)
                    for b in (6, 7):
                        project(g, f"o{b}", [0, 1, 2])
                    for b in range(B):
                        project(g, f"p{b}", [3])

        IT = B // U
        names = ["k_ss", "k_ms", "k_rr", "k_fn", "k_T", "k_hi", "k_lo", "k_mm", "k_b", "k2_ss", "k2_ms", "k2_rr",
                 "k_n", "k_T2", "k_out", "x1", "y0", "b0", "x2", "q_mm", "q_b", "q_ss", "q_ms", "q_rr", "q_n", "q_T",
                 "q_out", "s_mm", "s_max", "s_neg", "s_exp", "s_ri", "s_rg", "p_T", "p_out", "pv", "x3", "ra", "lg",
                 "lg_max", "lg_neg", "lg_exp", "lg_ri", "pr", "gt", "eq", "tri", "cnt", "rank", "keep", "we", "ws",
                 "hw", "hw_T", "hw_out", "o_mm", "ob", "x4"]
        names += [f"{s}{n}" for n in range(3) for s in ("bn", "ag", "ve", "rs", "xn", "T", "hi", "lo")]
        S = {n: sem(f"t_{n}") for n in names}
        s_cl = [sem(f"t_ctx_in{u}") for u in range(U)]
        s_xl = [sem(f"t_x_in{u}") for u in range(U)]
        s_st = [sem(f"t_stored{u}") for u in range(U)]
        s_raw = [sem(f"t_raw{n}") for n in range(NW)]
        s_rra = sem("t_raw_ra")
        s_rest = sem("t_rest_in")
        s_prep = sem("t_dve_prep")
        s_wh = [sem(f"t_wh{n}") for n in range(NW + 1)]
        s_wl = [sem(f"t_wl{n}") for n in range(NW + 1)]
        s_wf = sem("t_ffn_weights")

        def at(it, u):
            return it * U + (u + 1)

        def perm(t):
            return t.rearrange("p (r s) -> p r s", s=8)

        raw_at = {W_KEY: 0, W_QRY: KC, W_BASE: 0}

        with nc.Block() as block2:

            @block2.sync
            def _(sp):
                def load_c(it, u):
                    sp.dma_start(cs[:, u, :], a["ctx"][:, it * U + u, :]).then_inc(s_cl[u], 16)

                def load_x(it, u):
                    sp.dma_start(xs[:, u, :], a["x"][:, it * U + u, :]).then_inc(s_xl[u], 16)

                for u in range(U):
                    load_c(0, u)
                sp.dma_start(stage[:, 0:KC, :], a["w_key"]).then_inc(s_raw[W_KEY], 16)
                sp.dma_start(rows[:, :, :], a["rows"].partition_broadcast(P)).then_inc(s_rest, 16)
                for u in range(U):
                    load_x(0, u)
                sp.dma_start(stage[:, KC:2 * KC, :], a["w_qry"]).then_inc(s_raw[W_QRY], 16)
                sp.wait_ge(s_wl[W_KEY], KC)
                sp.dma_start(stage[:, 0:KC, :], a["w_base"]).then_inc(s_raw[W_BASE], 16)
                sp.wait_ge(s_wl[W_QRY], KC)
                sp.dma_start(stage[:, KC:KC + 2, :].rearrange("p a (b n) -> p (a b) n", b=2),
                             a["w_ra"]).then_inc(s_rra, 16)
                for u in range(U):
                    sp.wait_ge(S["pv"], at(0, u))
                    load_c(1, u)
                for u in range(U):
                    sp.wait_ge(S["x4"], at(0, u))
                    sp.dma_start(out[u, :, :], xs[:, u, :]).then_inc(s_st[u], 16)
                for u in range(U):
                    sp.wait_ge(s_st[u], 16)
                    load_x(1, u)
                for u in range(U):
                    sp.wait_ge(S["x4"], at(1, u))
                    sp.dma_start(out[U + u, :, :], xs[:, u, :]).then_inc(s_st[u], 16)
                for u in range(U):
                    sp.wait_ge(s_st[u], 32)

            @block2.gpsimd
            def _(pool):
                def root(it, sig, dst, src, done):
                    for u in range(U):
                        pool.wait_ge(S[sig], at(it, u))
                        pool.tensor_tensor(sc1[:, u, dst:dst + 1], sc1[:, u, src:src + 1], mhalf[:, 0:1],
                                           ALU.pow).then_inc(S[done], 1)

                with pool.Fori(0, IT) as it:
                    root(it, "k_ms", K_RR, K_MS, "k_rr")
                    root(it, "ve0", S_RS, S_VE, "rs0")
                    root(it, "k2_ms", K_RR, K_MS, "k2_rr")
                    root(it, "ve1", S_RS, S_VE, "rs1")
                    root(it, "q_ms", S_RR, S_MS, "q_rr")
                    root(it, "ve2", S_RS, S_VE, "rs2")

            @block2.scalar
            def _(act):
                act.dma_start(qw[:, :], a["qw"]).then_inc(s_raw[W_FFN], 16)
                act.dma_start(zq[:, :], a["zq"]).then_inc(s_raw[W_FFN], 16)
                act.dma_start(scl[:, :], a["scl"]).then_inc(s_raw[W_FFN], 16)
                act.dma_start(wbm[:, :], a["w_bm"]).then_inc(s_rest, 16)
                act.dma_start(rb[:, :], a["rb"].partition_broadcast(P)).then_inc(s_rest, 16)
                act.dma_start(emap_i[:, :], a["emap"].partition_broadcast(P)).then_inc(s_rest, 16)
                act.dma_start(consts[:, :], a["consts"].partition_broadcast(P)).then_inc(s_rest, 16)

                def w_hi(n):
                    act.wait_ge(s_raw[n], 16)
                    for c in range(KC):
                        act.activation(wt[n][:, 0, c, :], stage[:, raw_at[n] + c, :], ACT.Copy).then_inc(s_wh[n], 1)

                def squares(it, sig, src, junk, col, done):
                    for u in range(U):
                        if sig is None:
                            act.wait_ge(s_cl[u], it * 16 + 16)
                        else:
                            act.wait_ge(S[sig], at(it, u))
                        act.activation(junk(u), src(u), ACT.Square,
                                       accum_out=sc1[:, u, col:col + 1]).then_inc(S[done], 1)

                def split_hi(it, t, bank0, done, used=None):
                    for u in range(U):
                        act.wait_ge(S[t], at(it, u))
                        if used:
                            act.wait_ge(S[used], at(it, u))
                        act.activation(tt[:, u, 0, :, :], bank[bank0 + u][:, :].rearrange("p (c t) -> p c t", c=KC),
                                       ACT.Copy).then_inc(S[done], 1)

                def weighted(it, t, bank0, dst, col, done):
                    for u in range(U):
                        act.wait_ge(S[t], at(it, u))
                        for c in range(KC):
                            ins = act.activation(dst[:, u, c, :], bank[bank0 + u][:, c * P:(c + 1) * P], ACT.Copy,
                                                 scale=cols[:, col, c:c + 1])
                        ins.then_inc(S[done], 1)

                w_hi(W_KEY)
                for c in range(KC):
                    act.wait_ge(s_wf, c + 1)
                    act.activation(wt[W_FFN][:, 0, c, :], tmp[:, c, :], ACT.Copy).then_inc(s_wh[W_FFN], 1)
                w_hi(W_QRY)
                w_hi(W_BASE)
                act.wait_ge(s_rra, 16)
                act.activation(wra[:, 0, :, :].rearrange("p c n -> p (c n)"),
                               stage[:, KC:KC + 2, :].rearrange("p a n -> p (a n)"), ACT.Copy).then_inc(s_wh[NW], 1)
                with act.Fori(0, IT) as it:
                    squares(it, None, lambda u: cs[:, u, :], lambda u: tmpk[:, u, :], K_SS, "k_ss")
                    split_hi(it, "k_T", 0, "k_hi")
                    split_hi(it, "T0", 4, "hi0", used="k_mm")
                    squares(it, "k_b", lambda u: tmpk[:, u, :], lambda u: kt1[:, u, :, :].rearrange("p c t -> p (c t)"),
                            K_SS, "k2_ss")
                    weighted(it, "k_T2", 0, kt1, 2, "k_out")
                    split_hi(it, "T1", 4, "hi1")
                    squares(it, "q_b", lambda u: tmp[:, u, :], lambda u: qt1[:, u, :, :].rearrange("p c t -> p (c t)"),
                            S_SS, "q_ss")
                    weighted(it, "q_T", 4, qt1, 1, "q_out")
                    for u in range(U):
                        act.wait_ge(S["s_neg"], at(it, u))
                        act.activation(pr1[:, u, :], bank[u][:, 0:P], ACT.Exp, bias=sc1[:, u, S_NM:S_NM + 1],
                                       accum_out=sc1[:, u, S_ES:S_ES + 1]).then_inc(S["s_exp"], 1)
                    for u in range(U):
                        act.wait_ge(S["p_T"], at(it, u))
                        act.activation(pt1[:, u, :], bank[4 + u][:, 0:P], ACT.Copy).then_inc(S["p_out"], 1)
                    split_hi(it, "T2", 4, "hi2")
                    for u in range(U):
                        act.wait_ge(S["lg_neg"], at(it, u))
                        act.activation(rt[:, u, 1, 0:ROUT], rt[:, u, 0, 0:ROUT], ACT.Exp, bias=sc1[:, u, S_NM:S_NM + 1],
                                       accum_out=sc1[:, u, S_ES:S_ES + 1]).then_inc(S["lg_exp"], 1)
                    for u in range(U):
                        act.wait_ge(S["hw_T"], at(it, u))
                        act.activation(pt1[:, u, :], bank[4 + u][:, 0:P], ACT.Copy).then_inc(S["hw_out"], 1)

            @block2.vector
            def _(dve):
                steps = [0]

                def prep(ins):
                    steps[0] += 1
                    ins.then_inc(s_prep, 1)
                    dve.wait_ge(s_prep, steps[0])

                def w_lo(n):
                    for c in range(KC):
                        dve.wait_ge(s_wh[n], c + 1)
                        dve.tensor_tensor(wt[n][:, 1, c, :], stage[:, raw_at[n] + c, :],
                                          wt[n][:, 0, c, :].bitcast(fp32), ALU.subtract).then_inc(s_wl[n], 1)

                dve.wait_ge(s_raw[W_FFN], 48)
                for s in range(8):
                    ins = dve.tensor_scalar(zint[:, :].rearrange("p (j s) -> p j s", s=8)[:, :, s], zq[:, :], 4 * s, 15,
                                            ALU.logical_shift_right, ALU.bitwise_and)
                    ins.then_inc(s_prep, 1)
                steps[0] += 8
                dve.wait_ge(s_prep, steps[0])
                prep(dve.tensor_scalar(zint[:, :], zint[:, :], 1, None, ALU.add))
                w_lo(W_KEY)
                for c in range(KC):
                    for h in range(2):
                        ps = slice(h * 64, h * 64 + 64)
                        ins = dve.tensor_scalar(wint[ps, :], qw[ps, :], 4 * (2 * c + h), 15,
                                                ALU.logical_shift_right, ALU.bitwise_and).then_inc(s_prep, 1)
                    steps[0] += 2
                    dve.wait_ge(s_prep, steps[0])
                    prep(dve.tensor_tensor(tmp[:, c, :], wint[:, :], zint[:, :], ALU.subtract))
                    dve.tensor_tensor(tmp[:, c, :], tmp[:, c, :], scl[:, :], ALU.mult).then_inc(s_wf, 1)
                for c in range(KC):
                    dve.wait_ge(s_wh[W_FFN], c + 1)
                    dve.tensor_tensor(wt[W_FFN][:, 1, c, :], tmp[:, c, :], wt[W_FFN][:, 0, c, :].bitcast(fp32),
                                      ALU.subtract).then_inc(s_wl[W_FFN], 1)
                w_lo(W_QRY)
                w_lo(W_BASE)
                dve.wait_ge(s_wh[NW], 1)
                dve.tensor_tensor(wra[:, 1, :, :].rearrange("p c n -> p (c n)"),
                                  stage[:, KC:KC + 2, :].rearrange("p a n -> p (a n)"),
                                  wra[:, 0, :, :].rearrange("p c n -> p (c n)").bitcast(fp32),
                                  ALU.subtract).then_inc(s_wl[NW], 1)
                dve.wait_ge(s_rest, 80)
                prep(dve.tensor_copy(emap[:, :], emap_i[:, :]))
                prep(dve.tensor_tensor(onehot[:, :, :], emap[:, :].unsqueeze(1).to_broadcast([P, NEXP, ROUT]),
                                       consts[:, ROUT * ROUT:].unsqueeze(2).to_broadcast([P, NEXP, ROUT]), ALU.is_equal))
                prep(dve.tensor_scalar(onehot[:, :, :], onehot[:, :, :], LORA_SCALE, None, ALU.mult))
                tri = consts[:, 0:ROUT * ROUT].rearrange("p (n m) -> p n m", n=ROUT)

                def each(it, f, waits, done):
                    for u in range(U):
                        for w in waits:
                            dve.wait_ge(S[w], at(it, u))
                        f(u).then_inc(S[done], 1)

                def col(u, c):
                    return sc1[:, u, c:c + 1]

                def mean_square(it, src, dst, sig, done):
                    each(it, lambda u: dve.tensor_scalar(col(u, dst), col(u, src), 1.0 / D, EPS_RMS1, ALU.mult, ALU.add),
                         [sig], done)

                def stats_of(it, n, x):
                    each(it, lambda u: dve.bn_stats(st1[:, u, :], xs[:, u, :]), [x], f"bn{n}")
                    for u in range(U):
                        dve.wait_ge(s_prep, steps[0])
                        dve.wait_ge(S[f"bn{n}"], at(it, u))
                        dve.bn_aggr(mv1[:, u, :], st1[:, u, :]).then_inc(S[f"ag{n}"], 1)
                    each(it, lambda u: dve.tensor_scalar(col(u, S_VE), mv1[:, u, 1:2], EPS_LN, None, ALU.add),
                         [f"ag{n}"], f"ve{n}")

                def normed(it, n):
                    def f(u):
                        dst, src = tmp[:, u, :], xs[:, u, :]
                        if n == 0:
                            dst, src = dst.rearrange("p (s r) -> p r s", s=8), perm(src)
                        return dve.tensor_scalar(dst, src, mv1[:, u, 0:1], col(u, S_RS), ALU.subtract, ALU.mult)
                    each(it, f, [f"rs{n}"], f"xn{n}")

                def split_lo(it, hi, bank0, done):
                    each(it, lambda u: dve.tensor_tensor(
                        tt[:, u, 1, :, :], bank[bank0 + u][:, :].rearrange("p (c t) -> p c t", c=KC),
                        tt[:, u, 0, :, :].bitcast(fp32), ALU.subtract), [hi], done)

                def biased(it, sig, bank0, row, dst, done):
                    each(it, lambda u: dve.tensor_tensor(dst[:, u, :], bank[bank0 + u][:, :], rows[:, row, :], ALU.add),
                         [sig], done)

                def gated(it, sig, g, done, ahead=0):
                    for u in range(U):
                        dve.wait_ge(S[sig], at(it, u + ahead))
                        dve.scalar_tensor_tensor(out=xs[:, u, :], in0=tmp[:, u, :], scalar=tg[:, g:g + 1],
                                                 in1=xs[:, u, :], op0=ALU.mult, op1=ALU.add).then_inc(S[done], 1)

                dve.sem_inc(S["ob"], U)
                with dve.Fori(0, IT) as it:
                    mean_square(it, K_SS, K_MS, "k_ss", "k_ms")
                    for u in range(U):
                        dve.wait_ge(s_xl[u], it * 16 + 16)
                        dve.scalar_tensor_tensor(out=xs[:, u, :], in0=acc[:, bass.ds(it * U + u, 1), :].rearrange("p a d -> p (a d)"),
                                                 scalar=tg[:, 0:1], in1=xs[:, u, :],
                                                 op0=ALU.mult, op1=ALU.add).then_inc(S["x1"], 1)
                    each(it, lambda u: dve.scalar_tensor_tensor(out=cs[:, u, :], in0=cs[:, u, :], scalar=col(u, K_RR),
                                                                in1=rows[:, R_FN, :], op0=ALU.mult, op1=ALU.mult),
                         ["k_rr"], "k_fn")
                    stats_of(it, 0, "x1")
                    split_lo(it, "k_hi", 0, "k_lo")
                    normed(it, 0)
                    split_lo(it, "hi0", 4, "lo0")
                    biased(it, "k_mm", 0, R_BK, tmpk, "k_b")
                    mean_square(it, K_SS, K_MS, "k2_ss", "k2_ms")
                    biased(it, "y0", 4, R_FFN, tmp, "b0")
                    each(it, lambda u: dve.tensor_scalar(tmpk[:, u, :], tmpk[:, u, :], col(u, K_RR), None, ALU.mult),
                         ["k2_rr"], "k_n")
                    gated(it, "b0", 2, "x2")
                    stats_of(it, 1, "x2")
                    normed(it, 1)
                    split_lo(it, "hi1", 4, "lo1")
                    biased(it, "q_mm", 0, R_BQ, tmp, "q_b")
                    mean_square(it, S_SS, S_MS, "q_ss", "q_ms")
                    each(it, lambda u: dve.tensor_scalar(tmp[:, u, :], tmp[:, u, :], col(u, S_RR), float(D) ** -0.5,
                                                         ALU.mult, ALU.mult), ["q_rr"], "q_n")
                    each(it, lambda u: dve.tensor_reduce(col(u, S_NM), bank[u][:, 0:P], AX, ALU.max), ["s_mm"], "s_max")
                    each(it, lambda u: dve.tensor_scalar(col(u, S_NM), col(u, S_NM), -1.0, None, ALU.mult),
                         ["s_max"], "s_neg")
                    each(it, lambda u: dve.reciprocal(col(u, S_RI), col(u, S_ES)), ["s_exp"], "s_ri")
                    each(it, lambda u: dve.tensor_tensor(col(u, S_RI), col(u, S_RI), tg[:, 1:2], ALU.mult),
                         ["s_ri"], "s_rg")
                    each(it, lambda u: dve.scalar_tensor_tensor(out=xs[:, u, :], in0=bank[u][:, :], scalar=col(u, S_RI),
                                                                in1=xs[:, u, :], op0=ALU.mult, op1=ALU.add),
                         ["s_rg", "pv"], "x3")
                    stats_of(it, 2, "x3")
                    normed(it, 2)
                    split_lo(it, "hi2", 4, "lo2")
                    lg, ex, pk, cnt = (lambda u, i=i: rt[:, u, i, 0:ROUT] for i in range(4))
                    each(it, lambda u: dve.tensor_tensor(lg(u), bank[u][:, ER:ER + ROUT], rb[:, :], ALU.add),
                         ["ra"], "lg")
                    each(it, lambda u: dve.tensor_reduce(col(u, S_NM), lg(u), AX, ALU.max), ["lg"], "lg_max")
                    each(it, lambda u: dve.tensor_scalar(col(u, S_NM), col(u, S_NM), -1.0, None, ALU.mult),
                         ["lg_max"], "lg_neg")
                    each(it, lambda u: dve.reciprocal(col(u, S_RI), col(u, S_ES)), ["lg_exp"], "lg_ri")
                    each(it, lambda u: dve.tensor_scalar(ex(u), ex(u), col(u, S_RI), None, ALU.mult), ["lg_ri"], "pr")
                    pm = lambda u: ex(u).unsqueeze(1).to_broadcast([P, ROUT, ROUT])
                    pn = lambda u: ex(u).unsqueeze(2).to_broadcast([P, ROUT, ROUT])
                    each(it, lambda u: dve.tensor_tensor(cmp[:, u, 0, :, :], pm(u), pn(u), ALU.is_gt), ["pr"], "gt")
                    each(it, lambda u: dve.tensor_tensor(cmp[:, u, 1, :, :], pm(u), pn(u), ALU.is_equal), ["pr"], "eq")
                    each(it, lambda u: dve.tensor_tensor(cmp[:, u, 1, :, :], cmp[:, u, 1, :, :], tri, ALU.mult),
                         ["eq"], "tri")
                    each(it, lambda u: dve.tensor_tensor(cmp[:, u, 0, :, :], cmp[:, u, 0, :, :], cmp[:, u, 1, :, :],
                                                         ALU.add), ["gt", "tri"], "cnt")
                    each(it, lambda u: dve.tensor_reduce(cnt(u), cmp[:, u, 0, :, :], AX, ALU.add), ["cnt"], "rank")
                    each(it, lambda u: dve.scalar_tensor_tensor(out=pk(u), in0=cnt(u), scalar=float(NEXP), in1=ex(u),
                                                                op0=ALU.is_lt, op1=ALU.mult), ["rank"], "keep")
                    each(it, lambda u: dve.tensor_tensor(wexp[:, u, :, :], onehot[:, :, :],
                                                         pk(u).unsqueeze(1).to_broadcast([P, NEXP, ROUT]), ALU.mult),
                         ["keep"], "we")
                    each(it, lambda u: dve.tensor_reduce(wsum[:, u, :], wexp[:, u, :, :], AX, ALU.add), ["we"], "ws")
                    each(it, lambda u: dve.tensor_tensor(
                        tmp[:, u, 0:ER].rearrange("p (e r) -> p e r", e=NEXP),
                        bank[u][:, 0:ER].rearrange("p (e r) -> p e r", e=NEXP),
                        wsum[:, u, :].unsqueeze(2).to_broadcast([P, NEXP, RANK]), ALU.mult), ["ws"], "hw")
                    biased(it, "o_mm", 0, R_BASE, tmp, "ob")
                    gated(it, "ob", 3, "x4", ahead=U)

            @block2.tensor
            def _(pe):
                def transpose(it, waits, src, bank0, done, n=KC):
                    for u in range(U):
                        for w in waits:
                            pe.wait_ge(S[w], at(it, u))
                        for c in range(n):
                            mm = pe.transpose(bank[bank0 + u][:, c * P:(c + 1) * P], src(u)[:, c * P:(c + 1) * P],
                                              ident[:, :])
                        mm.then_inc(S[done], 1)

                def product(it, waits, w, n, bank0, done, more=None):
                    for u in range(U):
                        for x in waits:
                            pe.wait_ge(S[x], at(it, u))
                        for c in range(KC):
                            for i, j in PASSES:
                                mm = pe.matmul(bank[bank0 + u][:, 0:n], tt[:, u, i, c, :], w[:, j, c, :],
                                               start=(c == 0 and i + j == 0), stop=(c == KC - 1 and i == 1 and not more))
                        if more:
                            mm = more(u)
                        mm.then_inc(S[done], 1)

                with pe.Fori(0, IT) as it:
                    for u in range(U):
                        pe.wait_ge(S["ob"], at(it, u))
                    transpose(it, ["k_fn"], lambda u: cs[:, u, :], 0, "k_T")
                    transpose(it, ["xn0"], lambda u: tmp[:, u, :], 4, "T0")
                    pe.wait_ge(s_wl[W_KEY], KC)
                    product(it, ["k_lo"], wt[W_KEY], D, 0, "k_mm")
                    pe.wait_ge(s_wl[W_FFN], KC)
                    product(it, ["lo0"], wt[W_FFN], D, 4, "y0")
                    transpose(it, ["k_n"], lambda u: tmpk[:, u, :], 0, "k_T2")
                    transpose(it, ["xn1"], lambda u: tmp[:, u, :], 4, "T1")
                    pe.wait_ge(s_wl[W_QRY], KC)
                    product(it, ["lo1", "k_out"], wt[W_QRY], D, 0, "q_mm")
                    transpose(it, ["q_n"], lambda u: tmp[:, u, :], 4, "q_T")
                    for u in range(U):
                        pe.wait_ge(S["q_out"], at(it, u))
                        for c in range(KC):
                            mm = pe.matmul(bank[u][:, 0:P], qt1[:, u, c, :], kt1[:, u, c, :], start=(c == 0), stop=(c == KC - 1))
                        mm.then_inc(S["s_mm"], 1)
                    transpose(it, ["s_exp"], lambda u: pr1[:, u, :], 4, "p_T", n=1)
                    for u in range(U):
                        pe.wait_ge(S["p_out"], at(it, u))
                        pe.matmul(bank[u][:, :], pt1[:, u, :], cs[:, u, :], start=True, stop=True).then_inc(S["pv"], 1)
                    transpose(it, ["xn2"], lambda u: tmp[:, u, :], 4, "T2")
                    pe.wait_ge(s_wl[NW], 1)
                    product(it, ["lo2"], wra, RAW, 0, "ra")
                    transpose(it, ["hw"], lambda u: tmp[:, u, :], 4, "hw_T", n=1)
                    pe.wait_ge(s_wl[W_BASE], KC)
                    product(it, ["hw_out"], wt[W_BASE], D, 0, "o_mm",
                            more=lambda u: pe.matmul(bank[u][:, :], pt1[:, u, :], wbm[:, :], start=False, stop=True))


def kernel(**inputs):
    import concourse.bacc as _bacc
    from concourse.bass_utils import run_bass_kernel_spmd as _run

    x = {k: np.asarray(v) for k, v in inputs.items()}
    lay = {}

    def head_major(w):
        return w.reshape(HEADS, P, KC, P).transpose(0, 3, 2, 1).reshape(HEADS, P, D)

    wq, wk = head_major(x["L0_xattn_w_q"]), head_major(x["L0_xattn_w_k"])
    wv = x["L0_xattn_w_v"].reshape(GROUPS, GH * P, KC, P).transpose(0, 2, 3, 1)
    wo = x["L0_xattn_w_out"].reshape(D, GROUPS, GH, P).transpose(1, 2, 3, 0)
    src = {"q": wq.reshape(GROUPS, GH, P, D), "k": wk.reshape(GROUPS, GH, P, D), "v": wv, "o": wo}
    w0 = np.stack([src[c[0]][:, int(c[1])] for c in CHUNKS], axis=1)
    lay["w0"] = w0.reshape(GROUPS * NCH // 2, 2, P, D).transpose(0, 2, 1, 3)
    lay["bias"] = x["L0_xattn_position_bias"].reshape(GROUPS, GH, P, P).transpose(0, 2, 1, 3)
    lay["x"] = x["x"].transpose(1, 0, 2)
    lay["ctx"] = x["ctx_4096"].transpose(1, 0, 2)
    lay["mask"] = x["mask_BxSxS2_bk0"].transpose(1, 0, 2)
    lay["gates"] = np.concatenate([x["g_xattn"], x["g_ffn"]])
    lay["cols"] = np.stack([x[k].reshape(KC, P).T for k in
                            ("L0_xattn_ln_weight", "L1_xattn_qn_w", "L1_xattn_kn_w")], axis=1)
    lay["ident"] = np.eye(P, dtype=np.float32)
    inner = lambda w: w.reshape(w.shape[0], KC, P).transpose(2, 1, 0)
    lay["w_key"] = inner(x["L1_xattn_Wk_w"])
    lay["w_qry"] = inner(x["L1_xattn_Wq_w"])
    lay["w_base"] = inner(x["L1_ffn_base_W"])
    lay["w_ra"] = inner(np.concatenate([x["L1_ffn_A"].reshape(ER, D), x["L1_ffn_router_W"],
                                        np.zeros((RAW - ER - ROUT, D), np.float32)]))
    lay["w_bm"] = x["L1_ffn_B"].transpose(0, 2, 1).reshape(ER, D)
    lay["rows"] = np.stack([x[k] for k in ("L0_ffn_bias", "L1_xattn_fn_w", "L1_xattn_Wq_b",
                                           "L1_xattn_Wk_b", "L1_ffn_base_b")])
    lay["rb"] = x["L1_ffn_router_b"]
    lay["emap"] = x["L1_ffn_expert_map"]
    lay["consts"] = np.concatenate([np.tril(np.ones((ROUT, ROUT), np.float32), -1).ravel(),
                                    np.arange(NEXP, dtype=np.float32)])
    lay["qw"] = np.tile(x["L0_ffn_qweight"], (2, 1))
    rep = P // 2 // KC
    lay["zq"] = np.tile(np.repeat(x["L0_ffn_qzeros"], rep, axis=0), (2, 1))
    lay["scl"] = np.tile(np.repeat(x["L0_ffn_scales"], rep, axis=0), (2, 1))

    nc = _bacc.Bacc("TRN2", target_bir_lowering=False, num_devices=1)
    arrays, aps = {}, {}
    for k, v in lay.items():
        v = np.ascontiguousarray(v)
        arrays[f"in_{k}"] = v
        dt = mybir.dt.uint8 if v.dtype == bool else mybir.dt.from_np(v.dtype)
        aps[k] = nc.dram_tensor(f"in_{k}", v.shape, dt, kind="ExternalInput").ap()
    out = nc.dram_tensor("out_0", (B, P, D), mybir.dt.float32, kind="ExternalOutput").ap()
    build(nc, aps, out)
    r = _run(nc, [arrays], core_ids=[0])
    return r.results[0]["out_0"]
```

```python
from contextlib import ExitStack

import concourse.bass as bass
from concourse import mybir
import numpy as np

P = 128
B = 8
D = 512
KC = D // P
TOK = B * P
HEADS = 32
GH = 4
GROUPS = HEADS // GH
NEXP = 8
RANK = 16
ER = NEXP * RANK
ROUT = 2 * NEXP - 1
RAW = 256
LORA_SCALE = 2.0
EPS_LN = 1e-5
EPS_RMS0 = 1e-5
EPS_RMS1 = 1e-6
MASKED = -1e30

CHUNKS = ["k0", "v0", "v1", "v2", "v3", "q0", "k1", "q1", "o0", "o1", "o2", "o3", "k2", "q2", "k3", "q3"]
NCH = len(CHUNKS)
SLOTS = 8
UNITS = (["k0a", "k0b"] + [f"v{b}" for b in range(B)] + ["q0a", "q0b"]
         + [f"{t}{h}{s}" for h in range(1, GH) for t in "kq" for s in "ab"]
         + [f"o{b}" for b in range(B)] + [f"p{b}" for b in range(B)])
NUNIT = len(UNITS)
RING = 4
ACT_UNITS = [u for u in UNITS if u[0] in "qkv"]
DVE_UNITS = [u for u in UNITS if u[0] in "op"]
PASSES = ((0, 0), (0, 1), (1, 0))


def build(nc, a, out):
    fp32, fp32r, i32, u8 = mybir.dt.float32, mybir.dt.float32r, mybir.dt.int32, mybir.dt.uint8
    ALU, ACT, AX = mybir.AluOpType, mybir.ActivationFunctionType, mybir.AxisListType.X

    cursor = [-(-nc.sbuf_base // 64) * 64]

    def place(name, shape, dt):
        size = int(np.prod(shape[1:])) * (1 if dt == u8 else 4)
        t = nc.alloc_sbuf_tensor_at(name, shape, dt, offset=cursor[0])
        cursor[0] += -(-size // 64) * 64
        assert cursor[0] <= nc.sbuf_usable_end, (name, cursor[0])
        return t

    acc = place("acc", [P, B, D], fp32)
    stage = place("stage", [P, SLOTS, D], fp32)
    ident = place("ident", [P, P], fp32)
    gates = place("gates", [P, 4], fp32)
    tg = place("tg", [P, 4], fp32)
    cols = place("cols", [P, 3, KC], fp32)
    mhalf = place("mhalf", [P, B], fp32)
    small0 = cursor[0]

    xt = place("xt", [P, 2, KC, TOK], fp32r)
    ct = place("ct", [P, 2, KC, TOK], fp32r)
    after_xc = cursor[0]
    wq = place("wq", [P, 2, KC, P], fp32r)
    wk = place("wk", [P, 2, KC, P], fp32r)
    wvo = place("wvo", [P, 2, KC, D], fp32r)
    bias = place("bias", [P, GH, P], fp32)
    maskneg = place("maskneg", [P, B, P], fp32)
    bm = place("bm", [P, 2, B, P], fp32)
    qt = place("qt", [P, TOK], fp32)
    kt = place("kt", [P, TOK], fp32)
    vals = place("vals", [P, B, D], fp32)
    prob = place("prob", [P, B, P], fp32)
    pt_at = cursor[0]
    pt = place("pt", [P, B, P], fp32)
    ao_at = cursor[0]
    ao = place("ao", [P, GH, 2, TOK], fp32r)
    anykey = place("anykey", [P, B], fp32)
    nmax = place("nmax", [P, B], fp32)
    esum = place("esum", [P, B], fp32)
    rinv = place("rinv", [P, B], fp32)
    stats = place("stats", [P, B, 6], fp32)
    mv = place("mv", [P, B, 2], fp32)
    vsum = place("vsum", [P, B], fp32)
    rstd = place("rstd", [P, B], fp32)
    rscale = place("rscale", [P, B], fp32)
    msq = place("msq", [P, B], fp32)
    rrms = place("rrms", [P, B], fp32)
    cursor[0] = ao_at
    craw = place("craw", [P, B, D], fp32)
    xraw = place("xraw", [P, B, D], fp32)
    masku = nc.alloc_sbuf_tensor_at("masku", [P, B, P], u8, offset=pt_at)
    maskf = prob

    cursor[0] = small0
    cs = place("cs", [P, B, D], fp32)
    wt_a = place("wt_a", [P, 2, KC, D], fp32r)
    wt_f = place("wt_f", [P, 2, KC, D], fp32r)
    kt1_at = cursor[0]
    kt1 = place("kt1", [P, B, KC, P], fp32)
    assert cursor[0] == after_xc
    cursor[0] = kt1_at
    qw = place("qw", [P, D], i32)
    zq = place("zq", [P, D // 8], i32)
    zint = place("zint", [P, D], i32)
    wint = place("wint", [P, D], i32)
    scl = place("scl", [P, D], fp32)
    cursor[0] = after_xc
    wt_q = place("wt_q", [P, 2, KC, D], fp32r)
    tmp = place("tmp", [P, B, D], fp32)
    HB = B // 2
    tt = place("tt", [P, HB, 2, KC, P], fp32r)
    qt1 = place("qt1", [P, B, KC, P], fp32)
    qf = qt1[:, :, :, :].rearrange("p u c t -> p u (c t)")
    wra = place("wra", [P, 2, KC, RAW], fp32r)
    wbm = place("wbm", [P, D], fp32)
    rows = place("rows", [P, 5, D], fp32)
    R_FFN, R_FN, R_BQ, R_BK, R_BASE = range(5)
    rb = place("rb", [P, ROUT], fp32)
    emap_i = place("emap_i", [P, ROUT], i32)
    emap = place("emap", [P, ROUT], fp32)
    consts = place("consts", [P, ROUT * ROUT + NEXP], fp32)
    onehot = place("onehot", [P, NEXP, ROUT], fp32)
    pr1 = place("pr1", [P, B, P], fp32)
    pt1 = place("pt1", [P, B, P], fp32)
    cmp = place("cmp", [P, 2, HB, ROUT, ROUT], fp32)
    wexp = place("wexp", [P, HB, NEXP, ROUT], fp32)
    wsum = place("wsum", [P, B, NEXP], fp32)
    rt = place("rt", [P, 4, B, ROUT], fp32)
    st1 = place("st1", [P, B, 6], fp32)
    mv1 = place("mv1", [P, B, 2], fp32)
    kss, kms, krr, ve1, rs1, nmr, qss, qms, qrr, nm1, es1, ri1 = (
        place(n, [P, B], fp32) for n in ("kss", "kms", "krr", "ve1", "rs1", "nmr", "qss", "qms", "qrr", "nm1", "es1", "ri1"))

    ctx = ExitStack()
    with ctx:
        bank = [ctx.enter_context(nc.psum_tensor(f"bank{i}", [P, D], fp32)) for i in range(8)]

        def sem(name):
            return ctx.enter_context(nc.semaphore(name))

        s_const = sem("const_in")
        s_cin = [sem(f"ctx_in{q}") for q in range(4)]
        s_xin = [sem(f"x_in{q}") for q in range(2)]
        s_min = sem("mask_in")
        s_bias = sem("bias_in")
        s_stage = [sem(f"stage_in{i}") for i in range(SLOTS // 2)]
        s_d = sem("dve_prep")
        s_a = sem("act_prep")
        s_g = sem("pool_prep")
        s_cT = sem("ctx_transposed")
        s_xT = sem("x_transposed")
        s_chi = sem("ctx_hi")
        s_clo = sem("ctx_lo")
        s_xhi = sem("x_hi")
        s_xlo = sem("x_lo")
        s_mneg = sem("maskneg_done")
        s_h = sem("layernorm_x")
        s_xr = sem("rmsnorm_x")
        s_mf = sem("mask_steps")
        s_whi = sem("weights_hi")
        s_wlo = sem("weights_lo")
        s_bm = sem("biasmask_done")
        s_unit = sem("unit_done")
        s_aev = sem("act_emptied")
        s_dev = sem("dve_emptied")
        s_s = sem("scores_done")
        s_sadd = sem("scores_read")
        s_smax = sem("scores_max")
        s_nmax = sem("negmax_done")
        s_exp = sem("exp_done")
        s_rinv = sem("rinv_steps")
        s_p = sem("probs_scaled")
        s_pt = sem("pt_done")
        s_pte = sem("pt_emptied")
        s_pv = sem("pv_done")
        s_aohi = sem("ao_hi")
        s_aolo = sem("ao_lo")
        s_out = sem("stored")

        ahead = SLOTS // 2
        npairs = GROUPS * NCH // 2
        ix = {c: i for i, c in enumerate(CHUNKS)}
        un = {u: i for i, u in enumerate(UNITS)}
        ax = {u: i for i, u in enumerate(ACT_UNITS)}
        dx = {u: i for i, u in enumerate(DVE_UNITS)}
        half = lambda s: slice(s * 512, s * 512 + 512)

        names = ["k_ss", "k_ms", "k_rr", "k_fn", "k_T", "k_hi", "k_lo", "k_mm", "k_b", "k2_ss", "k2_ms", "k2_rr",
                 "k_n", "k_T2", "k_out", "x1", "y0", "x2", "q_mm", "q_b", "q_ss", "q_ms", "q_rr", "q_n", "q_T",
                 "q_outa", "q_outd", "s_mm", "s_max", "s_neg", "s_exp", "s_ri", "s_rg", "p_T", "p_out", "pv", "x3",
                 "ra", "ra_out", "lg_exp", "router", "hw", "hw_T", "hw_out", "o_mm", "x4", "rows", "rsf", "rsb", "gt", "o_mm2"]
        names += [f"{n}{i}" for i in range(3) for n in ("bn", "ag", "ve", "rs", "nr", "xn", "T", "hi", "lo")]
        S = {n: sem(f"t_{n}") for n in names}
        s_cl = [sem(f"t_ctx_in{q}") for q in range(2)]
        s_xl = [sem(f"t_x_in{q}") for q in range(2)]
        s_rk, s_rf, s_rq, s_rbase, s_rra, s_rest = (sem(f"t_raw_{n}") for n in ("key", "ffn", "query", "base", "ra", "rest"))
        s_wh = sem("t_weights_hi")
        s_wl = sem("t_weights_lo")
        s_wf = sem("t_ffn_weights")
        W_KEY, W_FFN, W_QRY, W_BASE, W_RA = (KC * n for n in range(5))
        s_prep = sem("t_dve_prep")
        last_proj = GROUPS * NUNIT + un[f"q{GH - 1}b"] + 1
        last_unit = (GROUPS + 1) * NUNIT
        HALVES = [range(0, HB), range(HB, B)]
        part = lambda q: slice(q * HB, q * HB + HB)
        def wchunk(n, c):
            if n == W_RA:
                raw = stage[:, 0:2, :].rearrange("p a (b n) -> p (a b) n", b=2)[:, c, :]
                return raw, wra[:, 0, c, :], wra[:, 1, c, :]
            slot = {W_KEY: 0, W_FFN: KC, W_QRY: 0, W_BASE: KC}[n]
            w = {W_KEY: wt_a, W_FFN: wt_f, W_QRY: wt_q, W_BASE: wt_a}[n]
            return stage[:, slot + c, :], w[:, 0, c, :], w[:, 1, c, :]

        with nc.Block() as block:

            @block.sync
            def _(sp):
                for q in range(4):
                    sp.dma_start(craw[:, 2 * q:2 * q + 2, :], a["ctx"][:, 2 * q:2 * q + 2, :]).then_inc(s_cin[q], 16)

                def load(pair, slot):
                    sp.dma_start(stage[:, 2 * slot:2 * slot + 2, :], a["w0"][pair, :, :, :]).then_inc(s_stage[slot], 16)

                for j in range(ahead):
                    load(j, j)
                    if j == 2:
                        for q in range(2):
                            sp.dma_start(xraw[:, 4 * q:4 * q + 4, :], a["x"][:, 4 * q:4 * q + 4, :]).then_inc(s_xin[q], 16)
                sp.dma_start(masku[:, :, :], a["mask"]).then_inc(s_min, 16)
                sp.dma_start(bias[:, :, :], a["bias"][0, :, :, :]).then_inc(s_bias, 16)
                with sp.Fori(0, GROUPS - 1) as g:
                    for j in range(NCH // 2):
                        sp.wait_ge(s_wlo, g * NCH + 2 * j + 2)
                        load(g * (NCH // 2) + (j + ahead), j % ahead)
                    sp.wait_ge(s_bm, g * GH + GH)
                    sp.dma_start(bias[:, :, :], a["bias"][g + 1, :, :, :]).then_inc(s_bias, 16)
                for j in range(NCH // 2 - ahead):
                    sp.wait_ge(s_wlo, (GROUPS - 1) * NCH + 2 * j + 2)
                    load((GROUPS - 1) * (NCH // 2) + j + ahead, j % ahead)

                sp.wait_ge(s_unit, last_proj)
                for q in range(2):
                    sp.dma_start(cs[:, part(q), :], a["ctx"][:, part(q), :]).then_inc(s_cl[q], 16)
                sp.wait_ge(s_wlo, GROUPS * NCH)
                sp.dma_start(stage[:, 0:KC, :], a["w_key"]).then_inc(s_rk, 16)
                sp.dma_start(qw[:, :], a["qw"]).then_inc(s_rf, 16)
                sp.dma_start(zq[:, :], a["zq"]).then_inc(s_rf, 16)
                sp.dma_start(scl[:, :], a["scl"]).then_inc(s_rf, 16)
                sp.wait_ge(s_unit, last_unit)
                sp.dma_start(rows[:, :, :], a["rows"].partition_broadcast(P)).then_inc(s_rest, 16)
                for q in range(2):
                    sp.dma_start(tmp[:, part(q), :], a["x"][:, part(q), :]).then_inc(s_xl[q], 16)
                sp.wait_ge(s_wl, W_KEY + KC)
                sp.dma_start(stage[:, 0:KC, :], a["w_qry"]).then_inc(s_rq, 16)
                sp.dma_start(wbm[:, :], a["w_bm"]).then_inc(s_rest, 16)
                sp.dma_start(rb[:, :], a["rb"].partition_broadcast(P)).then_inc(s_rest, 16)
                sp.dma_start(emap_i[:, :], a["emap"].partition_broadcast(P)).then_inc(s_rest, 16)
                sp.dma_start(consts[:, :], a["consts"].partition_broadcast(P)).then_inc(s_rest, 16)
                sp.wait_ge(s_wl, W_FFN + KC)
                sp.dma_start(stage[:, KC:2 * KC, :], a["w_base"]).then_inc(s_rbase, 16)
                sp.wait_ge(s_wl, W_QRY + KC)
                sp.dma_start(stage[:, 0:2, :].rearrange("p a (b n) -> p (a b) n", b=2), a["w_ra"]).then_inc(s_rra, 16)
                for u in range(B):
                    sp.wait_ge(S["x4"], u + 1)
                    sp.dma_start(out[u, :, :], acc[:, u, :]).then_inc(s_out, 16)
                sp.wait_ge(s_out, 16 * B)

            @block.gpsimd
            def _(pool):
                pool.memset(mhalf[:, :], -0.5).then_inc(s_g, 1)
                pool.wait_ge(s_g, 1)
                def w_lo(g, c):
                    i = ix[c]
                    kind, h = c[0], int(c[1])
                    src = stage[:, i % SLOTS, :]
                    if kind in "qk":
                        w = wq if kind == "q" else wk
                        hi, lo = (w[:, s, :, :].rearrange("p c d -> p (c d)") for s in (0, 1))
                    else:
                        hi, lo = wvo[:, 0, h, :], wvo[:, 1, h, :]
                    pool.wait_ge(s_whi, g * NCH + i + 1)
                    pool.tensor_tensor(lo, src, hi.bitcast(fp32), ALU.subtract).then_inc(s_wlo, 1)

                def biasmask(g, h):
                    if h == 0:
                        pool.wait_ge(s_bias, g * 16 + 16)
                    pool.wait_ge(s_sadd, g * 2 * GH + 2 * h + 1)
                    pool.tensor_tensor(bm[:, h % 2, :, :], maskneg[:, :, :],
                                       bias[:, h:h + 1, :].to_broadcast([P, B, P]), ALU.add).then_inc(s_bm, 1)

                def rest(g):
                    w_lo(g, "q0")
                    biasmask(g, 0)
                    for c in ("k1", "q1", "o0", "o1", "o2", "o3"):
                        w_lo(g, c)
                    biasmask(g, 1)
                    w_lo(g, "k2")
                    w_lo(g, "q2")
                    biasmask(g, 2)
                    w_lo(g, "k3")
                    w_lo(g, "q3")
                    biasmask(g, 3)

                first = ("k0", "v0", "v1", "v2", "v3")
                for c in first:
                    w_lo(0, c)
                pool.wait_ge(s_d, 2 * B + 1)
                pool.tensor_tensor(rstd[:, :], vsum[:, :], mhalf[:, :], ALU.pow).then_inc(s_g, 1)
                pool.wait_ge(s_d, 2 * B + 3)
                pool.tensor_tensor(rrms[:, :], msq[:, :], mhalf[:, :], ALU.pow).then_inc(s_g, 1)
                pool.wait_ge(s_mneg, 1)
                rest(0)
                with pool.Fori(1, GROUPS) as g:
                    for c in first:
                        w_lo(g, c)
                    rest(g)

                def w_split_lo(n):
                    for c in range(KC):
                        raw, hi, lo = wchunk(n, c)
                        pool.wait_ge(s_wh, n + c + 1)
                        pool.tensor_tensor(lo, raw, hi.bitcast(fp32), ALU.subtract).then_inc(s_wl, 1)

                def add_row(q, row, xn, done):
                    pool.wait_ge(S["rows"], 2)
                    for u in HALVES[q]:
                        pool.wait_ge(S[xn], u + 1)
                        pool.tensor_tensor(acc[:, u, :], acc[:, u, :], rows[:, row, :], ALU.add).then_inc(S[done], 1)

                def half_root(q, sig, dst, src, done):
                    pool.wait_ge(S[sig], q + 1)
                    pool.tensor_tensor(dst[:, part(q)], src[:, part(q)], mhalf[:, 0:HB], ALU.pow).then_inc(S[done], 1)

                w_split_lo(W_KEY)
                for q in range(2):
                    half_root(q, "k_ms", krr, kms, "k_rr")
                w_split_lo(W_FFN)
                for q in range(2):
                    half_root(q, "ve0", rs1, ve1, "rs0")
                w_split_lo(W_QRY)
                for q in range(2):
                    add_row(q, R_FFN, "xn0", "rsf")
                for q in range(2):
                    half_root(q, "k2_ms", krr, kms, "k2_rr")
                w_split_lo(W_BASE)
                half_root(0, "ve1", rs1, ve1, "rs1")
                half_root(1, "ve1", rs1, ve1, "rs1")
                w_split_lo(W_RA)
                for q in range(2):
                    half_root(q, "q_ms", qrr, qms, "q_rr")
                for q in range(2):
                    half_root(q, "ve2", rs1, ve1, "rs2")
                for q in range(2):
                    add_row(q, R_BASE, "xn2", "rsb")

            @block.scalar
            def _(act):
                act.dma_start(ident[:, :], a["ident"]).then_inc(s_const, 16)
                act.dma_start(gates[:, :], a["gates"].partition_broadcast(P)).then_inc(s_const, 16)
                act.dma_start(cols[:, :, :], a["cols"]).then_inc(s_const, 16)
                act.wait_ge(s_const, 48)
                act.activation(tg[:, :], gates[:, :], ACT.Tanh).then_inc(s_a, 1)
                for b in range(B):
                    act.wait_ge(s_cT, b + 1)
                    act.activation(ct[:, 0, :, b * P:(b + 1) * P], bank[b][:, :].rearrange("p (c t) -> p c t", c=KC),
                                   ACT.Copy).then_inc(s_chi, 1)
                def w_hi(g, c):
                    i = ix[c]
                    kind, h = c[0], int(c[1])
                    act.wait_ge(s_stage[i // 2 % ahead], g * 32 + 16 * (i // 2 // ahead) + 16)
                    if kind in "qk":
                        last = un[f"{kind}{h - 1}b"] + NUNIT if h else un[f"{kind}{GH - 1}b"]
                        hi = (wq if kind == "q" else wk)[:, 0, :, :].rearrange("p c d -> p (c d)")
                    else:
                        last = un[f"v{B - 1}"] + NUNIT if kind == "o" else un[f"{'p' if h == GH - 1 else 'o'}{B - 1}"]
                        hi = wvo[:, 0, h, :]
                    act.wait_ge(s_unit, g * NUNIT + last + 1)
                    act.activation(hi, stage[:, i % SLOTS, :], ACT.Copy).then_inc(s_whi, 1)

                def empty(g, u):
                    i = un[u]
                    act.wait_ge(s_unit, g * NUNIT + NUNIT + i + 1)
                    if u[0] == "v":
                        dst = vals[:, int(u[1]), :]
                    else:
                        dst = (qt if u[0] == "q" else kt)[:, half("ab".index(u[2]))]
                    act.activation(dst, bank[i % RING][:, :], ACT.Copy).then_inc(s_aev, 1)

                def exps(g, h):
                    for s in range(2):
                        act.wait_ge(s_nmax, g * 2 * GH + 2 * h + s + 1)
                        for b in range(4 * s, 4 * s + 4):
                            act.activation(prob[:, b, :], prob[:, b, :], ACT.Exp, bias=nmax[:, b:b + 1],
                                           accum_out=esum[:, b:b + 1]).then_inc(s_exp, 1)

                def ao_hi(g, h):
                    for s in range(2):
                        act.wait_ge(s_pv, g * 2 * GH + 2 * h + s + 1)
                        act.activation(ao[:, h, 0, half(s)], bank[6 + s][:, :], ACT.Copy).then_inc(s_aohi, 1)

                def x_hi(b):
                    act.wait_ge(s_xT, b + 1)
                    for c in range(KC):
                        act.activation(xt[:, 0, c, b * P:(b + 1) * P], bank[4 + b % 4][:, c * P:(c + 1) * P],
                                       ACT.Copy, scale=cols[:, 0, c:c + 1]).then_inc(s_xhi, 1)

                def group(g, first):
                    for c in ("k0", "v0", "v1", "v2", "v3"):
                        w_hi(g, c)
                    empty(g, "k0a")
                    empty(g, "k0b")
                    w_hi(g, "q0")
                    w_hi(g, "k1")
                    for b in range(B):
                        if first and b >= B - 2:
                            for x in range(4):
                                x_hi(4 * (b - B + 2) + x)
                        empty(g, f"v{b}")
                    empty(g, "q0a")
                    empty(g, "q0b")
                    w_hi(g, "q1")
                    for j in range(GH):
                        w_hi(g, f"o{j}")
                    exps(g, 0)
                    for h in range(1, GH):
                        empty(g, f"k{h}a")
                        empty(g, f"k{h}b")
                        if h < GH - 1:
                            w_hi(g, f"k{h + 1}")
                        empty(g, f"q{h}a")
                        empty(g, f"q{h}b")
                        if h < GH - 1:
                            w_hi(g, f"q{h + 1}")
                        ao_hi(g, h - 1)
                        exps(g, h)
                    ao_hi(g, GH - 1)

                group(0, True)
                with act.Fori(1, GROUPS) as g:
                    group(g, False)

                def w_split_hi(n, c, ready, count):
                    raw, hi, lo = wchunk(n, c)
                    act.wait_ge(ready, count)
                    act.activation(hi, raw, ACT.Copy).then_inc(s_wh, 1)

                def split_hi(u, t, used, done):
                    act.wait_ge(S[t], u + 1)
                    if used:
                        act.wait_ge(S[used], (u - HB if u >= HB else u + HB) + 1)
                    act.activation(tt[:, u % HB, 0, :, :], bank[u][:, :].rearrange("p (c t) -> p c t", c=KC),
                                   ACT.Copy).then_inc(S[done], 1)

                def squares(u, sig, src, junk, dst, done):
                    act.wait_ge(S[sig], u + 1)
                    act.activation(junk, src, ACT.Square, accum_out=dst[:, u:u + 1]).then_inc(S[done], 1)

                def normed(u, n):
                    act.wait_ge(S[f"nr{n}"], u // HB + 1)
                    dst, src = tmp[:, u, :], acc[:, u, :]
                    if n == 0:
                        dst, src = dst.rearrange("p (s r) -> p r s", s=8), src.rearrange("p (r s) -> p r s", s=8)
                    act.activation(dst, src, ACT.Identity, bias=nmr[:, u:u + 1],
                                   scale=rs1[:, u:u + 1]).then_inc(S[f"xn{n}"], 1)

                def weighted(u, t, dst, col, done):
                    act.wait_ge(S[t], u + 1)
                    for c in range(KC):
                        ins = act.activation(dst[:, u, c, :], bank[u][:, c * P:(c + 1) * P], ACT.Copy,
                                             scale=cols[:, col, c:c + 1])
                    ins.then_inc(S[done], 1)

                for c in range(KC):
                    if c == 0:
                        act.wait_ge(s_unit, last_proj)
                    w_split_hi(W_KEY, c, s_rk, 16)
                for u in range(B):
                    act.wait_ge(s_cl[u // HB], 16)
                    if u >= KC:
                        act.wait_ge(S["k_ss"], u - KC + 1)
                    act.activation(stage[:, KC + u % KC, :], cs[:, u, :], ACT.Square,
                                   accum_out=kss[:, u:u + 1]).then_inc(S["k_ss"], 1)
                act.wait_ge(s_unit, last_unit)
                for u in HALVES[0]:
                    split_hi(u, "k_T", None, "k_hi")
                w_split_hi(W_FFN, 0, s_wf, 1)
                w_split_hi(W_FFN, 1, s_wf, 2)
                split_hi(4, "k_T", "k_mm", "k_hi")
                split_hi(5, "k_T", "k_mm", "k_hi")
                w_split_hi(W_FFN, 2, s_wf, 3)
                split_hi(6, "k_T", "k_mm", "k_hi")
                split_hi(7, "k_T", "k_mm", "k_hi")
                w_split_hi(W_FFN, 3, s_wf, 4)
                for q in range(2):
                    for u in HALVES[q]:
                        normed(u, 0)
                    for u in HALVES[q]:
                        squares(u, "k_b", qf[:, u, :], kt1[:, u, :, :].rearrange("p c t -> p (c t)"), kss, "k2_ss")
                for u in HALVES[0]:
                    split_hi(u, "T0", "k_mm", "hi0")
                for c in range(KC):
                    w_split_hi(W_QRY, c, s_rq, 16)
                for u in HALVES[1]:
                    split_hi(u, "T0", "y0", "hi0")
                for c in range(KC):
                    if c == 0:
                        act.wait_ge(S["k_mm"], B)
                    w_split_hi(W_BASE, c, s_rbase, 16)
                for u in HALVES[0]:
                    normed(u, 1)
                for u in range(B):
                    weighted(u, "k_T2", kt1, 2, "k_out")
                for u in HALVES[0]:
                    split_hi(u, "T1", "y0", "hi1")
                for u in HALVES[1]:
                    normed(u, 1)
                for u in HALVES[0]:
                    squares(u, "q_b", tmp[:, u, :], qf[:, u, :], qss, "q_ss")
                for u in HALVES[1]:
                    split_hi(u, "T1", "q_mm", "hi1")
                for c in range(KC):
                    w_split_hi(W_RA, c, s_rra, 16)
                for u in HALVES[1]:
                    squares(u, "q_b", tmp[:, u, :], qf[:, u, :], qss, "q_ss")
                for u in range(0, B, 2):
                    weighted(u, "q_T", qt1, 1, "q_outa")
                for q in range(2):
                    for u in HALVES[q]:
                        act.wait_ge(S["s_neg"], q + 1)
                        act.activation(pr1[:, u, :], bank[u][:, 0:P], ACT.Exp, bias=nm1[:, u:u + 1],
                                       scale=float(D) ** -0.5, accum_out=es1[:, u:u + 1]).then_inc(S["s_exp"], 1)
                for u in range(B):
                    act.wait_ge(S["p_T"], u + 1)
                    act.activation(pt1[:, u, :], bank[u][:, 0:P], ACT.Copy).then_inc(S["p_out"], 1)
                for u in HALVES[0]:
                    normed(u, 2)

                def ra_out(u):
                    act.wait_ge(S["ra"], u + 1)
                    act.activation(qf[:, u, 0:ER + ROUT], bank[HB + u % HB][:, 0:ER + ROUT], ACT.Copy).then_inc(S["ra_out"], 1)

                def split_hi2(u):
                    act.wait_ge(S["T2"], u + 1)
                    if u >= HB:
                        act.wait_ge(S["o_mm"], u - HB + 1)
                    else:
                        act.wait_ge(S["q_mm"], u + HB + 1)
                    act.activation(tt[:, u % HB, 0, :, :], bank[u][:, :].rearrange("p (c t) -> p c t", c=KC),
                                   ACT.Copy).then_inc(S["hi2"], 1)

                def router_exp(q):
                    act.wait_ge(S["router"], 10 * q + 3)
                    act.activation(rt[:, 1, part(q), :], rt[:, 0, part(q), :], ACT.Exp).then_inc(S["lg_exp"], 1)

                def hw_out(u):
                    act.wait_ge(S["hw_T"], u + 1)
                    act.activation(pt1[:, u, :], bank[(u + HB) % B][:, 0:P], ACT.Copy).then_inc(S["hw_out"], 1)

                for u in HALVES[0]:
                    split_hi2(u)
                for u in HALVES[1]:
                    normed(u, 2)
                for u in HALVES[0]:
                    ra_out(u)
                router_exp(0)
                for u in HALVES[1]:
                    split_hi2(u)
                for u in HALVES[1]:
                    ra_out(u)
                for u in HALVES[0]:
                    hw_out(u)
                router_exp(1)
                for u in HALVES[1]:
                    hw_out(u)

            @block.vector
            def _(dve):
                dve.sem_inc(s_dev, len(DVE_UNITS))
                dve.sem_inc(s_sadd, 2)
                dve.sem_inc(s_aolo, 2)
                for b in range(B):
                    dve.wait_ge(s_chi, b + 1)
                    dve.tensor_tensor(ct[:, 1, :, b * P:(b + 1) * P], bank[b][:, :].rearrange("p (c t) -> p c t", c=KC),
                                      ct[:, 0, :, b * P:(b + 1) * P].bitcast(fp32), ALU.subtract).then_inc(s_clo, 1)
                for b in range(B):
                    if b % 4 == 0:
                        dve.wait_ge(s_xin[b // 4], 16)
                    dve.bn_stats(stats[:, b, :], xraw[:, b, :]).then_inc(s_d, 1)
                for b in range(B):
                    dve.wait_ge(s_d, b + 1)
                    dve.bn_aggr(mv[:, b, :], stats[:, b, :]).then_inc(s_d, 1)
                dve.wait_ge(s_d, 2 * B)
                dve.tensor_scalar(vsum[:, :], mv[:, :, 1], EPS_LN, None, ALU.add).then_inc(s_d, 1)
                dve.wait_ge(s_g, 2)
                dve.tensor_tensor(msq[:, :], rstd[:, :], rstd[:, :], ALU.mult).then_inc(s_d, 1)
                dve.wait_ge(s_d, 2 * B + 2)
                dve.tensor_tensor(rscale[:, :], msq[:, :], mv[:, :, 1], ALU.mult).then_inc(s_mf, 1)
                dve.wait_ge(s_mf, 1)
                dve.tensor_scalar(msq[:, :], rscale[:, :], EPS_RMS0, None, ALU.add).then_inc(s_d, 1)
                for b in range(B):
                    dve.tensor_scalar(acc[:, b, :], xraw[:, b, :], mv[:, b, 0:1], rstd[:, b:b + 1],
                                      ALU.subtract, ALU.mult).then_inc(s_h, 1)
                dve.wait_ge(s_g, 3)
                for b in range(B):
                    dve.wait_ge(s_h, b + 1)
                    dve.tensor_scalar(xraw[:, b, :], acc[:, b, :], rrms[:, b:b + 1], None, ALU.mult).then_inc(s_xr, 1)
                dve.wait_ge(s_min, 16)
                dve.tensor_copy(maskf[:, :, :], masku[:, :, :]).then_inc(s_mf, 1)
                dve.wait_ge(s_mf, 2)
                dve.tensor_scalar(maskneg[:, :, :], maskf[:, :, :], 1.0, -MASKED, ALU.subtract, ALU.mult).then_inc(s_mneg, 1)
                dve.tensor_reduce(anykey[:, :], maskf[:, :, :], AX, ALU.max).then_inc(s_mf, 1)
                for b in range(B):
                    dve.wait_ge(s_xhi, b * KC + KC)
                    for c in range(KC):
                        dve.scalar_tensor_tensor(out=xt[:, 1, c, b * P:(b + 1) * P], in0=bank[4 + b % 4][:, c * P:(c + 1) * P],
                                                 scalar=cols[:, 0, c:c + 1],
                                                 in1=xt[:, 0, c, b * P:(b + 1) * P].bitcast(fp32),
                                                 op0=ALU.mult, op1=ALU.subtract).then_inc(s_xlo, 1)
                dve.wait_ge(s_mf, 3)

                def softmax_in(g, h):
                    n = g * 2 * GH + 2 * h
                    dve.wait_ge(s_bm, g * GH + h + 1)
                    for s in range(2):
                        bs = slice(4 * s, 4 * s + 4)
                        dve.wait_ge(s_s, n + s + 1)
                        dve.tensor_tensor(prob[:, bs, :], bank[4 + s][:, :].rearrange("p (b k) -> p b k", b=4),
                                          bm[:, h % 2, bs, :], ALU.add).then_inc(s_sadd, 1)
                        dve.wait_ge(s_sadd, n + s + 3)
                        dve.tensor_reduce(rinv[:, bs], prob[:, bs, :], AX, ALU.max).then_inc(s_smax, 1)
                        dve.wait_ge(s_smax, n + s + 1)
                        dve.tensor_scalar(nmax[:, bs], rinv[:, bs], -1.0, None, ALU.mult).then_inc(s_nmax, 1)

                def softmax_out(g, h, s):
                    n = g * 2 * GH + 2 * h + s
                    bs = slice(4 * s, 4 * s + 4)
                    dve.wait_ge(s_exp, g * B * GH + h * B + 4 * s + 4)
                    dve.reciprocal(rinv[:, bs], esum[:, bs]).then_inc(s_rinv, 1)
                    dve.wait_ge(s_rinv, 2 * n + 1)
                    dve.tensor_tensor(rinv[:, bs], rinv[:, bs], anykey[:, bs], ALU.mult).then_inc(s_rinv, 1)
                    dve.wait_ge(s_rinv, 2 * n + 2)
                    dve.tensor_tensor(prob[:, bs, :], prob[:, bs, :],
                                      rinv[:, bs].unsqueeze(2).to_broadcast([P, 4, P]), ALU.mult).then_inc(s_p, 1)

                def pt_out(g, h):
                    for s in range(2):
                        dve.wait_ge(s_pt, g * 2 * GH + 2 * h + s + 1)
                        dve.tensor_copy(pt[:, 4 * s:4 * s + 4, :],
                                        bank[6 + s][:, :].rearrange("p (b k) -> p b k", b=4)).then_inc(s_pte, 1)

                def ao_lo(g, h):
                    for s in range(2):
                        dve.wait_ge(s_aohi, g * 2 * GH + 2 * h + s + 1)
                        dve.tensor_tensor(ao[:, h, 1, half(s)], bank[6 + s][:, :], ao[:, h, 0, half(s)].bitcast(fp32),
                                          ALU.subtract).then_inc(s_aolo, 1)

                def add_out(g, u):
                    i, b = un[u], int(u[1])
                    dve.wait_ge(s_unit, g * NUNIT + NUNIT + i + 1)
                    dve.wait_ge(s_dev, g * len(DVE_UNITS) + len(DVE_UNITS) + dx[u] - 7)
                    dve.tensor_tensor(acc[:, b, :], acc[:, b, :], bank[i % RING][:, :], ALU.add).then_inc(s_dev, 1)

                with dve.Fori(0, GROUPS) as g:
                    for h in range(GH):
                        softmax_in(g, h)
                        if h == 3:
                            add_out(g, "o0")
                            add_out(g, "o1")
                        softmax_out(g, h, 0)
                        if h == 3:
                            add_out(g, "o2")
                        softmax_out(g, h, 1)
                        if h == 3:
                            add_out(g, "o3")
                        pt_out(g, h)
                        if h == 3:
                            add_out(g, "o4")
                            add_out(g, "o5")
                        ao_lo(g, h)
                    add_out(g, "o6")
                    add_out(g, "o7")
                    for b in range(B):
                        add_out(g, f"p{b}")

                def mean_square(q, sig, src, dst, done):
                    dve.wait_ge(S[sig], (q + 1) * HB)
                    dve.tensor_scalar(dst[:, part(q)], src[:, part(q)], 1.0 / D, EPS_RMS1, ALU.mult, ALU.add).then_inc(S[done], 1)

                def x_stats(u, n, x):
                    dve.wait_ge(S[x], u + 1)
                    dve.bn_stats(st1[:, u, :], acc[:, u, :]).then_inc(S[f"bn{n}"], 1)
                    dve.wait_ge(S[f"bn{n}"], u + 1)
                    dve.bn_aggr(mv1[:, u, :], st1[:, u, :]).then_inc(S[f"ag{n}"], 1)

                def variances(q, n):
                    dve.wait_ge(S[f"ag{n}"], (q + 1) * HB)
                    dve.tensor_scalar(ve1[:, part(q)], mv1[:, part(q), 1], EPS_LN, None, ALU.add).then_inc(S[f"ve{n}"], 1)

                def offsets(q, n):
                    dve.wait_ge(S[f"rs{n}"], q + 1)
                    dve.scalar_tensor_tensor(out=nmr[:, part(q)], in0=mv1[:, part(q), 0], scalar=-1.0, in1=rs1[:, part(q)],
                                             op0=ALU.mult, op1=ALU.mult).then_inc(S[f"nr{n}"], 1)

                def split_lo(u, hi, done):
                    dve.wait_ge(S[hi], u + 1)
                    dve.tensor_tensor(tt[:, u % HB, 1, :, :], bank[u][:, :].rearrange("p (c t) -> p c t", c=KC),
                                      tt[:, u % HB, 0, :, :].bitcast(fp32), ALU.subtract).then_inc(S[done], 1)

                def biased(u, sig, row, dst, done):
                    dve.wait_ge(S[sig], u + 1)
                    dve.tensor_tensor(dst, bank[u][:, :], rows[:, row, :], ALU.add).then_inc(S[done], 1)

                def gated(u, sig, scalar, done):
                    dve.wait_ge(S[sig], u + 1)
                    dve.scalar_tensor_tensor(out=acc[:, u, :], in0=bank[u][:, :], scalar=scalar, in1=acc[:, u, :],
                                             op0=ALU.mult, op1=ALU.add).then_inc(S[done], 1)

                def x1(u):
                    dve.wait_ge(s_xl[u // HB], 16)
                    dve.scalar_tensor_tensor(out=acc[:, u, :], in0=acc[:, u, :], scalar=tg[:, 0:1], in1=tmp[:, u, :],
                                             op0=ALU.mult, op1=ALU.add).then_inc(S["x1"], 1)

                def dequant(c):
                    if c:
                        dve.wait_ge(s_wf, c)
                    for h in range(2):
                        ps = slice(h * 64, h * 64 + 64)
                        dve.tensor_scalar(wint[ps, :], qw[ps, :], 4 * (2 * c + h), 15,
                                          ALU.logical_shift_right, ALU.bitwise_and).then_inc(s_prep, 1)
                    dve.wait_ge(s_prep, 9 + 3 * c + 2)
                    if c == 0:
                        dve.wait_ge(S["k_ss"], B)
                    dve.tensor_tensor(stage[:, KC + c, :], wint[:, :], zint[:, :], ALU.subtract).then_inc(s_prep, 1)
                    dve.wait_ge(s_prep, 9 + 3 * c + 3)
                    dve.tensor_tensor(stage[:, KC + c, :], stage[:, KC + c, :], scl[:, :], ALU.mult).then_inc(s_wf, 1)

                for q in range(2):
                    mean_square(q, "k_ss", kss, kms, "k_ms")
                dve.wait_ge(s_rf, 48)
                for s in range(8):
                    dve.tensor_scalar(zint[:, :].rearrange("p (j s) -> p j s", s=8)[:, :, s], zq[:, :], 4 * s, 15,
                                      ALU.logical_shift_right, ALU.bitwise_and).then_inc(s_prep, 1)
                dve.wait_ge(s_prep, 8)
                dve.tensor_scalar(zint[:, :], zint[:, :], 1, None, ALU.add).then_inc(s_prep, 1)
                dve.wait_ge(s_prep, 9)
                dve.wait_ge(s_rest, 80)
                for u in range(B):
                    dve.wait_ge(S["k_rr"], u // HB + 1)
                    dve.scalar_tensor_tensor(out=cs[:, u, :], in0=cs[:, u, :], scalar=krr[:, u:u + 1],
                                             in1=rows[:, R_FN, :], op0=ALU.mult, op1=ALU.mult).then_inc(S["k_fn"], 1)
                for u in HALVES[0]:
                    split_lo(u, "k_hi", "k_lo")
                dequant(0)
                dequant(1)
                split_lo(4, "k_hi", "k_lo")
                split_lo(5, "k_hi", "k_lo")
                dequant(2)
                split_lo(6, "k_hi", "k_lo")
                split_lo(7, "k_hi", "k_lo")
                dequant(3)
                for row, g in ((R_FFN, 2), (R_BASE, 3)):
                    dve.tensor_scalar(rows[:, row, :], rows[:, row, :], tg[:, g:g + 1], None, ALU.mult).then_inc(S["rows"], 1)
                for q in range(2):
                    for u in HALVES[q]:
                        if u == 0:
                            dve.wait_ge(s_dev, (GROUPS + 1) * len(DVE_UNITS))
                        x1(u)
                    for u in HALVES[q]:
                        x_stats(u, 0, "x1")
                    variances(q, 0)
                    for u in HALVES[q]:
                        biased(u, "k_mm", R_BK, qf[:, u, :], "k_b")
                    offsets(q, 0)
                for u in HALVES[0]:
                    split_lo(u, "hi0", "lo0")
                for q in range(2):
                    mean_square(q, "k2_ss", kss, kms, "k2_ms")
                for q in range(2):
                    for u in HALVES[q]:
                        dve.wait_ge(S["k2_rr"], q + 1)
                        dve.tensor_scalar(qf[:, u, :], qf[:, u, :], krr[:, u:u + 1], None, ALU.mult).then_inc(S["k_n"], 1)
                for u in HALVES[1]:
                    split_lo(u, "hi0", "lo0")
                for q in range(2):
                    for u in HALVES[q]:
                        dve.wait_ge(S["rsf"], u + 1)
                        gated(u, "y0", tg[:, 2:3], "x2")
                        x_stats(u, 1, "x2")
                    variances(q, 1)
                    offsets(q, 1)
                for u in HALVES[0]:
                    split_lo(u, "hi1", "lo1")
                for u in HALVES[0]:
                    biased(u, "q_mm", R_BQ, tmp[:, u, :], "q_b")
                for u in HALVES[1]:
                    split_lo(u, "hi1", "lo1")
                mean_square(0, "q_ss", qss, qms, "q_ms")

                def q_n(u):
                    dve.wait_ge(S["q_rr"], u // HB + 1)
                    dve.tensor_scalar(tmp[:, u, :], tmp[:, u, :], qrr[:, u:u + 1], None, ALU.mult).then_inc(S["q_n"], 1)

                def q_outd(u):
                    dve.wait_ge(S["q_T"], u + 1)
                    for c in range(KC):
                        ins = dve.tensor_scalar(qt1[:, u, c, :], bank[u][:, c * P:(c + 1) * P], cols[:, 1, c:c + 1],
                                                None, ALU.mult)
                    ins.then_inc(S["q_outd"], 1)

                for u in HALVES[0]:
                    q_n(u)
                for u in HALVES[1]:
                    biased(u, "q_mm", R_BQ, tmp[:, u, :], "q_b")
                mean_square(1, "q_ss", qss, qms, "q_ms")
                q_outd(1)
                q_outd(3)
                for u in HALVES[1]:
                    q_n(u)
                q_outd(5)
                q_outd(7)
                for q in range(2):
                    for u in HALVES[q]:
                        dve.wait_ge(S["s_mm"], u + 1)
                        dve.tensor_reduce(nm1[:, u:u + 1], bank[u][:, 0:P], AX, ALU.max).then_inc(S["s_max"], 1)
                    dve.wait_ge(S["s_max"], (q + 1) * HB)
                    dve.tensor_scalar(nm1[:, part(q)], nm1[:, part(q)], -float(D) ** -0.5, None, ALU.mult).then_inc(S["s_neg"], 1)
                for q in range(2):
                    dve.wait_ge(S["s_exp"], (q + 1) * HB)
                    dve.reciprocal(ri1[:, part(q)], es1[:, part(q)]).then_inc(S["s_ri"], 1)
                    dve.wait_ge(S["s_ri"], q + 1)
                    dve.tensor_scalar(ri1[:, part(q)], ri1[:, part(q)], tg[:, 1:2], None, ALU.mult).then_inc(S["s_rg"], 1)
                    dve.wait_ge(S["s_rg"], q + 1)
                    for u in HALVES[q]:
                        gated(u, "pv", ri1[:, u:u + 1], "x3")
                        x_stats(u, 2, "x3")
                    variances(q, 2)
                    offsets(q, 2)

                dve.tensor_copy(emap[:, :], emap_i[:, :]).then_inc(s_prep, 1)
                dve.wait_ge(s_prep, 22)
                dve.tensor_tensor(onehot[:, :, :], emap[:, :].unsqueeze(1).to_broadcast([P, NEXP, ROUT]),
                                  consts[:, ROUT * ROUT:].unsqueeze(2).to_broadcast([P, NEXP, ROUT]), ALU.is_equal).then_inc(s_prep, 1)
                dve.wait_ge(s_prep, 23)
                dve.tensor_scalar(onehot[:, :, :], onehot[:, :, :], LORA_SCALE, None, ALU.mult).then_inc(s_prep, 1)
                dve.wait_ge(s_prep, 24)
                tri = consts[:, 0:ROUT * ROUT].rearrange("p (n m) -> p n m", n=ROUT).unsqueeze(1).to_broadcast([P, HB, ROUT, ROUT])

                def router(q):
                    us = part(q)
                    lg, ex, pk, rank = (rt[:, i, us, :] for i in range(4))
                    bc = [P, HB, ROUT]
                    pm = ex.unsqueeze(2).to_broadcast([P, HB, ROUT, ROUT])
                    pn = ex.unsqueeze(3).to_broadcast([P, HB, ROUT, ROUT])
                    n = 10 * q

                    def then(k, ins):
                        ins.then_inc(S["router"], 1)
                        dve.wait_ge(S["router"], n + k)

                    dve.wait_ge(S["ra_out"], (q + 1) * HB)
                    then(1, dve.tensor_tensor(lg, qf[:, us, ER:ER + ROUT], rb[:, :].unsqueeze(1).to_broadcast(bc), ALU.add))
                    then(2, dve.tensor_reduce(nm1[:, us], lg, AX, ALU.max))
                    then(3, dve.tensor_tensor(lg, lg, nm1[:, us].unsqueeze(2).to_broadcast(bc), ALU.subtract))
                    dve.wait_ge(S["lg_exp"], q + 1)
                    then(4, dve.tensor_reduce(es1[:, us], ex, AX, ALU.add))
                    then(5, dve.reciprocal(ri1[:, us], es1[:, us]))
                    then(6, dve.tensor_tensor(ex, ex, ri1[:, us].unsqueeze(2).to_broadcast(bc), ALU.mult))
                    dve.tensor_tensor(cmp[:, 0], pm, pn, ALU.is_gt).then_inc(S["gt"], 1)
                    dve.tensor_tensor(cmp[:, 1], pm, pn, ALU.is_equal).then_inc(S["gt"], 1)
                    dve.wait_ge(S["gt"], 4 * q + 2)
                    dve.tensor_tensor(cmp[:, 1], cmp[:, 1], tri, ALU.mult).then_inc(S["gt"], 1)
                    dve.wait_ge(S["gt"], 4 * q + 3)
                    dve.tensor_tensor(cmp[:, 0], cmp[:, 0], cmp[:, 1], ALU.add).then_inc(S["gt"], 1)
                    dve.wait_ge(S["gt"], 4 * q + 4)
                    then(7, dve.tensor_reduce(rank, cmp[:, 0], AX, ALU.add))
                    then(8, dve.scalar_tensor_tensor(out=pk, in0=rank, scalar=float(NEXP), in1=ex, op0=ALU.is_lt, op1=ALU.mult))
                    then(9, dve.tensor_tensor(wexp[:, :], onehot[:, :, :].unsqueeze(1).to_broadcast([P, HB, NEXP, ROUT]),
                                              pk.unsqueeze(2).to_broadcast([P, HB, NEXP, ROUT]), ALU.mult))
                    then(10, dve.tensor_reduce(wsum[:, us, :], wexp[:, :], AX, ALU.add))
                    for u in HALVES[q]:
                        dve.tensor_tensor(tmp[:, u, 0:ER].rearrange("p (e r) -> p e r", e=NEXP),
                                          qf[:, u, 0:ER].rearrange("p (e r) -> p e r", e=NEXP),
                                          wsum[:, u, :].unsqueeze(2).to_broadcast([P, NEXP, RANK]), ALU.mult).then_inc(S["hw"], 1)

                for u in HALVES[0]:
                    split_lo(u, "hi2", "lo2")
                router(0)
                for u in HALVES[1]:
                    split_lo(u, "hi2", "lo2")
                router(1)
                for u in range(B):
                    dve.wait_ge(S["rsb"], u + 1)
                    gated(u, "o_mm2", tg[:, 3:4], "x4")

            @block.tensor
            def _(pe):
                pe.sem_inc(s_unit, NUNIT)
                pe.wait_ge(s_const, 48)
                for b in range(B):
                    if b % 2 == 0:
                        pe.wait_ge(s_cin[b // 2], 16)
                    for c in range(KC):
                        mm = pe.transpose(bank[b][:, c * P:(c + 1) * P], craw[:, b, c * P:(c + 1) * P], ident[:, :])
                    mm.then_inc(s_cT, 1)
                pe.wait_ge(s_clo, B)

                def x_transposed(b):
                    pe.wait_ge(s_xr, b + 1)
                    if b >= 4:
                        pe.wait_ge(s_xlo, (b - 3) * KC)
                    for c in range(KC):
                        mm = pe.transpose(bank[4 + b % 4][:, c * P:(c + 1) * P], xraw[:, b, c * P:(c + 1) * P], ident[:, :])
                    mm.then_inc(s_xT, 1)

                def bank_free(g, u):
                    i = un[u]
                    before = UNITS[i - RING]
                    if before in dx:
                        n = dx[before] + 1 + (len(DVE_UNITS) if i >= RING else 0)
                        pe.wait_ge(s_dev, g * len(DVE_UNITS) + n)
                    else:
                        pe.wait_ge(s_aev, g * len(ACT_UNITS) + ax[before] + 1)

                def weights(g, c):
                    pe.wait_ge(s_wlo, g * NCH + ix[c] + 1)

                def proj(g, kind, h, s):
                    u = f"{kind}{h}{'ab'[s]}"
                    w, t = (wq, xt) if kind == "q" else (wk, ct)
                    if s == 0:
                        weights(g, f"{kind}{h}")
                    bank_free(g, u)
                    for c in range(KC):
                        for i, j in PASSES:
                            mm = pe.matmul(bank[un[u] % RING][:, :], w[:, i, c, :], t[:, j, c, half(s)],
                                           start=(c == 0 and i + j == 0), stop=(c == KC - 1 and i == 1))
                    mm.then_inc(s_unit, 1)

                def value(g, b):
                    u = f"v{b}"
                    if b == 0:
                        weights(g, "v3")
                    bank_free(g, u)
                    for c in range(KC):
                        for i, j in PASSES:
                            mm = pe.matmul(bank[un[u] % RING][:, :], ct[:, i, c, b * P:(b + 1) * P], wvo[:, j, c, :],
                                           start=(c == 0 and i + j == 0), stop=(c == KC - 1 and i == 1))
                    mm.then_inc(s_unit, 1)

                def scores(g, h):
                    pe.wait_ge(s_aev, g * len(ACT_UNITS) + ax[f"q{h}b"] + 1)
                    for s in range(2):
                        pe.wait_ge(s_sadd, g * 2 * GH + 2 * h + s + 1)
                        for b in range(4 * s, 4 * s + 4):
                            mm = pe.matmul(bank[4 + s][:, (b - 4 * s) * P:(b - 4 * s + 1) * P],
                                           qt[:, b * P:(b + 1) * P], kt[:, b * P:(b + 1) * P], start=True, stop=True)
                        mm.then_inc(s_s, 1)

                def transposes(g, h):
                    n = g * 2 * GH + 2 * h
                    for s in range(2):
                        pe.wait_ge(s_p, n + s + 1)
                        pe.wait_ge(s_aolo, n + s + 1)
                        for b in range(4 * s, 4 * s + 4):
                            mm = pe.transpose(bank[6 + s][:, (b - 4 * s) * P:(b - 4 * s + 1) * P], prob[:, b, :], ident[:, :])
                        mm.then_inc(s_pt, 1)

                def attend(g, h):
                    if h == 0:
                        pe.wait_ge(s_aev, g * len(ACT_UNITS) + ax[f"v{B - 1}"] + 1)
                    for s in range(2):
                        pe.wait_ge(s_pte, g * 2 * GH + 2 * h + s + 1)
                        for b in range(4 * s, 4 * s + 4):
                            mm = pe.matmul(bank[6 + s][:, (b - 4 * s) * P:(b - 4 * s + 1) * P],
                                           vals[:, b, h * P:(h + 1) * P], pt[:, b, :], start=True, stop=True)
                        mm.then_inc(s_pv, 1)

                def project(g, u, heads):
                    b = int(u[1])
                    if u == "o0":
                        weights(g, "o3")
                    pe.wait_ge(s_aolo, g * 2 * GH + 2 * max(heads) + b // 4 + 3)
                    bank_free(g, u)
                    for h in heads:
                        for i, j in PASSES:
                            mm = pe.matmul(bank[un[u] % RING][:, :], ao[:, h, i, b * P:(b + 1) * P], wvo[:, j, h, :],
                                           start=(h == heads[0] and i + j == 0), stop=(h == heads[-1] and i == 1))
                    mm.then_inc(s_unit, 1)

                def group(g, first):
                    proj(g, "k", 0, 0)
                    proj(g, "k", 0, 1)
                    for b in range(B):
                        if first and b >= B - 2:
                            for x in range(4):
                                x_transposed(4 * (b - B + 2) + x)
                        value(g, b)
                    for s in range(2):
                        if first:
                            pe.wait_ge(s_xlo, (s + 1) * 4 * KC)
                        proj(g, "q", 0, s)
                    scores(g, 0)
                    for h in range(1, GH):
                        proj(g, "k", h, 0)
                        proj(g, "k", h, 1)
                        proj(g, "q", h, 0)
                        transposes(g, h - 1)
                        proj(g, "q", h, 1)
                        attend(g, h - 1)
                        scores(g, h)
                    for b in range(4):
                        project(g, f"o{b}", [0, 1, 2])
                    transposes(g, GH - 1)
                    for b in (4, 5):
                        project(g, f"o{b}", [0, 1, 2])
                    attend(g, GH - 1)
                    for b in (6, 7):
                        project(g, f"o{b}", [0, 1, 2])
                    for b in range(B):
                        project(g, f"p{b}", [GH - 1])

                group(0, True)
                with pe.Fori(1, GROUPS) as g:
                    group(g, False)

                def transpose(us, waits, src, done, n=KC, to=lambda u: u):
                    for u in us:
                        for w in waits:
                            pe.wait_ge(S[w], u + 1)
                        for c in range(n):
                            mm = pe.transpose(bank[to(u)][:, c * P:(c + 1) * P], src[:, u, c * P:(c + 1) * P], ident[:, :])
                        mm.then_inc(S[done], 1)

                def product(u, lo, w, n, done, to, last=True):
                    pe.wait_ge(S[lo], u + 1)
                    for c in range(KC):
                        for i, j in PASSES:
                            mm = pe.matmul(bank[to][:, 0:n], tt[:, u % HB, i, c, :], w[:, j, c, :],
                                           start=(c == 0 and i + j == 0), stop=(c == KC - 1 and i == 1 and last))
                    mm.then_inc(S[done], 1)

                pe.wait_ge(s_dev, (GROUPS + 1) * len(DVE_UNITS))
                for q in range(2):
                    transpose(HALVES[q], ["k_fn"], cs, "k_T")
                    if q == 0:
                        pe.wait_ge(s_wl, W_KEY + KC)
                    for u in HALVES[q]:
                        product(u, "k_lo", wt_a, D, "k_mm", u)
                for q in range(2):
                    transpose(HALVES[q], ["xn0", "k_b"], tmp, "T0")
                    if q == 0:
                        pe.wait_ge(s_wl, W_FFN + KC)
                    for u in HALVES[q]:
                        product(u, "lo0", wt_f, D, "y0", u)
                transpose(range(B), ["k_n", "x2"], qf, "k_T2")
                for q in range(2):
                    transpose(HALVES[q], ["xn1", "k_out"], tmp, "T1")
                    if q == 0:
                        pe.wait_ge(s_wl, W_QRY + KC)
                    for u in HALVES[q]:
                        product(u, "lo1", wt_q, D, "q_mm", u)
                for q in range(2):
                    transpose(HALVES[q], ["q_n"], tmp, "q_T")
                    for u in HALVES[q]:
                        pe.wait_ge(S["q_outd" if u % 2 else "q_outa"], u // 2 + 1)
                        for c in range(KC):
                            mm = pe.matmul(bank[u][:, 0:P], qt1[:, u, c, :], kt1[:, u, c, :], start=(c == 0), stop=(c == KC - 1))
                        mm.then_inc(S["s_mm"], 1)
                for q in range(2):
                    transpose(HALVES[q], ["s_exp"], pr1, "p_T", n=1)
                    for u in HALVES[q]:
                        pe.wait_ge(S["p_out"], u + 1)
                        pe.matmul(bank[u][:, :], pt1[:, u, :], cs[:, u, :], start=True, stop=True).then_inc(S["pv"], 1)
                transpose(HALVES[0], ["xn2"], tmp, "T2")
                pe.wait_ge(s_wl, W_RA + KC)
                for u in HALVES[0]:
                    pe.wait_ge(S["x3"], HB + u + 1)
                    product(u, "lo2", wra, RAW, "ra", HB + u)
                    product(u, "lo2", wt_a, D, "o_mm", u, last=False)
                pe.wait_ge(S["ra_out"], HB)
                transpose(HALVES[1], ["xn2"], tmp, "T2")
                for u in HALVES[1]:
                    product(u, "lo2", wra, RAW, "ra", u)
                pe.wait_ge(S["ra_out"], B)

                def experts(u):
                    pe.wait_ge(S["hw_out"], u + 1)
                    pe.matmul(bank[u][:, :], pt1[:, u, :], wbm[:, :], start=False, stop=True).then_inc(S["o_mm2"], 1)

                transpose(HALVES[0], ["hw"], tmp, "hw_T", n=1, to=lambda u: HB + u)
                for u in HALVES[0]:
                    experts(u)
                for u in HALVES[1]:
                    pe.wait_ge(S["hw_out"], u - HB + 1)
                    product(u, "lo2", wt_a, D, "o_mm", u, last=False)
                pe.wait_ge(S["x4"], HB)
                transpose(HALVES[1], ["hw"], tmp, "hw_T", n=1, to=lambda u: u - HB)
                for u in HALVES[1]:
                    experts(u)


def kernel(**inputs):
    import concourse.bacc as _bacc
    from concourse.bass_utils import run_bass_kernel_spmd as _run

    x = {k: np.asarray(v) for k, v in inputs.items()}
    lay = {}

    def head_major(w):
        return w.reshape(HEADS, P, KC, P).transpose(0, 3, 2, 1).reshape(HEADS, P, D)

    wq, wk = head_major(x["L0_xattn_w_q"]), head_major(x["L0_xattn_w_k"])
    wv = x["L0_xattn_w_v"].reshape(GROUPS, GH * P, KC, P).transpose(0, 2, 3, 1)
    wo = x["L0_xattn_w_out"].reshape(D, GROUPS, GH, P).transpose(1, 2, 3, 0)
    src = {"q": wq.reshape(GROUPS, GH, P, D), "k": wk.reshape(GROUPS, GH, P, D), "v": wv, "o": wo}
    w0 = np.stack([src[c[0]][:, int(c[1])] for c in CHUNKS], axis=1)
    lay["w0"] = w0.reshape(GROUPS * NCH // 2, 2, P, D).transpose(0, 2, 1, 3)
    lay["bias"] = x["L0_xattn_position_bias"].reshape(GROUPS, GH, P, P).transpose(0, 2, 1, 3)
    lay["x"] = x["x"].transpose(1, 0, 2)
    lay["ctx"] = x["ctx_4096"].transpose(1, 0, 2)
    lay["mask"] = x["mask_BxSxS2_bk0"].transpose(1, 0, 2)
    lay["gates"] = np.concatenate([x["g_xattn"], x["g_ffn"]])
    lay["cols"] = np.stack([x[k].reshape(KC, P).T for k in
                            ("L0_xattn_ln_weight", "L1_xattn_qn_w", "L1_xattn_kn_w")], axis=1)
    lay["ident"] = np.eye(P, dtype=np.float32)
    inner = lambda w: w.reshape(w.shape[0], KC, P).transpose(2, 1, 0)
    lay["w_key"] = inner(x["L1_xattn_Wk_w"])
    lay["w_qry"] = inner(x["L1_xattn_Wq_w"])
    lay["w_base"] = inner(x["L1_ffn_base_W"])
    lay["w_ra"] = inner(np.concatenate([x["L1_ffn_A"].reshape(ER, D), x["L1_ffn_router_W"],
                                        np.zeros((RAW - ER - ROUT, D), np.float32)]))
    lay["w_bm"] = x["L1_ffn_B"].transpose(0, 2, 1).reshape(ER, D)
    lay["rows"] = np.stack([x[k] for k in ("L0_ffn_bias", "L1_xattn_fn_w", "L1_xattn_Wq_b",
                                           "L1_xattn_Wk_b", "L1_ffn_base_b")])
    lay["rb"] = x["L1_ffn_router_b"]
    lay["emap"] = x["L1_ffn_expert_map"]
    lay["consts"] = np.concatenate([np.tril(np.ones((ROUT, ROUT), np.float32), -1).ravel(),
                                    np.arange(NEXP, dtype=np.float32)])
    lay["qw"] = np.tile(x["L0_ffn_qweight"], (2, 1))
    rep = P // 2 // KC
    lay["zq"] = np.tile(np.repeat(x["L0_ffn_qzeros"], rep, axis=0), (2, 1))
    lay["scl"] = np.tile(np.repeat(x["L0_ffn_scales"], rep, axis=0), (2, 1))

    nc = _bacc.Bacc("TRN2", target_bir_lowering=False, num_devices=1)
    arrays, aps = {}, {}
    for k, v in lay.items():
        v = np.ascontiguousarray(v)
        arrays[f"in_{k}"] = v
        dt = mybir.dt.uint8 if v.dtype == bool else mybir.dt.from_np(v.dtype)
        aps[k] = nc.dram_tensor(f"in_{k}", v.shape, dt, kind="ExternalInput").ap()
    out = nc.dram_tensor("out_0", (B, P, D), mybir.dt.float32, kind="ExternalOutput").ap()
    build(nc, aps, out)
    r = _run(nc, [arrays], core_ids=[0])
    return r.results[0]["out_0"]
```

```python
from contextlib import ExitStack

import concourse.bass as bass
from concourse import mybir
import numpy as np

P = 128
B = 8
D = 512
KC = D // P
TOK = B * P
HEADS = 32
GH = 4
GROUPS = HEADS // GH
NEXP = 8
RANK = 16
ER = NEXP * RANK
ROUT = 2 * NEXP - 1
RAW = 256
LORA_SCALE = 2.0
EPS_LN = 1e-5
EPS_RMS0 = 1e-5
EPS_RMS1 = 1e-6
MASKED = -1e30

CHUNKS = ["k0", "v0", "v1", "v2", "v3", "q0", "k1", "q1", "o0", "o1", "o2", "o3", "k2", "q2", "k3", "q3"]
NCH = len(CHUNKS)
SLOTS = 8
UNITS = (["k0a", "k0b"] + [f"v{b}" for b in range(B)] + ["q0a", "q0b"]
         + [f"{t}{h}{s}" for h in range(1, GH) for t in "kq" for s in "ab"]
         + [f"o{b}" for b in range(B)] + [f"p{b}" for b in range(B)])
NUNIT = len(UNITS)
RING = 4
ACT_UNITS = [u for u in UNITS if u[0] in "qkv"]
DVE_UNITS = [u for u in UNITS if u[0] in "op"]
PASSES = ((0, 0), (0, 1), (1, 0))


def build(nc, a, out):
    fp32, fp32r, i32, u8 = mybir.dt.float32, mybir.dt.float32r, mybir.dt.int32, mybir.dt.uint8
    ALU, ACT, AX = mybir.AluOpType, mybir.ActivationFunctionType, mybir.AxisListType.X

    cursor = [-(-nc.sbuf_base // 64) * 64]

    def place(name, shape, dt):
        size = int(np.prod(shape[1:])) * (1 if dt == u8 else 4)
        t = nc.alloc_sbuf_tensor_at(name, shape, dt, offset=cursor[0])
        cursor[0] += -(-size // 64) * 64
        assert cursor[0] <= nc.sbuf_usable_end, (name, cursor[0])
        return t

    acc = place("acc", [P, B, D], fp32)
    stage = place("stage", [P, SLOTS, D], fp32)
    ident = place("ident", [P, P], fp32)
    gates = place("gates", [P, 4], fp32)
    tg = place("tg", [P, 4], fp32)
    cols = place("cols", [P, 3, KC], fp32)
    mhalf = place("mhalf", [P, B], fp32)
    kss, kms, krr = (place(n, [P, B], fp32) for n in ("kss", "kms", "krr"))
    small0 = cursor[0]

    xt = place("xt", [P, 2, KC, TOK], fp32r)
    ct = place("ct", [P, 2, KC, TOK], fp32r)
    after_xc = cursor[0]
    wq = place("wq", [P, 2, KC, P], fp32r)
    wk = place("wk", [P, 2, KC, P], fp32r)
    after_qk = cursor[0]
    wvo = place("wvo", [P, 2, KC, D], fp32r)
    bias = place("bias", [P, GH, P], fp32)
    maskneg = place("maskneg", [P, B, P], fp32)
    bm = place("bm", [P, 2, B, P], fp32)
    qt = place("qt", [P, TOK], fp32)
    kt = place("kt", [P, TOK], fp32)
    vals = place("vals", [P, B, D], fp32)
    prob = place("prob", [P, B, P], fp32)
    pt_at = cursor[0]
    pt = place("pt", [P, B, P], fp32)
    ao_at = cursor[0]
    ao = place("ao", [P, GH, 2, TOK], fp32r)
    anykey = place("anykey", [P, B], fp32)
    nmax = place("nmax", [P, B], fp32)
    esum = place("esum", [P, B], fp32)
    rinv = place("rinv", [P, B], fp32)
    stats = place("stats", [P, B, 6], fp32)
    mv = place("mv", [P, B, 2], fp32)
    vsum = place("vsum", [P, B], fp32)
    rstd = place("rstd", [P, B], fp32)
    rscale = place("rscale", [P, B], fp32)
    msq = place("msq", [P, B], fp32)
    rrms = place("rrms", [P, B], fp32)
    cursor[0] = ao_at
    craw = place("craw", [P, B, D], fp32)
    xraw = place("xraw", [P, B, D], fp32)
    masku = nc.alloc_sbuf_tensor_at("masku", [P, B, P], u8, offset=pt_at)
    maskf = prob

    cursor[0] = small0
    cs = place("cs", [P, B, D], fp32)
    wt_a = place("wt_a", [P, 2, KC, D], fp32r)
    wt_f = place("wt_f", [P, 2, KC, D], fp32r)
    kt1_at = cursor[0]
    kt1 = place("kt1", [P, B, KC, P], fp32)
    assert cursor[0] == after_xc
    cursor[0] = kt1_at
    qw = place("qw", [P, D], i32)
    zq = place("zq", [P, D // 8], i32)
    zint = place("zint", [P, D], i32)
    wint = place("wint", [P, D], i32)
    scl = place("scl", [P, D], fp32)
    cursor[0] = after_xc
    fnw = place("fnw", [P, D], fp32)
    bkr = place("bkr", [P, D], fp32)
    wbm = place("wbm", [P, D], fp32)
    rb = place("rb", [P, ROUT], fp32)
    emap_i = place("emap_i", [P, ROUT], i32)
    consts = place("consts", [P, ROUT * ROUT + NEXP], fp32)
    assert cursor[0] <= after_qk
    cursor[0] = after_qk
    wt_q = place("wt_q", [P, 2, KC, D], fp32r)
    tmp = place("tmp", [P, B, D], fp32)
    HB = B // 2
    tt = place("tt", [P, HB, 2, KC, P], fp32r)
    qt1 = place("qt1", [P, B, KC, P], fp32)
    qf = qt1[:, :, :, :].rearrange("p u c t -> p u (c t)")
    wra = place("wra", [P, 2, KC, RAW], fp32r)
    rows = place("rows", [P, 3, D], fp32)
    R_FFN, R_BQ, R_BASE = range(3)
    emap = place("emap", [P, ROUT], fp32)
    onehot = place("onehot", [P, NEXP, ROUT], fp32)
    pr1 = place("pr1", [P, B, P], fp32)
    pt1 = place("pt1", [P, B, P], fp32)
    cmp = place("cmp", [P, 2, HB, ROUT, ROUT], fp32)
    wexp = place("wexp", [P, HB, NEXP, ROUT], fp32)
    wsum = place("wsum", [P, B, NEXP], fp32)
    rt = place("rt", [P, 4, B, ROUT], fp32)
    st1 = place("st1", [P, B, 6], fp32)
    mv1 = place("mv1", [P, B, 2], fp32)
    k2ss, k2ms, k2rr, ve1, rs1, nmr, qss, qms, qrr, qsc, nm1, es1, ri1 = (
        place(n, [P, B], fp32) for n in ("k2ss", "k2ms", "k2rr", "ve1", "rs1", "nmr", "qss", "qms", "qrr", "qsc", "nm1", "es1", "ri1"))

    ctx = ExitStack()
    with ctx:
        bank = [ctx.enter_context(nc.psum_tensor(f"bank{i}", [P, D], fp32)) for i in range(8)]

        def sem(name):
            return ctx.enter_context(nc.semaphore(name))

        s_const = sem("const_in")
        s_cin = [sem(f"ctx_in{q}") for q in range(4)]
        s_xin = [sem(f"x_in{q}") for q in range(2)]
        s_min = sem("mask_in")
        s_bias = sem("bias_in")
        s_stage = [sem(f"stage_in{i}") for i in range(SLOTS // 2)]
        s_d = sem("dve_prep")
        s_a = sem("act_prep")
        s_g = sem("pool_prep")
        s_cT = sem("ctx_transposed")
        s_xT = sem("x_transposed")
        s_css = sem("ctx_squares")
        s_chi = sem("ctx_hi")
        s_clo = sem("ctx_lo")
        s_xhi = sem("x_hi")
        s_xlo = sem("x_lo")
        s_mneg = sem("maskneg_done")
        s_h = sem("layernorm_x")
        s_xr = sem("rmsnorm_x")
        s_mf = sem("mask_steps")
        s_whi = sem("weights_hi")
        s_wlo = sem("weights_lo")
        s_bm = sem("biasmask_done")
        s_unit = sem("unit_done")
        s_aev = sem("act_emptied")
        s_dev = sem("dve_emptied")
        s_s = sem("scores_done")
        s_sadd = sem("scores_read")
        s_smax = sem("scores_max")
        s_nmax = sem("negmax_done")
        s_exp = sem("exp_done")
        s_rinv = sem("rinv_steps")
        s_p = sem("probs_scaled")
        s_pt = sem("pt_done")
        s_pte = sem("pt_emptied")
        s_pv = sem("pv_done")
        s_aohi = sem("ao_hi")
        s_aolo = sem("ao_lo")
        s_out = sem("stored")

        ahead = SLOTS // 2
        npairs = GROUPS * NCH // 2
        ix = {c: i for i, c in enumerate(CHUNKS)}
        un = {u: i for i, u in enumerate(UNITS)}
        ax = {u: i for i, u in enumerate(ACT_UNITS)}
        dx = {u: i for i, u in enumerate(DVE_UNITS)}
        half = lambda s: slice(s * 512, s * 512 + 512)

        names = ["k_sc", "k_fn", "k_T", "k_hi", "k_lo", "k_mm", "k_b", "k2_ss", "k2_ms", "k2_rr",
                 "k_n", "k_T2", "k_out", "x1", "y0", "x2", "q_mm", "q_b", "q_ss", "q_ms", "q_rr", "s_scale", "q_T",
                 "q_outa", "q_outd", "s_mm", "s_max", "s_neg", "s_exp", "s_ri", "s_rg", "p_T", "p_out", "pv", "x3",
                 "ra", "ra_out", "lg_exp", "router", "hw", "hw_T", "hw_out", "o_mm", "x4", "rows", "rsf", "rsb", "gt", "o_mm2"]
        names += [f"{n}{i}" for i in range(3) for n in ("bn", "ag", "ve", "rs", "nr", "xn", "T", "hi", "lo")]
        S = {n: sem(f"t_{n}") for n in names}
        s_cl = [sem(f"t_ctx_in{q}") for q in range(4)]
        s_xl = [sem(f"t_x_in{q}") for q in range(2)]
        s_rk, s_rf, s_rq, s_rbase, s_rra, s_rest = (sem(f"t_raw_{n}") for n in ("key", "ffn", "query", "base", "ra", "rest"))
        s_fnw = sem("t_fnw_in")
        s_early = sem("t_early_in")
        s_wh = sem("t_weights_hi")
        s_wl = sem("t_weights_lo")
        s_wf = sem("t_ffn_weights")
        W_KEY, W_FFN, W_QRY, W_BASE, W_RA = (KC * n for n in range(5))
        s_prep = sem("t_dve_prep")
        last_proj = GROUPS * NUNIT + un[f"q{GH - 1}b"] + 1
        last_unit = (GROUPS + 1) * NUNIT
        HALVES = [range(0, HB), range(HB, B)]
        part = lambda q: slice(q * HB, q * HB + HB)
        def wchunk(n, c):
            if n == W_RA:
                raw = stage[:, 0:2, :].rearrange("p a (b n) -> p (a b) n", b=2)[:, c, :]
                return raw, wra[:, 0, c, :], wra[:, 1, c, :]
            slot = {W_KEY: 0, W_FFN: KC, W_QRY: 0, W_BASE: KC}[n]
            w = {W_KEY: wt_a, W_FFN: wt_f, W_QRY: wt_q, W_BASE: wt_a}[n]
            return stage[:, slot + c, :], w[:, 0, c, :], w[:, 1, c, :]

        with nc.Block() as block:

            @block.sync
            def _(sp):
                for q in range(4):
                    sp.dma_start(craw[:, 2 * q:2 * q + 2, :], a["ctx"][:, 2 * q:2 * q + 2, :]).then_inc(s_cin[q], 16)

                def load(pair, slot):
                    sp.dma_start(stage[:, 2 * slot:2 * slot + 2, :], a["w0"][pair, :, :, :]).then_inc(s_stage[slot], 16)

                for j in range(ahead):
                    load(j, j)
                    if j == 2:
                        for q in range(2):
                            sp.dma_start(xraw[:, 4 * q:4 * q + 4, :], a["x"][:, 4 * q:4 * q + 4, :]).then_inc(s_xin[q], 16)
                sp.dma_start(masku[:, :, :], a["mask"]).then_inc(s_min, 16)
                sp.dma_start(bias[:, :, :], a["bias"][0, :, :, :]).then_inc(s_bias, 16)
                with sp.Fori(0, GROUPS - 1) as g:
                    for j in range(NCH // 2):
                        sp.wait_ge(s_wlo, g * NCH + 2 * j + 2)
                        load(g * (NCH // 2) + (j + ahead), j % ahead)
                    sp.wait_ge(s_bm, g * GH + GH)
                    sp.dma_start(bias[:, :, :], a["bias"][g + 1, :, :, :]).then_inc(s_bias, 16)
                for j in range(NCH // 2 - ahead):
                    sp.wait_ge(s_wlo, (GROUPS - 1) * NCH + 2 * j + 2)
                    load((GROUPS - 1) * (NCH // 2) + j + ahead, j % ahead)

                sp.wait_ge(s_unit, last_proj)
                for q in range(4):
                    sp.dma_start(cs[:, 2 * q:2 * q + 2, :], a["ctx"][:, 2 * q:2 * q + 2, :]).then_inc(s_cl[q], 16)
                    if q == 0:
                        sp.dma_start(fnw[:, :], a["fnw"].partition_broadcast(P)).then_inc(s_fnw, 16)
                    if q == 1:
                        sp.wait_ge(s_wlo, GROUPS * NCH)
                        sp.dma_start(stage[:, 0:KC, :], a["w_key"]).then_inc(s_rk, 16)
                sp.dma_start(qw[:, :], a["qw"]).then_inc(s_rf, 16)
                sp.dma_start(zq[:, :], a["zq"]).then_inc(s_rf, 16)
                sp.dma_start(scl[:, :], a["scl"]).then_inc(s_rf, 16)
                sp.dma_start(bkr[:, :], a["bk"].partition_broadcast(P)).then_inc(s_early, 16)
                sp.dma_start(rb[:, :], a["rb"].partition_broadcast(P)).then_inc(s_early, 16)
                sp.dma_start(emap_i[:, :], a["emap"].partition_broadcast(P)).then_inc(s_early, 16)
                sp.dma_start(consts[:, :], a["consts"].partition_broadcast(P)).then_inc(s_early, 16)
                sp.dma_start(wbm[:, :], a["w_bm"]).then_inc(s_early, 16)
                sp.wait_ge(s_unit, last_unit)
                sp.dma_start(rows[:, :, :], a["rows"].partition_broadcast(P)).then_inc(s_rest, 16)
                for q in range(2):
                    sp.dma_start(tmp[:, part(q), :], a["x"][:, part(q), :]).then_inc(s_xl[q], 16)
                sp.wait_ge(s_wl, W_KEY + KC)
                sp.dma_start(stage[:, 0:KC, :], a["w_qry"]).then_inc(s_rq, 16)
                sp.wait_ge(s_wl, W_FFN + KC)
                sp.dma_start(stage[:, KC:2 * KC, :], a["w_base"]).then_inc(s_rbase, 16)
                sp.wait_ge(s_wl, W_QRY + KC)
                sp.dma_start(stage[:, 0:2, :].rearrange("p a (b n) -> p (a b) n", b=2), a["w_ra"]).then_inc(s_rra, 16)
                for u in range(B):
                    sp.wait_ge(S["x4"], u + 1)
                    sp.dma_start(out[u, :, :], acc[:, u, :]).then_inc(s_out, 16)
                sp.wait_ge(s_out, 16 * B)

            @block.gpsimd
            def _(pool):
                pool.memset(mhalf[:, :], -0.5).then_inc(s_g, 1)
                pool.wait_ge(s_g, 1)
                def w_lo(g, c):
                    i = ix[c]
                    kind, h = c[0], int(c[1])
                    src = stage[:, i % SLOTS, :]
                    if kind in "qk":
                        w = wq if kind == "q" else wk
                        hi, lo = (w[:, s, :, :].rearrange("p c d -> p (c d)") for s in (0, 1))
                    else:
                        hi, lo = wvo[:, 0, h, :], wvo[:, 1, h, :]
                    pool.wait_ge(s_whi, g * NCH + i + 1)
                    pool.tensor_tensor(lo, src, hi.bitcast(fp32), ALU.subtract).then_inc(s_wlo, 1)

                def biasmask(g, h):
                    if h == 0:
                        pool.wait_ge(s_bias, g * 16 + 16)
                    pool.wait_ge(s_sadd, g * 2 * GH + 2 * h + 1)
                    pool.tensor_tensor(bm[:, h % 2, :, :], maskneg[:, :, :],
                                       bias[:, h:h + 1, :].to_broadcast([P, B, P]), ALU.add).then_inc(s_bm, 1)

                def rest(g):
                    w_lo(g, "q0")
                    biasmask(g, 0)
                    for c in ("k1", "q1", "o0", "o1", "o2", "o3"):
                        w_lo(g, c)
                    biasmask(g, 1)
                    w_lo(g, "k2")
                    w_lo(g, "q2")
                    biasmask(g, 2)
                    w_lo(g, "k3")
                    w_lo(g, "q3")
                    biasmask(g, 3)

                first = ("k0", "v0", "v1", "v2", "v3")
                for c in first:
                    w_lo(0, c)
                pool.wait_ge(s_d, 2 * B + 1)
                pool.tensor_tensor(rstd[:, :], vsum[:, :], mhalf[:, :], ALU.pow).then_inc(s_g, 1)
                pool.wait_ge(s_d, 2 * B + 3)
                pool.tensor_tensor(rrms[:, :], msq[:, :], mhalf[:, :], ALU.pow).then_inc(s_g, 1)
                pool.wait_ge(s_css, B)
                pool.tensor_scalar(kms[:, :], kss[:, :], 1.0 / D, EPS_RMS1, ALU.mult, ALU.add).then_inc(s_g, 1)
                pool.wait_ge(s_g, 4)
                pool.tensor_tensor(krr[:, :], kms[:, :], mhalf[:, :], ALU.pow).then_inc(s_g, 1)
                pool.wait_ge(s_mneg, 1)
                rest(0)
                with pool.Fori(1, GROUPS) as g:
                    for c in first:
                        w_lo(g, c)
                    rest(g)

                def w_split_lo(n):
                    for c in range(KC):
                        raw, hi, lo = wchunk(n, c)
                        pool.wait_ge(s_wh, n + c + 1)
                        pool.tensor_tensor(lo, raw, hi.bitcast(fp32), ALU.subtract).then_inc(s_wl, 1)

                def add_row(q, row, xn, done):
                    pool.wait_ge(S["rows"], 2)
                    for u in HALVES[q]:
                        pool.wait_ge(S[xn], u + 1)
                        pool.tensor_tensor(acc[:, u, :], acc[:, u, :], rows[:, row, :], ALU.add).then_inc(S[done], 1)

                def half_root(q, sig, dst, src, done):
                    pool.wait_ge(S[sig], q + 1)
                    pool.tensor_tensor(dst[:, part(q)], src[:, part(q)], mhalf[:, 0:HB], ALU.pow).then_inc(S[done], 1)

                pool.wait_ge(s_fnw, 16)
                w_split_lo(W_KEY)
                for u in range(B):
                    pool.wait_ge(S["k_sc"], u + 1)
                    pool.tensor_tensor(cs[:, u, :], cs[:, u, :], fnw[:, :], ALU.mult).then_inc(S["k_fn"], 1)
                half_root(0, "ve0", rs1, ve1, "rs0")
                w_split_lo(W_FFN)
                half_root(1, "ve0", rs1, ve1, "rs0")
                half_root(0, "k2_ms", k2rr, k2ms, "k2_rr")
                add_row(0, R_FFN, "xn0", "rsf")
                half_root(1, "k2_ms", k2rr, k2ms, "k2_rr")
                half_root(0, "ve1", rs1, ve1, "rs1")
                add_row(1, R_FFN, "xn0", "rsf")
                w_split_lo(W_QRY)
                half_root(1, "ve1", rs1, ve1, "rs1")
                w_split_lo(W_BASE)
                half_root(0, "q_ms", qrr, qms, "q_rr")
                w_split_lo(W_RA)
                half_root(1, "q_ms", qrr, qms, "q_rr")
                for u in range(B):
                    pool.wait_ge(S["ve2"], u + 1)
                    pool.tensor_tensor(rs1[:, u:u + 1], ve1[:, u:u + 1], mhalf[:, 0:1], ALU.pow).then_inc(S["rs2"], 1)
                for q in range(2):
                    add_row(q, R_BASE, "xn2", "rsb")

            @block.scalar
            def _(act):
                act.dma_start(ident[:, :], a["ident"]).then_inc(s_const, 16)
                act.dma_start(gates[:, :], a["gates"].partition_broadcast(P)).then_inc(s_const, 16)
                act.dma_start(cols[:, :, :], a["cols"]).then_inc(s_const, 16)
                act.wait_ge(s_const, 48)
                act.activation(tg[:, :], gates[:, :], ACT.Tanh).then_inc(s_a, 1)
                for b in range(B):
                    act.wait_ge(s_cT, b + 1)
                    act.activation(ct[:, 0, :, b * P:(b + 1) * P], bank[b][:, :].rearrange("p (c t) -> p c t", c=KC),
                                   ACT.Copy).then_inc(s_chi, 1)
                for b in range(B):
                    if b >= 2:
                        act.wait_ge(s_css, b - 1)
                    act.activation(kt[:, half(b % 2)], craw[:, b, :], ACT.Square,
                                   accum_out=kss[:, b:b + 1]).then_inc(s_css, 1)
                def w_hi(g, c):
                    i = ix[c]
                    kind, h = c[0], int(c[1])
                    act.wait_ge(s_stage[i // 2 % ahead], g * 32 + 16 * (i // 2 // ahead) + 16)
                    if kind in "qk":
                        last = un[f"{kind}{h - 1}b"] + NUNIT if h else un[f"{kind}{GH - 1}b"]
                        hi = (wq if kind == "q" else wk)[:, 0, :, :].rearrange("p c d -> p (c d)")
                    else:
                        last = un[f"v{B - 1}"] + NUNIT if kind == "o" else un[f"{'p' if h == GH - 1 else 'o'}{B - 1}"]
                        hi = wvo[:, 0, h, :]
                    act.wait_ge(s_unit, g * NUNIT + last + 1)
                    act.activation(hi, stage[:, i % SLOTS, :], ACT.Copy).then_inc(s_whi, 1)

                def empty(g, u):
                    i = un[u]
                    act.wait_ge(s_unit, g * NUNIT + NUNIT + i + 1)
                    if u[0] == "v":
                        dst = vals[:, int(u[1]), :]
                    else:
                        dst = (qt if u[0] == "q" else kt)[:, half("ab".index(u[2]))]
                    act.activation(dst, bank[i % RING][:, :], ACT.Copy).then_inc(s_aev, 1)

                def exps(g, h):
                    for s in range(2):
                        act.wait_ge(s_nmax, g * 2 * GH + 2 * h + s + 1)
                        for b in range(4 * s, 4 * s + 4):
                            act.activation(prob[:, b, :], prob[:, b, :], ACT.Exp, bias=nmax[:, b:b + 1],
                                           accum_out=esum[:, b:b + 1]).then_inc(s_exp, 1)

                def ao_hi(g, h):
                    for s in range(2):
                        act.wait_ge(s_pv, g * 2 * GH + 2 * h + s + 1)
                        act.activation(ao[:, h, 0, half(s)], bank[6 + s][:, :], ACT.Copy).then_inc(s_aohi, 1)

                def x_hi(b):
                    act.wait_ge(s_xT, b + 1)
                    for c in range(KC):
                        act.activation(xt[:, 0, c, b * P:(b + 1) * P], bank[4 + b % 4][:, c * P:(c + 1) * P],
                                       ACT.Copy, scale=cols[:, 0, c:c + 1]).then_inc(s_xhi, 1)

                def group(g, first):
                    for c in ("k0", "v0", "v1", "v2", "v3"):
                        w_hi(g, c)
                    empty(g, "k0a")
                    empty(g, "k0b")
                    w_hi(g, "q0")
                    w_hi(g, "k1")
                    for b in range(B):
                        if first and b >= B - 2:
                            for x in range(4):
                                x_hi(4 * (b - B + 2) + x)
                        empty(g, f"v{b}")
                    empty(g, "q0a")
                    empty(g, "q0b")
                    w_hi(g, "q1")
                    for j in range(GH):
                        w_hi(g, f"o{j}")
                    exps(g, 0)
                    for h in range(1, GH):
                        empty(g, f"k{h}a")
                        empty(g, f"k{h}b")
                        if h < GH - 1:
                            w_hi(g, f"k{h + 1}")
                        empty(g, f"q{h}a")
                        empty(g, f"q{h}b")
                        if h < GH - 1:
                            w_hi(g, f"q{h + 1}")
                        ao_hi(g, h - 1)
                        exps(g, h)
                    ao_hi(g, GH - 1)

                group(0, True)
                with act.Fori(1, GROUPS) as g:
                    group(g, False)

                def w_split_hi(n, c, ready, count):
                    raw, hi, lo = wchunk(n, c)
                    act.wait_ge(ready, count)
                    act.activation(hi, raw, ACT.Copy).then_inc(s_wh, 1)

                def split_hi(u, t, used, done):
                    act.wait_ge(S[t], u + 1)
                    if used:
                        act.wait_ge(S[used], (u - HB if u >= HB else u + HB) + 1)
                    act.activation(tt[:, u % HB, 0, :, :], bank[u][:, :].rearrange("p (c t) -> p c t", c=KC),
                                   ACT.Copy).then_inc(S[done], 1)

                def squares(u, sig, src, junk, dst, done):
                    act.wait_ge(S[sig], u + 1)
                    act.activation(junk, src, ACT.Square, accum_out=dst[:, u:u + 1]).then_inc(S[done], 1)

                def normed(u, n):
                    act.wait_ge(S[f"nr{n}"], u + 1 if n == 2 else u // HB + 1)
                    dst, src = tmp[:, u, :], acc[:, u, :]
                    if n == 0:
                        dst, src = dst.rearrange("p (s r) -> p r s", s=8), src.rearrange("p (r s) -> p r s", s=8)
                    act.activation(dst, src, ACT.Identity, bias=nmr[:, u:u + 1],
                                   scale=rs1[:, u:u + 1]).then_inc(S[f"xn{n}"], 1)

                def weighted(u, t, dst, col, done):
                    act.wait_ge(S[t], u + 1)
                    for c in range(KC):
                        ins = act.activation(dst[:, u, c, :], bank[u][:, c * P:(c + 1) * P], ACT.Copy,
                                             scale=cols[:, col, c:c + 1])
                    ins.then_inc(S[done], 1)

                for c in range(KC):
                    if c == 0:
                        act.wait_ge(s_unit, last_proj)
                    w_split_hi(W_KEY, c, s_rk, 16)
                for u in range(B):
                    if u % 2 == 0:
                        act.wait_ge(s_cl[u // 2], 16)
                    act.activation(cs[:, u, :], cs[:, u, :], ACT.Copy, scale=krr[:, u:u + 1]).then_inc(S["k_sc"], 1)
                act.wait_ge(s_unit, last_unit)
                for u in HALVES[0]:
                    split_hi(u, "k_T", None, "k_hi")
                w_split_hi(W_FFN, 0, s_wf, 1)
                w_split_hi(W_FFN, 1, s_wf, 2)
                split_hi(4, "k_T", "k_mm", "k_hi")
                split_hi(5, "k_T", "k_mm", "k_hi")
                split_hi(6, "k_T", "k_mm", "k_hi")
                split_hi(7, "k_T", "k_mm", "k_hi")
                for u in HALVES[0]:
                    normed(u, 0)
                w_split_hi(W_FFN, 2, s_wf, 3)
                w_split_hi(W_FFN, 3, s_wf, 4)
                for u in HALVES[0]:
                    split_hi(u, "T0", "k_mm", "hi0")
                for u in HALVES[1]:
                    normed(u, 0)
                for u in range(B):
                    squares(u, "k_b", qf[:, u, :], kt1[:, u, :, :].rearrange("p c t -> p (c t)"), k2ss, "k2_ss")
                for u in HALVES[1]:
                    split_hi(u, "T0", "y0", "hi0")
                for c in range(KC):
                    w_split_hi(W_QRY, c, s_rq, 16)
                for u in HALVES[0]:
                    normed(u, 1)
                for u in HALVES[0]:
                    weighted(u, "k_T2", kt1, 2, "k_out")
                for c in range(KC):
                    if c == 0:
                        act.wait_ge(S["k_mm"], B)
                    w_split_hi(W_BASE, c, s_rbase, 16)
                for u in HALVES[0]:
                    split_hi(u, "T1", "y0", "hi1")
                for u in HALVES[1]:
                    weighted(u, "k_T2", kt1, 2, "k_out")
                for u in HALVES[1]:
                    normed(u, 1)

                def queries_squares(u):
                    if u:
                        act.wait_ge(S["q_ss"], u)
                    squares(u, "q_b", tmp[:, u, :], pt1[:, HB:B, :].rearrange("p u t -> p (u t)"), qss, "q_ss")

                for u in HALVES[0]:
                    queries_squares(u)
                split_hi(4, "T1", "q_mm", "hi1")
                split_hi(5, "T1", "q_mm", "hi1")
                weighted(0, "q_T", qt1, 1, "q_outa")
                weighted(2, "q_T", qt1, 1, "q_outa")
                split_hi(6, "T1", "q_mm", "hi1")
                split_hi(7, "T1", "q_mm", "hi1")
                for c in range(KC):
                    w_split_hi(W_RA, c, s_rra, 16)

                def scores_exp(q):
                    for u in HALVES[q]:
                        act.wait_ge(S["s_neg"], q + 1)
                        act.activation(pr1[:, u, :], bank[u][:, 0:P], ACT.Exp, bias=nm1[:, u:u + 1],
                                       scale=qsc[:, u:u + 1], accum_out=es1[:, u:u + 1]).then_inc(S["s_exp"], 1)

                def probs_out(q):
                    for u in HALVES[q]:
                        act.wait_ge(S["p_T"], u + 1)
                        act.activation(pt1[:, u, :], bank[u][:, 0:P], ACT.Copy).then_inc(S["p_out"], 1)

                scores_exp(0)
                for u in HALVES[1]:
                    queries_squares(u)
                probs_out(0)
                weighted(4, "q_T", qt1, 1, "q_outa")
                weighted(6, "q_T", qt1, 1, "q_outa")
                scores_exp(1)
                probs_out(1)

                def ra_out(u):
                    act.wait_ge(S["ra"], u + 1)
                    act.activation(qf[:, u, 0:ER + ROUT], bank[u][:, 0:ER + ROUT], ACT.Copy).then_inc(S["ra_out"], 1)

                def split_hi2(u):
                    act.wait_ge(S["T2"], u + 1)
                    if u >= HB:
                        act.wait_ge(S["o_mm"], u - HB + 1)
                    else:
                        act.wait_ge(S["q_mm"], u + HB + 1)
                    act.activation(tt[:, u % HB, 0, :, :], bank[u][:, :].rearrange("p (c t) -> p c t", c=KC),
                                   ACT.Copy).then_inc(S["hi2"], 1)

                def router_exp(q):
                    act.wait_ge(S["router"], 10 * q + 3)
                    act.activation(rt[:, 1, part(q), :], rt[:, 0, part(q), :], ACT.Exp).then_inc(S["lg_exp"], 1)

                def hw_out(u):
                    act.wait_ge(S["hw_T"], u + 1)
                    act.activation(pt1[:, u, :], bank[(u + HB) % B][:, 0:P], ACT.Copy).then_inc(S["hw_out"], 1)

                for u in HALVES[0]:
                    normed(u, 2)
                    if u:
                        split_hi2(u - 1)
                split_hi2(HB - 1)
                for u in HALVES[0]:
                    ra_out(u)
                for u in HALVES[1]:
                    normed(u, 2)
                router_exp(0)
                for u in HALVES[1]:
                    split_hi2(u)
                for u in HALVES[1]:
                    ra_out(u)
                for u in HALVES[0]:
                    hw_out(u)
                router_exp(1)
                for u in HALVES[1]:
                    hw_out(u)

            @block.vector
            def _(dve):
                dve.sem_inc(s_dev, len(DVE_UNITS))
                dve.sem_inc(s_sadd, 2)
                dve.sem_inc(s_aolo, 2)
                for b in range(B):
                    dve.wait_ge(s_chi, b + 1)
                    dve.tensor_tensor(ct[:, 1, :, b * P:(b + 1) * P], bank[b][:, :].rearrange("p (c t) -> p c t", c=KC),
                                      ct[:, 0, :, b * P:(b + 1) * P].bitcast(fp32), ALU.subtract).then_inc(s_clo, 1)
                for b in range(B):
                    if b % 4 == 0:
                        dve.wait_ge(s_xin[b // 4], 16)
                    dve.bn_stats(stats[:, b, :], xraw[:, b, :]).then_inc(s_d, 1)
                for b in range(B):
                    dve.wait_ge(s_d, b + 1)
                    dve.bn_aggr(mv[:, b, :], stats[:, b, :]).then_inc(s_d, 1)
                dve.wait_ge(s_d, 2 * B)
                dve.tensor_scalar(vsum[:, :], mv[:, :, 1], EPS_LN, None, ALU.add).then_inc(s_d, 1)
                dve.wait_ge(s_g, 2)
                dve.tensor_tensor(msq[:, :], rstd[:, :], rstd[:, :], ALU.mult).then_inc(s_d, 1)
                dve.wait_ge(s_d, 2 * B + 2)
                dve.tensor_tensor(rscale[:, :], msq[:, :], mv[:, :, 1], ALU.mult).then_inc(s_mf, 1)
                dve.wait_ge(s_mf, 1)
                dve.tensor_scalar(msq[:, :], rscale[:, :], EPS_RMS0, None, ALU.add).then_inc(s_d, 1)
                for b in range(B):
                    dve.tensor_scalar(acc[:, b, :], xraw[:, b, :], mv[:, b, 0:1], rstd[:, b:b + 1],
                                      ALU.subtract, ALU.mult).then_inc(s_h, 1)
                dve.wait_ge(s_g, 3)
                for b in range(B):
                    dve.wait_ge(s_h, b + 1)
                    dve.tensor_scalar(xraw[:, b, :], acc[:, b, :], rrms[:, b:b + 1], None, ALU.mult).then_inc(s_xr, 1)
                dve.wait_ge(s_min, 16)
                dve.tensor_copy(maskf[:, :, :], masku[:, :, :]).then_inc(s_mf, 1)
                dve.wait_ge(s_mf, 2)
                dve.tensor_scalar(maskneg[:, :, :], maskf[:, :, :], 1.0, -MASKED, ALU.subtract, ALU.mult).then_inc(s_mneg, 1)
                dve.tensor_reduce(anykey[:, :], maskf[:, :, :], AX, ALU.max).then_inc(s_mf, 1)
                for b in range(B):
                    dve.wait_ge(s_xhi, b * KC + KC)
                    for c in range(KC):
                        dve.scalar_tensor_tensor(out=xt[:, 1, c, b * P:(b + 1) * P], in0=bank[4 + b % 4][:, c * P:(c + 1) * P],
                                                 scalar=cols[:, 0, c:c + 1],
                                                 in1=xt[:, 0, c, b * P:(b + 1) * P].bitcast(fp32),
                                                 op0=ALU.mult, op1=ALU.subtract).then_inc(s_xlo, 1)
                dve.wait_ge(s_mf, 3)

                def softmax_in(g, h):
                    n = g * 2 * GH + 2 * h
                    dve.wait_ge(s_bm, g * GH + h + 1)
                    for s in range(2):
                        bs = slice(4 * s, 4 * s + 4)
                        dve.wait_ge(s_s, n + s + 1)
                        dve.tensor_tensor(prob[:, bs, :], bank[4 + s][:, :].rearrange("p (b k) -> p b k", b=4),
                                          bm[:, h % 2, bs, :], ALU.add).then_inc(s_sadd, 1)
                        dve.wait_ge(s_sadd, n + s + 3)
                        dve.tensor_reduce(rinv[:, bs], prob[:, bs, :], AX, ALU.max).then_inc(s_smax, 1)
                        dve.wait_ge(s_smax, n + s + 1)
                        dve.tensor_scalar(nmax[:, bs], rinv[:, bs], -1.0, None, ALU.mult).then_inc(s_nmax, 1)

                def softmax_out(g, h, s):
                    n = g * 2 * GH + 2 * h + s
                    bs = slice(4 * s, 4 * s + 4)
                    dve.wait_ge(s_exp, g * B * GH + h * B + 4 * s + 4)
                    dve.reciprocal(rinv[:, bs], esum[:, bs]).then_inc(s_rinv, 1)
                    dve.wait_ge(s_rinv, 2 * n + 1)
                    dve.tensor_tensor(rinv[:, bs], rinv[:, bs], anykey[:, bs], ALU.mult).then_inc(s_rinv, 1)
                    dve.wait_ge(s_rinv, 2 * n + 2)
                    dve.tensor_tensor(prob[:, bs, :], prob[:, bs, :],
                                      rinv[:, bs].unsqueeze(2).to_broadcast([P, 4, P]), ALU.mult).then_inc(s_p, 1)

                def pt_out(g, h):
                    for s in range(2):
                        dve.wait_ge(s_pt, g * 2 * GH + 2 * h + s + 1)
                        dve.tensor_copy(pt[:, 4 * s:4 * s + 4, :],
                                        bank[6 + s][:, :].rearrange("p (b k) -> p b k", b=4)).then_inc(s_pte, 1)

                def ao_lo(g, h):
                    for s in range(2):
                        dve.wait_ge(s_aohi, g * 2 * GH + 2 * h + s + 1)
                        dve.tensor_tensor(ao[:, h, 1, half(s)], bank[6 + s][:, :], ao[:, h, 0, half(s)].bitcast(fp32),
                                          ALU.subtract).then_inc(s_aolo, 1)

                def add_out(g, u):
                    i, b = un[u], int(u[1])
                    dve.wait_ge(s_unit, g * NUNIT + NUNIT + i + 1)
                    dve.wait_ge(s_dev, g * len(DVE_UNITS) + len(DVE_UNITS) + dx[u] - 7)
                    dve.tensor_tensor(acc[:, b, :], acc[:, b, :], bank[i % RING][:, :], ALU.add).then_inc(s_dev, 1)

                with dve.Fori(0, GROUPS) as g:
                    for h in range(GH):
                        softmax_in(g, h)
                        if h == 3:
                            add_out(g, "o0")
                            add_out(g, "o1")
                        softmax_out(g, h, 0)
                        if h == 3:
                            add_out(g, "o2")
                        softmax_out(g, h, 1)
                        if h == 3:
                            add_out(g, "o3")
                        pt_out(g, h)
                        if h == 3:
                            add_out(g, "o4")
                            add_out(g, "o5")
                        ao_lo(g, h)
                    add_out(g, "o6")
                    add_out(g, "o7")
                    for b in range(B):
                        add_out(g, f"p{b}")

                def mean_square(q, sig, src, dst, done):
                    dve.wait_ge(S[sig], (q + 1) * HB)
                    dve.tensor_scalar(dst[:, part(q)], src[:, part(q)], 1.0 / D, EPS_RMS1, ALU.mult, ALU.add).then_inc(S[done], 1)

                def x_stats(u, n, x):
                    dve.wait_ge(S[x], u + 1)
                    dve.bn_stats(st1[:, u, :], acc[:, u, :]).then_inc(S[f"bn{n}"], 1)
                    dve.wait_ge(S[f"bn{n}"], u + 1)
                    dve.bn_aggr(mv1[:, u, :], st1[:, u, :]).then_inc(S[f"ag{n}"], 1)

                def variances(q, n):
                    dve.wait_ge(S[f"ag{n}"], (q + 1) * HB)
                    dve.tensor_scalar(ve1[:, part(q)], mv1[:, part(q), 1], EPS_LN, None, ALU.add).then_inc(S[f"ve{n}"], 1)

                def offsets(q, n):
                    dve.wait_ge(S[f"rs{n}"], q + 1)
                    dve.scalar_tensor_tensor(out=nmr[:, part(q)], in0=mv1[:, part(q), 0], scalar=-1.0, in1=rs1[:, part(q)],
                                             op0=ALU.mult, op1=ALU.mult).then_inc(S[f"nr{n}"], 1)

                def offset(u):
                    dve.wait_ge(S["rs2"], u + 1)
                    dve.scalar_tensor_tensor(out=nmr[:, u:u + 1], in0=mv1[:, u, 0:1], scalar=-1.0, in1=rs1[:, u:u + 1],
                                             op0=ALU.mult, op1=ALU.mult).then_inc(S["nr2"], 1)

                def split_lo(u, hi, done):
                    dve.wait_ge(S[hi], u + 1)
                    dve.tensor_tensor(tt[:, u % HB, 1, :, :], bank[u][:, :].rearrange("p (c t) -> p c t", c=KC),
                                      tt[:, u % HB, 0, :, :].bitcast(fp32), ALU.subtract).then_inc(S[done], 1)

                def biased(u, sig, row, dst, done):
                    dve.wait_ge(S[sig], u + 1)
                    dve.tensor_tensor(dst, bank[u][:, :], row, ALU.add).then_inc(S[done], 1)

                def gated(u, sig, scalar, done):
                    dve.wait_ge(S[sig], u + 1)
                    dve.scalar_tensor_tensor(out=acc[:, u, :], in0=bank[u][:, :], scalar=scalar, in1=acc[:, u, :],
                                             op0=ALU.mult, op1=ALU.add).then_inc(S[done], 1)

                def x1(u):
                    dve.wait_ge(s_xl[u // HB], 16)
                    dve.scalar_tensor_tensor(out=acc[:, u, :], in0=acc[:, u, :], scalar=tg[:, 0:1], in1=tmp[:, u, :],
                                             op0=ALU.mult, op1=ALU.add).then_inc(S["x1"], 1)

                def dequant(c):
                    if c:
                        dve.wait_ge(s_wf, c)
                    for h in range(2):
                        ps = slice(h * 64, h * 64 + 64)
                        dve.tensor_scalar(wint[ps, :], qw[ps, :], 4 * (2 * c + h), 15,
                                          ALU.logical_shift_right, ALU.bitwise_and).then_inc(s_prep, 1)
                    dve.wait_ge(s_prep, 9 + 3 * c + 2)
                    dve.tensor_tensor(stage[:, KC + c, :], wint[:, :], zint[:, :], ALU.subtract).then_inc(s_prep, 1)
                    dve.wait_ge(s_prep, 9 + 3 * c + 3)
                    dve.tensor_tensor(stage[:, KC + c, :], stage[:, KC + c, :], scl[:, :], ALU.mult).then_inc(s_wf, 1)

                dve.wait_ge(s_rf, 48)
                for s in range(8):
                    dve.tensor_scalar(zint[:, :].rearrange("p (j s) -> p j s", s=8)[:, :, s], zq[:, :], 4 * s, 15,
                                      ALU.logical_shift_right, ALU.bitwise_and).then_inc(s_prep, 1)
                dve.wait_ge(s_prep, 8)
                dve.tensor_scalar(zint[:, :], zint[:, :], 1, None, ALU.add).then_inc(s_prep, 1)
                dve.wait_ge(s_prep, 9)
                def x1_half(q):
                    for u in HALVES[q]:
                        x1(u)
                    for u in HALVES[q]:
                        x_stats(u, 0, "x1")
                    variances(q, 0)

                def x2(u):
                    dve.wait_ge(S["rsf"], u + 1)
                    gated(u, "y0", tg[:, 2:3], "x2")
                    x_stats(u, 1, "x2")

                def keys_normed(q):
                    mean_square(q, "k2_ss", k2ss, k2ms, "k2_ms")
                    dve.wait_ge(S["k2_rr"], q + 1)
                    for u in HALVES[q]:
                        dve.tensor_scalar(qf[:, u, :], qf[:, u, :], k2rr[:, u:u + 1], None, ALU.mult).then_inc(S["k_n"], 1)

                for u in HALVES[0]:
                    split_lo(u, "k_hi", "k_lo")
                dequant(0)
                dequant(1)
                dve.wait_ge(s_rest, 16)
                for row, g in ((R_FFN, 2), (R_BASE, 3)):
                    dve.tensor_scalar(rows[:, row, :], rows[:, row, :], tg[:, g:g + 1], None, ALU.mult).then_inc(S["rows"], 1)
                dve.wait_ge(s_dev, (GROUPS + 1) * len(DVE_UNITS))
                x1_half(0)
                split_lo(4, "k_hi", "k_lo")
                split_lo(5, "k_hi", "k_lo")
                offsets(0, 0)
                dve.wait_ge(s_early, 80)
                for u in HALVES[0]:
                    biased(u, "k_mm", bkr[:, :], qf[:, u, :], "k_b")
                split_lo(6, "k_hi", "k_lo")
                split_lo(7, "k_hi", "k_lo")
                dequant(2)
                dequant(3)
                split_lo(0, "hi0", "lo0")
                split_lo(1, "hi0", "lo0")
                x1_half(1)
                split_lo(2, "hi0", "lo0")
                split_lo(3, "hi0", "lo0")
                offsets(1, 0)
                for u in HALVES[1]:
                    biased(u, "k_mm", bkr[:, :], qf[:, u, :], "k_b")
                keys_normed(0)
                split_lo(4, "hi0", "lo0")
                split_lo(5, "hi0", "lo0")
                x2(0)
                x2(1)
                split_lo(6, "hi0", "lo0")
                x2(2)
                split_lo(7, "hi0", "lo0")
                x2(3)
                variances(0, 1)
                keys_normed(1)
                offsets(0, 1)
                x2(4)
                x2(5)
                x2(6)
                split_lo(0, "hi1", "lo1")
                split_lo(1, "hi1", "lo1")
                x2(7)
                variances(1, 1)
                split_lo(2, "hi1", "lo1")
                split_lo(3, "hi1", "lo1")
                offsets(1, 1)
                for u in HALVES[0]:
                    biased(u, "q_mm", rows[:, R_BQ, :], tmp[:, u, :], "q_b")

                def q_outd(u):
                    dve.wait_ge(S["q_T"], u + 1)
                    for c in range(KC):
                        ins = dve.tensor_scalar(qt1[:, u, c, :], bank[u][:, c * P:(c + 1) * P], cols[:, 1, c:c + 1],
                                                None, ALU.mult)
                    ins.then_inc(S["q_outd"], 1)

                def scores_max(q):
                    for u in HALVES[q]:
                        dve.wait_ge(S["s_mm"], u + 1)
                        dve.tensor_reduce(nm1[:, u:u + 1], bank[u][:, 0:P], AX, ALU.max).then_inc(S["s_max"], 1)
                    dve.wait_ge(S["q_rr"], q + 1)
                    dve.tensor_scalar(qsc[:, part(q)], qrr[:, part(q)], float(D) ** -0.5, None, ALU.mult).then_inc(S["s_scale"], 1)
                    dve.wait_ge(S["s_max"], (q + 1) * HB)
                    dve.wait_ge(S["s_scale"], q + 1)
                    dve.scalar_tensor_tensor(out=nm1[:, part(q)], in0=nm1[:, part(q)], scalar=-1.0, in1=qsc[:, part(q)],
                                             op0=ALU.mult, op1=ALU.mult).then_inc(S["s_neg"], 1)

                def x3_half(q):
                    dve.wait_ge(S["s_exp"], (q + 1) * HB)
                    dve.reciprocal(ri1[:, part(q)], es1[:, part(q)]).then_inc(S["s_ri"], 1)
                    dve.wait_ge(S["s_ri"], q + 1)
                    dve.tensor_scalar(ri1[:, part(q)], ri1[:, part(q)], tg[:, 1:2], None, ALU.mult).then_inc(S["s_rg"], 1)
                    dve.wait_ge(S["s_rg"], q + 1)
                    for u in HALVES[q]:
                        gated(u, "pv", ri1[:, u:u + 1], "x3")
                        x_stats(u, 2, "x3")
                        dve.wait_ge(S["ag2"], u + 1)
                        dve.tensor_scalar(ve1[:, u:u + 1], mv1[:, u, 1:2], EPS_LN, None, ALU.add).then_inc(S["ve2"], 1)
                        if u % HB:
                            offset(u - 1)

                split_lo(4, "hi1", "lo1")
                split_lo(5, "hi1", "lo1")
                mean_square(0, "q_ss", qss, qms, "q_ms")
                q_outd(1)
                q_outd(3)
                split_lo(6, "hi1", "lo1")
                split_lo(7, "hi1", "lo1")
                scores_max(0)
                for u in HALVES[1]:
                    biased(u, "q_mm", rows[:, R_BQ, :], tmp[:, u, :], "q_b")
                mean_square(1, "q_ss", qss, qms, "q_ms")
                q_outd(5)
                q_outd(7)
                scores_max(1)
                x3_half(0)
                offset(HB - 1)
                for u in HALVES[0]:
                    split_lo(u, "hi2", "lo2")
                x3_half(1)
                offset(B - 1)

                dve.tensor_copy(emap[:, :], emap_i[:, :]).then_inc(s_prep, 1)
                dve.wait_ge(s_prep, 22)
                dve.tensor_tensor(onehot[:, :, :], emap[:, :].unsqueeze(1).to_broadcast([P, NEXP, ROUT]),
                                  consts[:, ROUT * ROUT:].unsqueeze(2).to_broadcast([P, NEXP, ROUT]), ALU.is_equal).then_inc(s_prep, 1)
                dve.wait_ge(s_prep, 23)
                dve.tensor_scalar(onehot[:, :, :], onehot[:, :, :], LORA_SCALE, None, ALU.mult).then_inc(s_prep, 1)
                dve.wait_ge(s_prep, 24)
                tri = consts[:, 0:ROUT * ROUT].rearrange("p (n m) -> p n m", n=ROUT).unsqueeze(1).to_broadcast([P, HB, ROUT, ROUT])

                def router(q, between):
                    us = part(q)
                    lg, ex, pk, rank = (rt[:, i, us, :] for i in range(4))
                    bc = [P, HB, ROUT]
                    pm = ex.unsqueeze(2).to_broadcast([P, HB, ROUT, ROUT])
                    pn = ex.unsqueeze(3).to_broadcast([P, HB, ROUT, ROUT])
                    n = 10 * q

                    def then(k, ins):
                        ins.then_inc(S["router"], 1)
                        dve.wait_ge(S["router"], n + k)

                    dve.wait_ge(S["ra_out"], (q + 1) * HB)
                    then(1, dve.tensor_tensor(lg, qf[:, us, ER:ER + ROUT], rb[:, :].unsqueeze(1).to_broadcast(bc), ALU.add))
                    then(2, dve.tensor_reduce(nm1[:, us], lg, AX, ALU.max))
                    then(3, dve.tensor_tensor(lg, lg, nm1[:, us].unsqueeze(2).to_broadcast(bc), ALU.subtract))
                    dve.wait_ge(S["lg_exp"], q + 1)
                    then(4, dve.tensor_reduce(es1[:, us], ex, AX, ALU.add))
                    then(5, dve.reciprocal(ri1[:, us], es1[:, us]))
                    then(6, dve.tensor_tensor(ex, ex, ri1[:, us].unsqueeze(2).to_broadcast(bc), ALU.mult))
                    dve.tensor_tensor(cmp[:, 0], pm, pn, ALU.is_gt).then_inc(S["gt"], 1)
                    dve.tensor_tensor(cmp[:, 1], pm, pn, ALU.is_equal).then_inc(S["gt"], 1)
                    between(0)
                    dve.wait_ge(S["gt"], 4 * q + 2)
                    dve.tensor_tensor(cmp[:, 1], cmp[:, 1], tri, ALU.mult).then_inc(S["gt"], 1)
                    between(1)
                    dve.wait_ge(S["gt"], 4 * q + 3)
                    dve.tensor_tensor(cmp[:, 0], cmp[:, 0], cmp[:, 1], ALU.add).then_inc(S["gt"], 1)
                    between(2)
                    dve.wait_ge(S["gt"], 4 * q + 4)
                    then(7, dve.tensor_reduce(rank, cmp[:, 0], AX, ALU.add))
                    between(3)
                    then(8, dve.scalar_tensor_tensor(out=pk, in0=rank, scalar=float(NEXP), in1=ex, op0=ALU.is_lt, op1=ALU.mult))
                    then(9, dve.tensor_tensor(wexp[:, :], onehot[:, :, :].unsqueeze(1).to_broadcast([P, HB, NEXP, ROUT]),
                                              pk.unsqueeze(2).to_broadcast([P, HB, NEXP, ROUT]), ALU.mult))
                    then(10, dve.tensor_reduce(wsum[:, us, :], wexp[:, :], AX, ALU.add))
                    for u in HALVES[q]:
                        dve.tensor_tensor(tmp[:, u, 0:ER].rearrange("p (e r) -> p e r", e=NEXP),
                                          qf[:, u, 0:ER].rearrange("p (e r) -> p e r", e=NEXP),
                                          wsum[:, u, :].unsqueeze(2).to_broadcast([P, NEXP, RANK]), ALU.mult).then_inc(S["hw"], 1)

                def x4(u):
                    dve.wait_ge(S["rsb"], u + 1)
                    gated(u, "o_mm2", tg[:, 3:4], "x4")

                router(0, between=lambda i: split_lo(HB + i, "hi2", "lo2"))
                router(1, between=x4)
                for u in HALVES[1]:
                    x4(u)

            @block.tensor
            def _(pe):
                pe.sem_inc(s_unit, NUNIT)
                pe.wait_ge(s_const, 48)
                for b in range(B):
                    if b % 2 == 0:
                        pe.wait_ge(s_cin[b // 2], 16)
                    for c in range(KC):
                        mm = pe.transpose(bank[b][:, c * P:(c + 1) * P], craw[:, b, c * P:(c + 1) * P], ident[:, :])
                    mm.then_inc(s_cT, 1)
                pe.wait_ge(s_clo, B)

                def x_transposed(b):
                    pe.wait_ge(s_xr, b + 1)
                    if b >= 4:
                        pe.wait_ge(s_xlo, (b - 3) * KC)
                    for c in range(KC):
                        mm = pe.transpose(bank[4 + b % 4][:, c * P:(c + 1) * P], xraw[:, b, c * P:(c + 1) * P], ident[:, :])
                    mm.then_inc(s_xT, 1)

                def bank_free(g, u):
                    i = un[u]
                    before = UNITS[i - RING]
                    if before in dx:
                        n = dx[before] + 1 + (len(DVE_UNITS) if i >= RING else 0)
                        pe.wait_ge(s_dev, g * len(DVE_UNITS) + n)
                    else:
                        pe.wait_ge(s_aev, g * len(ACT_UNITS) + ax[before] + 1)

                def weights(g, c):
                    pe.wait_ge(s_wlo, g * NCH + ix[c] + 1)

                def proj(g, kind, h, s):
                    u = f"{kind}{h}{'ab'[s]}"
                    w, t = (wq, xt) if kind == "q" else (wk, ct)
                    if s == 0:
                        weights(g, f"{kind}{h}")
                    bank_free(g, u)
                    for c in range(KC):
                        for i, j in PASSES:
                            mm = pe.matmul(bank[un[u] % RING][:, :], w[:, i, c, :], t[:, j, c, half(s)],
                                           start=(c == 0 and i + j == 0), stop=(c == KC - 1 and i == 1))
                    mm.then_inc(s_unit, 1)

                def value(g, b):
                    u = f"v{b}"
                    if b == 0:
                        weights(g, "v3")
                    bank_free(g, u)
                    for c in range(KC):
                        for i, j in PASSES:
                            mm = pe.matmul(bank[un[u] % RING][:, :], ct[:, i, c, b * P:(b + 1) * P], wvo[:, j, c, :],
                                           start=(c == 0 and i + j == 0), stop=(c == KC - 1 and i == 1))
                    mm.then_inc(s_unit, 1)

                def scores(g, h):
                    pe.wait_ge(s_aev, g * len(ACT_UNITS) + ax[f"q{h}b"] + 1)
                    for s in range(2):
                        pe.wait_ge(s_sadd, g * 2 * GH + 2 * h + s + 1)
                        for b in range(4 * s, 4 * s + 4):
                            mm = pe.matmul(bank[4 + s][:, (b - 4 * s) * P:(b - 4 * s + 1) * P],
                                           qt[:, b * P:(b + 1) * P], kt[:, b * P:(b + 1) * P], start=True, stop=True)
                        mm.then_inc(s_s, 1)

                def transposes(g, h):
                    n = g * 2 * GH + 2 * h
                    for s in range(2):
                        pe.wait_ge(s_p, n + s + 1)
                        pe.wait_ge(s_aolo, n + s + 1)
                        for b in range(4 * s, 4 * s + 4):
                            mm = pe.transpose(bank[6 + s][:, (b - 4 * s) * P:(b - 4 * s + 1) * P], prob[:, b, :], ident[:, :])
                        mm.then_inc(s_pt, 1)

                def attend(g, h):
                    if h == 0:
                        pe.wait_ge(s_aev, g * len(ACT_UNITS) + ax[f"v{B - 1}"] + 1)
                    for s in range(2):
                        pe.wait_ge(s_pte, g * 2 * GH + 2 * h + s + 1)
                        for b in range(4 * s, 4 * s + 4):
                            mm = pe.matmul(bank[6 + s][:, (b - 4 * s) * P:(b - 4 * s + 1) * P],
                                           vals[:, b, h * P:(h + 1) * P], pt[:, b, :], start=True, stop=True)
                        mm.then_inc(s_pv, 1)

                def project(g, u, heads):
                    b = int(u[1])
                    if u == "o0":
                        weights(g, "o3")
                    pe.wait_ge(s_aolo, g * 2 * GH + 2 * max(heads) + b // 4 + 3)
                    bank_free(g, u)
                    for h in heads:
                        for i, j in PASSES:
                            mm = pe.matmul(bank[un[u] % RING][:, :], ao[:, h, i, b * P:(b + 1) * P], wvo[:, j, h, :],
                                           start=(h == heads[0] and i + j == 0), stop=(h == heads[-1] and i == 1))
                    mm.then_inc(s_unit, 1)

                def group(g, first):
                    proj(g, "k", 0, 0)
                    proj(g, "k", 0, 1)
                    for b in range(B):
                        if first and b >= B - 2:
                            for x in range(4):
                                x_transposed(4 * (b - B + 2) + x)
                        value(g, b)
                    for s in range(2):
                        if first:
                            pe.wait_ge(s_xlo, (s + 1) * 4 * KC)
                        proj(g, "q", 0, s)
                    scores(g, 0)
                    for h in range(1, GH):
                        proj(g, "k", h, 0)
                        proj(g, "k", h, 1)
                        proj(g, "q", h, 0)
                        transposes(g, h - 1)
                        proj(g, "q", h, 1)
                        attend(g, h - 1)
                        scores(g, h)
                    for b in range(4):
                        project(g, f"o{b}", [0, 1, 2])
                    transposes(g, GH - 1)
                    for b in (4, 5):
                        project(g, f"o{b}", [0, 1, 2])
                    attend(g, GH - 1)
                    for b in (6, 7):
                        project(g, f"o{b}", [0, 1, 2])
                    for b in range(B):
                        project(g, f"p{b}", [GH - 1])

                group(0, True)
                with pe.Fori(1, GROUPS) as g:
                    group(g, False)

                def transpose(us, waits, src, done, n=KC, to=lambda u: u):
                    for u in us:
                        for w in waits:
                            pe.wait_ge(S[w], u + 1)
                        for c in range(n):
                            mm = pe.transpose(bank[to(u)][:, c * P:(c + 1) * P], src[:, u, c * P:(c + 1) * P], ident[:, :])
                        mm.then_inc(S[done], 1)

                def product(u, lo, w, n, done, to, last=True):
                    pe.wait_ge(S[lo], u + 1)
                    for c in range(KC):
                        for i, j in PASSES:
                            mm = pe.matmul(bank[to][:, 0:n], tt[:, u % HB, i, c, :], w[:, j, c, :],
                                           start=(c == 0 and i + j == 0), stop=(c == KC - 1 and i == 1 and last))
                    mm.then_inc(S[done], 1)

                pe.wait_ge(s_dev, (GROUPS + 1) * len(DVE_UNITS))
                transpose(HALVES[0], ["k_fn"], cs, "k_T")
                pe.wait_ge(s_wl, W_KEY + KC)
                for u in HALVES[0]:
                    product(u, "k_lo", wt_a, D, "k_mm", u)
                transpose(HALVES[1], ["k_fn"], cs, "k_T")
                for u in (4, 5):
                    product(u, "k_lo", wt_a, D, "k_mm", u)
                transpose(HALVES[0], ["xn0", "k_b"], tmp, "T0")
                for u in (6, 7):
                    product(u, "k_lo", wt_a, D, "k_mm", u)
                pe.wait_ge(s_wl, W_FFN + KC)
                for u in (0, 1):
                    product(u, "lo0", wt_f, D, "y0", u)
                transpose(HALVES[1], ["xn0", "k_b"], tmp, "T0")
                for u in (2, 3, 4, 5):
                    product(u, "lo0", wt_f, D, "y0", u)
                transpose(HALVES[0], ["k_n", "x2"], qf, "k_T2")
                for u in (6, 7):
                    product(u, "lo0", wt_f, D, "y0", u)
                transpose(HALVES[0], ["xn1", "k_out"], tmp, "T1")
                pe.wait_ge(s_wl, W_QRY + KC)
                for u in (0, 1):
                    product(u, "lo1", wt_q, D, "q_mm", u)
                transpose(HALVES[1], ["k_n", "x2"], qf, "k_T2")
                for u in (2, 3):
                    product(u, "lo1", wt_q, D, "q_mm", u)
                transpose(HALVES[1], ["xn1", "k_out"], tmp, "T1")
                transpose(HALVES[0], ["q_b"], tmp, "q_T")

                def scores(q):
                    for u in HALVES[q]:
                        pe.wait_ge(S["q_outd" if u % 2 else "q_outa"], u // 2 + 1)
                        for c in range(KC):
                            mm = pe.matmul(bank[u][:, 0:P], qt1[:, u, c, :], kt1[:, u, c, :], start=(c == 0), stop=(c == KC - 1))
                        mm.then_inc(S["s_mm"], 1)

                def attention(q):
                    for u in HALVES[q]:
                        pe.wait_ge(S["p_out"], u + 1)
                        pe.matmul(bank[u][:, :], pt1[:, u, :], cs[:, u, :], start=True, stop=True).then_inc(S["pv"], 1)

                for u in (4, 5):
                    product(u, "lo1", wt_q, D, "q_mm", u)
                scores(0)
                for u in (6, 7):
                    product(u, "lo1", wt_q, D, "q_mm", u)
                transpose(HALVES[0], ["s_exp"], pr1, "p_T", n=1)
                transpose(HALVES[1], ["q_b"], tmp, "q_T")
                attention(0)
                scores(1)
                transpose(HALVES[1], ["s_exp"], pr1, "p_T", n=1)
                attention(1)
                pe.wait_ge(s_wl, W_RA + KC)
                for u in HALVES[0]:
                    transpose([u], ["xn2"], tmp, "T2")
                    if u:
                        product(u - 1, "lo2", wra, RAW, "ra", u - 1)
                product(HB - 1, "lo2", wra, RAW, "ra", HB - 1)
                pe.wait_ge(s_wl, W_BASE + KC)
                for u in HALVES[0]:
                    pe.wait_ge(S["ra_out"], u + 1)
                    product(u, "lo2", wt_a, D, "o_mm", u, last=False)
                for u in HALVES[1]:
                    transpose([u], ["xn2"], tmp, "T2")
                for u in HALVES[1]:
                    product(u, "lo2", wra, RAW, "ra", u)
                pe.wait_ge(S["ra_out"], B)

                def experts(u):
                    pe.wait_ge(S["hw_out"], u + 1)
                    pe.matmul(bank[u][:, :], pt1[:, u, :], wbm[:, :], start=False, stop=True).then_inc(S["o_mm2"], 1)

                transpose(HALVES[0], ["hw"], tmp, "hw_T", n=1, to=lambda u: HB + u)
                for u in HALVES[0]:
                    experts(u)
                for u in HALVES[1]:
                    pe.wait_ge(S["hw_out"], u - HB + 1)
                    product(u, "lo2", wt_a, D, "o_mm", u, last=False)
                pe.wait_ge(S["x4"], HB)
                transpose(HALVES[1], ["hw"], tmp, "hw_T", n=1, to=lambda u: u - HB)
                for u in HALVES[1]:
                    experts(u)


def kernel(**inputs):
    import concourse.bacc as _bacc
    from concourse.bass_utils import run_bass_kernel_spmd as _run

    x = {k: np.asarray(v) for k, v in inputs.items()}
    lay = {}

    def head_major(w):
        return w.reshape(HEADS, P, KC, P).transpose(0, 3, 2, 1).reshape(HEADS, P, D)

    wq, wk = head_major(x["L0_xattn_w_q"]), head_major(x["L0_xattn_w_k"])
    wv = x["L0_xattn_w_v"].reshape(GROUPS, GH * P, KC, P).transpose(0, 2, 3, 1)
    wo = x["L0_xattn_w_out"].reshape(D, GROUPS, GH, P).transpose(1, 2, 3, 0)
    src = {"q": wq.reshape(GROUPS, GH, P, D), "k": wk.reshape(GROUPS, GH, P, D), "v": wv, "o": wo}
    w0 = np.stack([src[c[0]][:, int(c[1])] for c in CHUNKS], axis=1)
    lay["w0"] = w0.reshape(GROUPS * NCH // 2, 2, P, D).transpose(0, 2, 1, 3)
    lay["bias"] = x["L0_xattn_position_bias"].reshape(GROUPS, GH, P, P).transpose(0, 2, 1, 3)
    lay["x"] = x["x"].transpose(1, 0, 2)
    lay["ctx"] = x["ctx_4096"].transpose(1, 0, 2)
    lay["mask"] = x["mask_BxSxS2_bk0"].transpose(1, 0, 2)
    lay["gates"] = np.concatenate([x["g_xattn"], x["g_ffn"]])
    lay["cols"] = np.stack([x[k].reshape(KC, P).T for k in
                            ("L0_xattn_ln_weight", "L1_xattn_qn_w", "L1_xattn_kn_w")], axis=1)
    lay["ident"] = np.eye(P, dtype=np.float32)
    inner = lambda w: w.reshape(w.shape[0], KC, P).transpose(2, 1, 0)
    lay["w_key"] = inner(x["L1_xattn_Wk_w"])
    lay["w_qry"] = inner(x["L1_xattn_Wq_w"])
    lay["w_base"] = inner(x["L1_ffn_base_W"])
    lay["w_ra"] = inner(np.concatenate([x["L1_ffn_A"].reshape(ER, D), x["L1_ffn_router_W"],
                                        np.zeros((RAW - ER - ROUT, D), np.float32)]))
    lay["w_bm"] = x["L1_ffn_B"].transpose(0, 2, 1).reshape(ER, D)
    lay["rows"] = np.stack([x[k] for k in ("L0_ffn_bias", "L1_xattn_Wq_b", "L1_ffn_base_b")])
    lay["fnw"] = x["L1_xattn_fn_w"]
    lay["bk"] = x["L1_xattn_Wk_b"]
    lay["rb"] = x["L1_ffn_router_b"]
    lay["emap"] = x["L1_ffn_expert_map"]
    lay["consts"] = np.concatenate([np.tril(np.ones((ROUT, ROUT), np.float32), -1).ravel(),
                                    np.arange(NEXP, dtype=np.float32)])
    lay["qw"] = np.tile(x["L0_ffn_qweight"], (2, 1))
    rep = P // 2 // KC
    lay["zq"] = np.tile(np.repeat(x["L0_ffn_qzeros"], rep, axis=0), (2, 1))
    lay["scl"] = np.tile(np.repeat(x["L0_ffn_scales"], rep, axis=0), (2, 1))

    nc = _bacc.Bacc("TRN2", target_bir_lowering=False, num_devices=1)
    arrays, aps = {}, {}
    for k, v in lay.items():
        v = np.ascontiguousarray(v)
        arrays[f"in_{k}"] = v
        dt = mybir.dt.uint8 if v.dtype == bool else mybir.dt.from_np(v.dtype)
        aps[k] = nc.dram_tensor(f"in_{k}", v.shape, dt, kind="ExternalInput").ap()
    out = nc.dram_tensor("out_0", (B, P, D), mybir.dt.float32, kind="ExternalOutput").ap()
    build(nc, aps, out)
    r = _run(nc, [arrays], core_ids=[0])
    return r.results[0]["out_0"]
```
